# Optimizing a Trainium2 kernel written in Bass

```python
import numpy as np
import jax
import jax.numpy as jnp

def _softmax(x, axis=-1):
    return jax.nn.softmax(x, axis=axis)

def _gelu(x):
    return jax.nn.gelu(x, approximate=True)

def _silu(x):
    return jax.nn.silu(x)

def _sigmoid(x):
    return jax.nn.sigmoid(x)

def _layernorm(x, axis=-1, eps=1e-05):
    m = jnp.mean(x, axis=axis, keepdims=True)
    v = jnp.var(x, axis=axis, keepdims=True)
    return (x - m) / jnp.sqrt(v + eps)

def _scatter_add(tgt, idx, src, axis=0):
    return tgt.at[idx].add(src)

def _segment_sum(src, seg, n):
    return jax.ops.segment_sum(src, seg, n)
kernel_name = 'mk_adj_ffn_d1_adj_r2_4898e6'

def setup_inputs(seed: int=0):
    np.random.seed(seed)
    _w = jnp.asarray

    def _rec_inputs():
        import jax
        import jax.numpy as jnp
        _gk = jax.random.key(seed)
        x = -0.0002928 + 1 * jax.random.normal(jax.random.fold_in(_gk, 1), (2048, 256), jnp.float32)
        _a = jax.random.bernoulli(jax.random.fold_in(_gk, 2), 0.000976562, (2048, 2048))
        _a = jnp.logical_or(_a, jnp.swapaxes(_a, -1, -2))
        _a = jnp.logical_or(_a, jnp.eye(2048, dtype=bool))
        _af = _a.astype(jnp.float32)
        adj = _af
        return (x, adj)
    x, adj = _rec_inputs()

    def _L0_gnn_setup():
        import jax, jax.numpy as jnp
        import numpy as np
        IN_C, HID_C = (256, 256)
        ALPHA = 0.2
        N = 4096
        NEG_BIG = -9000000000000000.0
        key = jax.random.key(seed)
        k1, k2, k3, k4, k5, k6, k7 = jax.random.split(key, 7)
        h = jax.random.normal(k1, (N, IN_C), dtype=jnp.float32)
        adj = jax.random.randint(k2, (N, N), 0, 2).astype(jnp.float32)
        gain = np.sqrt(2.0 / (1.0 + ALPHA ** 2))
        lim_W = gain * np.sqrt(6.0 / (2 * IN_C + HID_C))
        W = jax.random.uniform(k3, (2 * IN_C, HID_C), jnp.float32, -lim_W, lim_W)
        lim_a = np.sqrt(1.0 / HID_C)
        a_w = jax.random.uniform(k4, (HID_C,), jnp.float32, -lim_a, lim_a)
        a_b = jax.random.uniform(k5, (), jnp.float32, -lim_a, lim_a)
        lim_fc = np.sqrt(1.0 / IN_C)
        fc_w = jax.random.uniform(k6, (IN_C, HID_C), jnp.float32, -lim_fc, lim_fc)
        fc_b = jax.random.uniform(k7, (HID_C,), jnp.float32, -lim_fc, lim_fc)
        return {'h': h, 'adj': adj, 'W': W, 'a_w': a_w, 'a_b': a_b, 'fc_w': fc_w, 'fc_b': fc_b}
    _L0_gnn_all = _L0_gnn_setup()
    _L0_gnn_in = {k: v for k, v in _L0_gnn_all.items() if k in ('W', 'a_w', 'a_b', 'fc_w', 'fc_b')}
    del _L0_gnn_all

    def _L0_ffn_setup():
        import jax, jax.numpy as jnp
        import numpy as np
        B, T, D, FF, E = (4, 1024, 256, 1024, 8)
        TOP_K = 2
        EPS = 0.01
        key = jax.random.key(seed)
        ks = jax.random.split(key, 7)
        s = 0.02
        return {'x': jax.random.normal(ks[0], (B, T, D), dtype=jnp.float32), 'Wg': jax.random.normal(ks[1], (D, E), dtype=jnp.float32) * s, 'bg': jnp.zeros((E,), dtype=jnp.float32), 'W1': jax.random.normal(ks[2], (E, D, FF), dtype=jnp.float32) * s, 'b1': jnp.zeros((E, FF), dtype=jnp.float32), 'W2': jax.random.normal(ks[3], (E, FF, D), dtype=jnp.float32) * s, 'b2': jnp.zeros((E, D), dtype=jnp.float32)}
    _L0_ffn_all = _L0_ffn_setup()
    _L0_ffn_in = {k: v for k, v in _L0_ffn_all.items() if k in ('Wg', 'bg', 'W1', 'b1', 'W2', 'b2')}
    del _L0_ffn_all
    return {'x': x, 'adj': adj, 'L0_gnn_W': _L0_gnn_in['W'], 'L0_gnn_a_w': _L0_gnn_in['a_w'], 'L0_gnn_a_b': _L0_gnn_in['a_b'], 'L0_gnn_fc_w': _L0_gnn_in['fc_w'], 'L0_gnn_fc_b': _L0_gnn_in['fc_b'], 'L0_ffn_Wg': _L0_ffn_in['Wg'], 'L0_ffn_bg': _L0_ffn_in['bg'], 'L0_ffn_W1': _L0_ffn_in['W1'], 'L0_ffn_b1': _L0_ffn_in['b1'], 'L0_ffn_W2': _L0_ffn_in['W2'], 'L0_ffn_b2': _L0_ffn_in['b2']}

def reference(x, adj, L0_gnn_W, L0_gnn_a_w, L0_gnn_a_b, L0_gnn_fc_w, L0_gnn_fc_b, L0_ffn_Wg, L0_ffn_bg, L0_ffn_W1, L0_ffn_b1, L0_ffn_W2, L0_ffn_b2):
    import jax
    import jax.numpy as jnp

    def _L0_gnn_ref(h, adj, W, a_w, a_b, fc_w, fc_b):
        import jax, jax.numpy as jnp
        import numpy as np
        IN_C, HID_C = (256, 256)
        ALPHA = 0.2
        N = 4096
        NEG_BIG = -9000000000000000.0
        Wh1 = h @ W[:IN_C]
        Wh2 = h @ W[IN_C:]
        s1 = Wh1 @ a_w
        s2 = Wh2 @ a_w
        e = s1[:, None] + s2[None, :] + a_b
        e = jnp.where(e >= 0, e, ALPHA * e)
        e = jnp.where(adj > 0, e, NEG_BIG)
        att = jax.nn.softmax(e, axis=1)
        return att @ (h @ fc_w + fc_b)

    def _L0_ffn_ref(x, Wg, bg, W1, b1, W2, b2):
        import jax, jax.numpy as jnp
        import numpy as np
        B, T, D, FF, E = (4, 1024, 256, 1024, 8)
        TOP_K = 2
        EPS = 0.01
        b, t, d = x.shape
        e = Wg.shape[1]
        logits = jnp.einsum('btd,de->bte', x, Wg) + bg
        gates = jax.nn.softmax(logits, axis=-1)
        vals, idx = jax.lax.top_k(gates, TOP_K)
        vals = vals / (jnp.sum(vals, axis=-1, keepdims=True) + EPS)
        w = jnp.sum(jax.nn.one_hot(idx, e, dtype=x.dtype) * vals[..., None], axis=-2)
        w = w.reshape(-1, e)
        xf = x.reshape(-1, d)
        h = jax.nn.relu(jnp.einsum('nd,edf->enf', xf, W1) + b1[:, None, :])
        y = jnp.einsum('enf,efd->end', h, W2) + b2[:, None, :]
        out = jnp.einsum('ne,end->nd', w, y)
        return out.reshape(b, t, d)
    x = x + _L0_gnn_ref(_layernorm(x, axis=-1), adj, L0_gnn_W, L0_gnn_a_w, L0_gnn_a_b, L0_gnn_fc_w, L0_gnn_fc_b)
    x = x + _L0_ffn_ref(_layernorm(x, axis=-1)[None], L0_ffn_Wg, L0_ffn_bg, L0_ffn_W1, L0_ffn_b1, L0_ffn_W2, L0_ffn_b2)[0]
    return x

_drawn_inputs = setup_inputs


def setup_inputs(seed=0):
    import zlib

    import numpy as np

    out = dict(_drawn_inputs(seed))
    spreads = {'L0_ffn_bg': (0.0, 0.1), 'L0_ffn_b1': (0.0, 0.268), 'L0_ffn_b2': (0.0, 0.1)}
    factors = {}
    for name, (base, spread) in spreads.items():
        noise = np.random.default_rng([zlib.crc32(name.encode()), seed]).standard_normal(out[name].shape)
        drawn = base * np.exp(spread * noise) if base else spread * noise
        out[name] = jnp.asarray(drawn.astype(out[name].dtype))
    for name, factor in factors.items():
        out[name] = (out[name] * factor).astype(out[name].dtype)
    return out
```

```python
from contextlib import ExitStack

import concourse.bass as bass
from concourse import mybir

F32 = mybir.dt.float32
F32R = mybir.dt.float32r
I32 = mybir.dt.int32
ALU = mybir.AluOpType
ACT = mybir.ActivationFunctionType
AXIS = mybir.AxisListType.X

P = 128
SLOPE = 0.2
MASKED = -9000000000000000.0
LN_EPS = 1e-05
GATE_EPS = 0.01
BANK = 512


def graph_attention_experts(nc, x, adj, gnn_w, a_w, a_b, fc_w, fc_b, gate_w, gate_b, w1, b1, w2, b2, out):
    N, D = x.shape
    E, _, FF = w1.shape
    T = N // P
    DB = D // P
    FB = FF // P
    QUADS = N // BANK
    JQ = BANK // P
    TOPK = 2
    PAIRS = TOPK * N
    TILE = 2 * P
    PAIR_TILES = (PAIRS - E) // TILE + E
    SLOTS = 2 * PAIR_TILES
    TE = T * E
    NO_TOKEN = 2.0 * N
    HBANKS = FB // 2
    B2K = 32 + E
    FCK = 33
    EARLY_ROWS, LATE_ROWS = slice(0, T - 2), slice(T - 2, T)
    HOTS = 4
    WARM_START, WARM_CHOICE, WARM_RANK, WARM_GATHER = 38, 26, 22, 24
    CONSTS = 8
    assert D == 256 and N == 2048 and FB == 8 and TE == P

    ctx = ExitStack()
    with ctx:
        def sb(name, shape, dt=F32):
            return ctx.enter_context(nc.sbuf_tensor(name, shape, dt))

        def sem(name):
            return ctx.enter_context(nc.semaphore(name))

        ident = sb("ident", [P, P])
        ones = sb("ones", [P, P])
        below = sb("below", [P, P])
        same_expert = sb("same_expert", [P, E])
        earlier = sb("earlier", [P, T, E])
        column = sb("column", [P, P])
        minus_one = sb("minus_one", [P, 1])
        table_scratch = sb("table_scratch", [P, 1])
        token = sb("token", [P, T])
        id_less = sb("id_less", [P, E])
        tile_limits = sb("tile_limits", [P, E])
        stats = sb("stats", [P, T, 6])
        moments = sb("moments", [P, T, 2])
        spread = sb("spread", [P, T])
        rstd = sb("rstd", [P, T])
        newton = sb("newton", [P, T])
        centre = sb("centre", [P, T])
        s1_pos = sb("s1_pos", [P, T])
        z_max = sb("z_max", [P, 2])
        relu_max = sb("relu_max", [P, 2])
        e_max = sb("e_max", [P, 2])
        neg_max = sb("neg_max", [P, 2])
        half_sums = sb("half_sums", [P, T, 2])
        row_sum = sb("row_sum", [P, T])
        row_rcp = sb("row_rcp", [P, T])
        ab_col = sb("ab_col", [P, 1])
        gate_ws = sb("gate_ws", [P, DB, E])
        gate_bs = sb("gate_bs", [P, E])
        b1_cols = sb("b1_cols", [P, E * FB])
        b2_parts = sb("b2_parts", [B2K, D], F32R)
        row_expert = sb("row_expert", [P, 1])
        b2_choice = sb("b2_choice", [B2K, PAIR_TILES])
        b2_select = sb("b2_select", [B2K, P], F32R)
        tile_expert = sb("tile_expert", [1, PAIR_TILES], I32)
        gather_idx = sb("gather_idx", [P, SLOTS], I32)
        add_idx = sb("add_idx", [P, SLOTS], I32)
        slot_weight = sb("slot_weight", [P, SLOTS])
        gather_now = sb("gather_now", [P, 2, 2], I32)
        add_now = sb("add_now", [P, 2, 2], I32)

        base = (nc.sbuf_base + 31) // 32 * 32

        def at(name, offset, shape, dt=F32):
            return nc.alloc_sbuf_tensor_at(name, shape, dt, offset=base + offset)

        K = 1024
        w1_sb = at("w1_sb", 0, [P, E, DB, FF])
        LOW = E * DB * FF * 4
        w2_sb = at("w2_sb", LOW, [P, E, FB, D])
        A = LOW + E * FB * D * 4
        B, C, X, Z = A + 16 * K, A + 32 * K, A + 48 * K, A + 64 * K
        v_hi = at("v_hi", LOW, [P, T, D], F32R)
        v_lo = at("v_lo", LOW + 16 * K, [P, T, D], F32R)
        s2_rows = at("s2_rows", LOW + 32 * K, [P, N])
        adj_sb = at("adj_sb", LOW + 40 * K, [P, 2, N])
        relu_part = at("relu_part", LOW + 56 * K, [P, N])
        z = at("z", A, [P, 2, N])
        probs = at("probs", B, [P, 2, N])
        pt_hi = at("pt_hi", C, [P, QUADS, BANK], F32R)
        pt_lo = at("pt_lo", C + 8 * K, [P, QUADS, BANK], F32R)
        x_sb = at("x_sb", X, [P, T, D])
        xn_t = at("xn_t", 32 * K, [P, DB, N])
        early = [48 * K]

        def spare(name, shape, dt=F32):
            size = 4
            for n in shape[1:]:
                size *= n
            offset = early[0]
            early[0] = offset + (size + 31) // 32 * 32
            assert early[0] <= LOW
            return at(name, offset, shape, dt)

        fc_ext = spare("fc_ext", [P, DB, D + 1])
        gnn_ws = spare("gnn_ws", [P, 2 * DB, D])
        aw_rows = spare("aw_rows", [P, D])
        products = spare("products", [P, 2 * DB, D])
        c2_cols = spare("c2_cols", [P, DB])
        c2_wide = spare("c2_wide", [P, DB, P])
        fcb_raw = spare("fcb_raw", [FCK, D])
        fcb_parts = spare("fcb_parts", [FCK, D], F32R)
        ones_r = spare("ones_r", [FCK, P], F32R)
        b2_rows = at("b2_rows", Z + 3 * K, [B2K, D])
        b1_raw = at("b1_raw", Z + 2 * K, [E * FB, P])
        xn = at("xn", B, [P, T, D])
        xn2 = at("xn2", A, [P, T, D])
        xn2_t = at("xn2_t", B, [P, DB, N])
        logits_t = at("logits_t", C, [E, N])
        rt = [X]

        def routing(name, shape, dt=F32):
            size = 4
            for n in shape[1:]:
                size *= n
            offset = rt[0]
            rt[0] = offset + (size + 31) // 32 * 32
            assert rt[0] <= Z
            return at(name, offset, shape, dt)

        logits = routing("logits", [P, T, E])
        gates = routing("gates", [P, T, E])
        gates2 = routing("gates2", [P, T, E])
        hots = routing("hots", [P, TOPK, T, E])
        cand = routing("cand", [P, T, E])
        chosen = routing("chosen", [P, T, E])
        picked = routing("picked", [P, TOPK, T, E])
        position = routing("position", [P, T, E])
        totals = routing("totals", [P, P])
        cmp = routing("cmp", [P, E, E])
        top = routing("top", [P, TOPK, T])
        top_id = routing("top_id", [P, TOPK, T])
        top_w = routing("top_w", [P, TOPK, T])
        norm = routing("norm", [P, T])
        tiles_of = routing("tiles_of", [P, E])
        tiles_end = routing("tiles_end", [P, E])
        base_tile = routing("base_tile", [P, E])
        pos = routing("pos", [P, TOPK, T])
        pos_int = routing("pos_int", [P, TOPK, T], I32)
        part_int = routing("part_int", [P, 2, TOPK, T], I32)
        part = routing("part", [P, 2, TOPK, T])
        ended = routing("ended", [P, PAIR_TILES, E - 1])
        ended_sum = routing("ended_sum", [P, PAIR_TILES])
        slots_t = routing("slots_t", [2 * SLOTS, P])
        slot_empty = routing("slot_empty", [P, SLOTS])
        in_row = at("in_row", B, [P, TOPK * T, P])
        in_slot = at("in_slot", Z, [P, TOPK * T, SLOTS])
        slot_vals = at("slot_vals", A, [P, TOPK * T, 2, SLOTS])
        w2_hi = at("w2_hi", A, [P, FB, D], F32R)
        w2_lo = at("w2_lo", A + 8 * K, [P, FB, D], F32R)
        h_hi = at("h_hi", B, [P, FB, TILE], F32R)
        h_lo = at("h_lo", B + 8 * K, [P, FB, TILE], F32R)
        w1_hi = at("w1_hi", C, [P, DB, FF], F32R)
        w1_lo = at("w1_lo", C + 8 * K, [P, DB, FF], F32R)
        xt_hi = at("xt_hi", X, [P, 2, DB, TILE], F32R)
        xt_lo = at("xt_lo", X + 4 * K, [P, 2, DB, TILE], F32R)
        h_full = at("h_full", X + 8 * K, [P, 2, BANK])
        y_sb = at("y_sb", X + 12 * K, [P, 2, 2, D])
        x_rows = at("x_rows", Z, [P, 2, 2, D])

        bank = [ctx.enter_context(nc.psum_tensor(f"bank{i}", [P, BANK], F32)) for i in range(8)]
        turn_bank, attn_bank, wide_bank, value_bank = bank[0:4], bank[4:6], bank[6:8], bank[4:8]
        h_bank, y_bank, xt_bank = bank[0:4], bank[4:6], bank[6:8]

        xn2_dram = nc.dram_tensor("xn2_dram", [N, D], F32).ap()

        x_in = [sem(f"x_in{g}") for g in range(4)]; small_in = sem("small_in"); late_in = sem("late_in")
        adj_in = [sem("adj_in0"), sem("adj_in1")]
        w1_in = sem("w1_in"); w2_in = sem("w2_in"); xn2_out = sem("xn2_out"); out_init = sem("out_init")
        rows_in = [sem("rows_in0"), sem("rows_in1")]; added = sem("added")
        consts = sem("consts"); pool_step = sem("pool_step")
        proj_step = sem("proj_step"); c_ready = sem("c_ready")
        ln_var = sem("ln_var"); ln_std = sem("ln_std"); ln_step = sem("ln_step"); ln_done = sem("ln_done"); xn_odd = sem("xn_odd"); xn_even = sem("xn_even"); centre_ready = sem("centre_ready")
        xt_turned = sem("xt_turned"); xt_even = sem("xt_even"); xt_odd = sem("xt_odd")
        s2_psum = sem("s2_psum"); s2_ready = sem("s2_ready")
        bias_zero = sem("bias_zero"); bias_hi = sem("bias_hi"); bias_ready = sem("bias_ready")
        v_psum = sem("v_psum"); v_hi_ready = sem("v_hi_ready"); v_ready = sem("v_ready")
        b1_turned = sem("b1_turned"); b1_ready = sem("b1_ready")
        s1_ready = sem("s1_ready"); preloaded = sem("preloaded")
        mask_ready = sem("mask_ready"); z_ready = sem("z_ready"); relu_ready = sem("relu_ready")
        e_max_ready = sem("e_max_ready"); e_ready = sem("e_ready"); probs_ready = sem("probs_ready"); sum_ready = sem("sum_ready")
        turned = sem("turned"); pt_hi_ready = sem("pt_hi_ready"); pt_lo_ready = sem("pt_lo_ready")
        attn_psum = sem("attn_psum"); rcp_ready = sem("rcp_ready"); x1_ready = sem("x1_ready")
        logits_psum = sem("logits_psum"); gate_psum = sem("gate_psum"); gate_ready = sem("gate_ready"); route = sem("route"); exp_ready = sem("exp_ready")
        logits_shifted = sem("logits_shifted"); weights_ready = sem("weights_ready")
        chosen_ready = sem("chosen_ready"); totals_psum = sem("totals_psum"); totals_ready = sem("totals_ready")
        position_psum = sem("position_psum"); slots_hot = sem("slots_hot"); rows_hot = sem("rows_hot"); pos_ready = sem("pos_ready"); vals_ready = sem("vals_ready"); slots_psum = sem("slots_psum"); slots_ready = sem("slots_ready"); slots_turned = sem("slots_turned")
        neg_max_ready = sem("neg_max_ready"); b2_zero = sem("b2_zero"); b2_hi = sem("b2_hi"); b2_lo = sem("b2_lo")
        b2_selected = sem("b2_selected"); routed_b1 = sem("routed_b1")
        tables = sem("tables"); experts_known = sem("experts_known"); one_rows = sem("one_rows")
        pool_passed = sem("pool_passed")
        gather_cols = sem("gather_cols"); add_cols = sem("add_cols")
        xt_psum = sem("xt_psum"); x_hi_ready = sem("x_hi_ready"); x_lo_ready = sem("x_lo_ready")
        w1_hi_ready = sem("w1_hi_ready"); w1_lo_ready = sem("w1_lo_ready")
        w2_hi_ready = sem("w2_hi_ready"); w2_lo_ready = sem("w2_lo_ready")
        h_psum = sem("h_psum"); h_full_ready = sem("h_full_ready")
        h_hi_ready = sem("h_hi_ready"); h_lo_ready = sem("h_lo_ready"); h_used = sem("h_used")
        y_ready = sem("y_ready")

        adj_tiles = adj.rearrange("(t p) j -> p t j", p=P)
        x_tiles = x.rearrange("(t p) d -> p t d", p=P)
        out_tiles = out.rearrange("(t p) d -> p t d", p=P)
        xn2_tiles = xn2_dram.rearrange("(t p) d -> p t d", p=P)
        w1_view = w1.rearrange("e (b p) f -> p e b f", p=P)
        w2_view = w2.rearrange("e (b p) d -> p e b d", p=P)

        XG = 4
        SMALL = 6
        LATE = 5

        def per_expert(ap, n=T):
            return ap.unsqueeze(2).to_broadcast([P, n, E])

        block = ctx.enter_context(nc.Block())

        @block.sync
        def _(sp):
            for g in range(XG):
                ts = slice(g * T // XG, (g + 1) * T // XG)
                sp.dma_start(x_sb[:, ts, :], x_tiles[:, ts, :]).then_inc(x_in[g], 16)
            sp.dma_start(gnn_ws[:, :, :], gnn_w.rearrange("(b p) f -> p b f", p=P)).then_inc(small_in, 16)
            sp.dma_start(aw_rows[:, :], a_w.unsqueeze(0).to_broadcast([P, D])).then_inc(small_in, 16)
            sp.dma_start(fc_ext[:, :, 0:D], fc_w.rearrange("(b p) f -> p b f", p=P)).then_inc(small_in, 16)
            sp.dma_start(ab_col[:, :], a_b.unsqueeze(0).to_broadcast([P, 1])).then_inc(small_in, 16)
            sp.wait_ge(bias_zero, 1)
            sp.dma_start(fcb_raw[0:1, :], fc_b.unsqueeze(0)).then_inc(small_in, 16)
            sp.dma_start(fcb_raw[32:33, :], fc_b.unsqueeze(0)).then_inc(small_in, 16)
            for t in range(2):
                sp.dma_start(adj_sb[:, t, :], adj_tiles[:, t, :]).then_inc(adj_in[t], 16)
            sp.dma_start(b1_raw[:, :], b1.rearrange("e (b p) -> (e b) p", p=P)).then_inc(late_in, 16)
            sp.wait_ge(b2_zero, 1)
            sp.dma_start(b2_rows[0:E, :], b2).then_inc(late_in, 16)
            sp.dma_start(b2_rows[32:B2K, :], b2).then_inc(late_in, 16)
            sp.dma_start(gate_ws[:, :, :], gate_w.rearrange("(b p) e -> p b e", p=P)).then_inc(late_in, 16)
            sp.dma_start(gate_bs[:, :], gate_b.unsqueeze(0).to_broadcast([P, E])).then_inc(late_in, 16)

            def load_w1(t, e, half):
                sp.dma_start(w1_sb[:, e, half, :], w1_view[:, e, half, :]).then_inc(w1_in, 16)

            with sp.Fori(0, T // 2 - 1) as k:
                for par in range(2):
                    sp.wait_ge(z_ready, 2 * k + par + 1)
                    sp.dma_start(adj_sb[:, par, :], adj_tiles[:, bass.ds(2 * k + par + 2, 1), :])\
                        .then_inc(adj_in[par], 16)
                    sp.dma_start(w1_sb[:, bass.ds(k, 1), par, :], w1_view[:, bass.ds(k, 1), par, :])\
                        .then_inc(w1_in, 16)
            for half in range(DB):
                sp.dma_start(w1_sb[:, E - 1, half, :], w1_view[:, E - 1, half, :]).then_inc(w1_in, 16)
            for g in range(XG):
                ts = slice(g * T // XG, (g + 1) * T // XG)
                sp.wait_ge(x1_ready, (g + 1) * T // XG)
                sp.dma_start(out_tiles[:, ts, :], x_sb[:, ts, :]).then_inc(out_init, 16)
            sp.wait_ge(attn_psum, T)
            sp.wait_ge(e_ready, 2 * T)
            sp.wait_ge(z_ready, T)
            for g in range(XG):
                ts = slice(g * T // XG, (g + 1) * T // XG)
                sp.wait_ge(xn_even, T // 2 + 2 * g + 2)
                sp.wait_ge(xn_odd, T // 2 + 2 * g + 2)
                sp.dma_start(xn2_tiles[:, ts, :], xn2[:, ts, :]).then_inc(xn2_out, 16)
            for e in range(E):
                sp.dma_start(w2_sb[:, e, :, :], w2_view[:, e, :, :]).then_inc(w2_in, 16)
            sp.wait_ge(out_init, 16 * XG)
            sp.wait_ge(added, 32 * PAIR_TILES)

        @block.gpsimd
        def _(pool):
            steps = [0]

            def after(instruction):
                instruction.then_inc(pool_step, 1)
                steps[0] += 1
                pool.wait_ge(pool_step, steps[0])

            pool.memset(ident[:, :], 0.0).then_inc(pool_step, 1)
            pool.memset(ones[:, :], 1.0).then_inc(pool_step, 1)
            pool.memset(fcb_raw[:, :], 0.0).then_inc(bias_zero, 1)
            pool.wait_ge(pool_step, 2)
            steps[0] = 2
            pool.affine_select(out=ident[:, :], in_=ident[:, :], compare_op=ALU.not_equal, fill=1.0, base=0,
                               pattern=[[-1, P]], channel_multiplier=1).then_inc(consts, 1)
            pool.affine_select(out=below[:, :], in_=ones[:, :], compare_op=ALU.is_gt, fill=0.0, base=0,
                               pattern=[[1, P]], channel_multiplier=-1).then_inc(consts, 1)
            pool.iota(column[:, :], [[1, P]], base=0, channel_multiplier=0,
                      allow_small_or_imprecise_dtypes=True).then_inc(consts, 1)
            pool.iota(token[:, :], [[P, T]], base=1, channel_multiplier=1,
                      allow_small_or_imprecise_dtypes=True).then_inc(consts, 1)
            pool.iota(id_less[:, :], [[1, E]], base=-E, channel_multiplier=0,
                      allow_small_or_imprecise_dtypes=True).then_inc(consts, 1)
            pool.iota(tile_limits[:, :], [[TILE, E]], base=0, channel_multiplier=0,
                      allow_small_or_imprecise_dtypes=True).then_inc(consts, 1)

            pool.iota(row_expert[:, :], [[0, 1]], base=0, channel_multiplier=1,
                      allow_small_or_imprecise_dtypes=True).then_inc(consts, 1)
            pool.memset(minus_one[:, :], -1.0).then_inc(consts, 1)
            pool.memset(b2_rows[:, :], 0.0).then_inc(b2_zero, 1)

            pool.wait_ge(consts, CONSTS)

            def total(t):
                pool.wait_ge(probs_ready, 2 * t + 2)
                pool.tensor_tensor(row_sum[:, bass.ds(t, 1)], half_sums[:, bass.ds(t, 1), 0],
                                   half_sums[:, bass.ds(t, 1), 1], ALU.add).then_inc(sum_ready, 1)

            def leaky(t, par):
                pool.wait_ge(relu_ready, 3 * t + 1)
                pool.tensor_tensor(e_max[:, par:par + 1], z_max[:, par:par + 1],
                                   relu_max[:, par:par + 1], ALU.add).then_inc(e_max_ready, 1)
                pool.wait_ge(e_max_ready, t + 1)
                pool.tensor_tensor(neg_max[:, par:par + 1], e_max[:, par:par + 1], minus_one[:, :], ALU.mult)\
                    .then_inc(neg_max_ready, 1)
                for half in range(2):
                    cols = slice(half * N // 2, (half + 1) * N // 2)
                    pool.wait_ge(relu_ready, 3 * t + 2 + half)
                    pool.tensor_tensor(z[:, par, cols], z[:, par, cols], relu_part[:, cols], ALU.add)\
                        .then_inc(e_ready, 1)

            leaky(0, 0)
            leaky(1, 1)
            with pool.Fori(1, T // 2) as k:
                for par in range(2):
                    total(2 * k + par - 2)
                    leaky(2 * k + par, par)
            total(T - 2)
            total(T - 1)

            kt = TOPK * T
            top_w_pairs = top_w[:, :, :].rearrange("p k t -> p (k t)").unsqueeze(2).to_broadcast([P, kt, SLOTS])
            pool.wait_ge(xn2_out, 16 * XG)
            for g in range(HOTS):
                ks = slice(g * kt // HOTS, (g + 1) * kt // HOTS)
                ts = slice(g * kt // HOTS % T, g * kt // HOTS % T + kt // HOTS)
                pool.wait_ge(slots_hot, g + 1)
                pool.tensor_tensor(slot_vals[:, ks, 0, :], in_slot[:, ks, :],
                                   token[:, ts].unsqueeze(2).to_broadcast([P, kt // HOTS, SLOTS]), ALU.mult)\
                    .then_inc(vals_ready, 1)
                pool.tensor_tensor(slot_vals[:, ks, 1, :], in_slot[:, ks, :], top_w_pairs[:, ks, :], ALU.mult)\
                    .then_inc(vals_ready, 1)

            pool.wait_ge(tables, 1)
            pool.wait_ge(slots_psum, 1)

            def gather(t, par):
                pool.tensor_copy(gather_now[:, par, :], gather_idx[:, bass.ds(2 * t, 2)]).then_inc(gather_cols, 1)
                pool.wait_ge(xn2_out, 16 * XG)
                pool.wait_ge(gather_cols, t + 1)
                pool.sem_inc(pool_passed, 1)
                for h in range(2):
                    pool.indirect_dma_start(
                        out=x_rows[:, par, h, :], out_offset=None, in_=xn2_dram,
                        in_offset=bass.IndirectOffsetOnAxis(ap=gather_now[:, par, h:h + 1], axis=0))\
                        .then_inc(rows_in[par], 16)

            def add(t, par):
                pool.tensor_copy(add_now[:, par, :], add_idx[:, bass.ds(2 * t, 2)]).then_inc(add_cols, 1)
                pool.wait_ge(add_cols, t + 1)
                pool.wait_ge(y_ready, 2 * t + 2)
                pool.wait_ge(out_init, 16 * XG)
                if not isinstance(t, int) or t > 0:
                    pool.wait_ge(added, 32 * t)
                    pool.sem_inc(pool_passed, 1)
                for h in range(2):
                    pool.indirect_dma_start(
                        out=out, out_offset=bass.IndirectOffsetOnAxis(ap=add_now[:, par, h:h + 1], axis=0),
                        in_=y_sb[:, par, h, :], in_offset=None, bounds_check=N - 1, oob_is_err=False,
                        compute_op=ALU.add).then_inc(added, 16)

            def step(t, par):
                if not isinstance(t, int) or t + 3 < PAIR_TILES:
                    if not isinstance(t, int) or t + 3 >= 2:
                        pool.wait_ge(xt_psum, t + 2)
                    gather(t + 3, 1 - par)
                if not isinstance(t, int) or t >= 1:
                    add(t - 1, 1 - par)

            gather(0, 0)
            gather(1, 1)
            pool.wait_ge(tables, 3)
            step(-1, 1)
            for t in range(0, 2):
                step(t, t % 2)
            with pool.Fori(1, PAIR_TILES // 2 - 1) as k:
                for par in range(2):
                    step(2 * k + par, par)
            for t in range(2 * (PAIR_TILES // 2 - 1), PAIR_TILES + 1):
                step(t, t % 2)

        def evict_turned(eng, stage, unit, copy, done, dst):
            g, b = unit // DB, unit % DB
            eng.wait_ge(xt_turned, stage * DB * QUADS + unit + 1)
            copy(dst[:, b, g * BANK:(g + 1) * BANK], turn_bank[unit % 4][:, :]).then_inc(done, 1)

        @block.scalar
        def _(act):
            def copy(dst, src):
                return act.activation(dst, src, ACT.Copy)

            def square_root(n, ts):
                act.wait_ge(ln_var, n)
                act.activation(spread[:, ts], newton[:, ts], ACT.Sqrt).then_inc(ln_std, 1)

            def preload(func, n):
                act.wait_ge(preloaded, n)
                act.activation(table_scratch[:, :], minus_one[:, :] if func == ACT.Exp else ones[:, 0:1], func)\
                    .then_inc(preloaded, 1)

            def normalise(t, dst, done):
                act.activation(dst[:, t, :], x_sb[:, t, :], ACT.Identity, scale=rstd[:, t:t + 1],
                               bias=centre[:, t:t + 1]).then_inc(done, 1)

            def relu_row(t, par):
                act.wait_ge(z_ready, t + 1)
                act.activation(relu_max[:, par:par + 1], z_max[:, par:par + 1], ACT.Relu,
                               scale=(1 - SLOPE) / SLOPE, bias=s1_pos[:, bass.ds(t, 1)]).then_inc(relu_ready, 1)

            def relu(t, par, half):
                cols = slice(half * N // 2, (half + 1) * N // 2)
                act.activation(relu_part[:, cols], z[:, par, cols], ACT.Relu, scale=(1 - SLOPE) / SLOPE,
                               bias=s1_pos[:, bass.ds(t, 1)]).then_inc(relu_ready, 1)

            def exponent(t, par, half):
                cols = slice(half * N // 2, (half + 1) * N // 2)
                act.wait_ge(e_ready, 2 * t + half + 1)
                if half == 0:
                    act.wait_ge(neg_max_ready, t + 1)
                if not isinstance(t, int) or t > 1:
                    act.wait_ge(turned, 4 * t + 2 * half - 6)
                act.activation(probs[:, par, cols], z[:, par, cols], ACT.Exp, bias=neg_max[:, par:par + 1],
                               accum_out=half_sums[:, bass.ds(t, 1), half]).then_inc(probs_ready, 1)

            def round_turned(t, q):
                act.wait_ge(turned, 4 * t + q + 1)
                copy(pt_hi[:, q, :], turn_bank[q][:, :]).then_inc(pt_hi_ready, 1)

            def attention(t, par):
                static = isinstance(t, int)
                here = not static or t >= 0
                following = not static or t + 1 < T
                ahead = not static or t + 2 < T
                if following:
                    exponent(t + 1, 1 - par, 0)
                if here:
                    round_turned(t, 2)
                if ahead:
                    relu_row(t + 2, par)
                    relu(t + 2, par, 0)
                if here:
                    round_turned(t, 3)
                if following:
                    exponent(t + 1, 1 - par, 1)
                if following:
                    round_turned(t + 1, 0)
                if ahead:
                    relu(t + 2, par, 1)
                if following:
                    round_turned(t + 1, 1)

            square_root(1, slice(0, T))
            act.wait_ge(centre_ready, 1)
            for t in range(1, T, 2):
                normalise(t, xn, xn_odd)
            for unit in range(0, DB * QUADS, 2):
                evict_turned(act, 0, unit, copy, xt_even, xn_t)
            preload(ACT.Exp, 0)
            for c in range(QUADS):
                act.wait_ge(s2_psum, c + 1)
                act.activation(s2_rows[:, c * BANK:(c + 1) * BANK], wide_bank[c % 2][:, :], ACT.Copy, scale=SLOPE)\
                    .then_inc(s2_ready, 1)

            def round_value(t):
                act.wait_ge(v_psum, t + 1)
                copy(v_hi[:, t, :], value_bank[t % 4][:, 0:D]).then_inc(v_hi_ready, 1)

            for t in range(0, 2):
                round_value(t)
            act.wait_ge(s1_ready, 1)
            relu_row(0, 0)
            relu(0, 0, 0)
            for t in range(2, 4):
                round_value(t)
            relu(0, 0, 1)
            for t in range(4, 8):
                round_value(t)
            exponent(0, 0, 0)
            act.wait_ge(s1_ready, 2)
            relu_row(1, 1)
            relu(1, 1, 0)
            for t in range(8, 10):
                round_value(t)
            exponent(0, 0, 1)
            for t in range(10, 12):
                round_value(t)
            relu(1, 1, 1)
            round_value(12)
            round_turned(0, 0)
            round_value(13)
            round_turned(0, 1)
            for t in range(14, T):
                round_value(t)

            act.wait_ge(s1_ready, T)
            for t in range(0, 2):
                attention(t, t % 2)
            with act.Fori(1, T // 2 - 2) as k:
                for par in range(2):
                    attention(2 * k + par, par)
            for t in range(T - 4, T - 1):
                attention(t, t % 2)
            square_root(2, EARLY_ROWS)
            attention(T - 1, 1)
            act.wait_ge(centre_ready, 2)
            for t in range(1, T - 2, 2):
                normalise(t, xn2, xn_odd)
            square_root(3, LATE_ROWS)
            evict_turned(act, 1, 0, copy, xt_even, xn2_t)
            evict_turned(act, 1, 1, copy, xt_odd, xn2_t)
            act.wait_ge(centre_ready, 3)
            normalise(T - 1, xn2, xn_odd)
            def gate_rows(g):
                act.wait_ge(gate_psum, g + 1)
                copy(logits_t[:, g * BANK:(g + 1) * BANK], wide_bank[g % 2][0:E, :]).then_inc(gate_ready, 1)

            for g in range(1, QUADS):
                evict_turned(act, 1, DB * g, copy, xt_even, xn2_t)
                gate_rows(g - 1)
            gate_rows(QUADS - 1)
            preload(ACT.Exp, 1)

            act.wait_ge(logits_shifted, 1)
            act.activation(gates2[:, :, :], logits[:, :, :], ACT.Exp).then_inc(exp_ready, 1)
            act.wait_ge(totals_psum, 1)
            copy(totals[:, :], wide_bank[0][:, 0:P]).then_inc(totals_ready, 1)
            act.wait_ge(b1_turned, 1)
            copy(b1_cols[:, :], wide_bank[1][:, 0:E * FB]).then_inc(b1_ready, 1)

            act.wait_ge(experts_known, 1)
            act.wait_ge(w1_in, 16 * DB * E)
            act.wait_ge(b1_ready, 1)

            def expert_of(t):
                return act.value_load(tile_expert[0:1, bass.ds(t, 1)], min_val=0, max_val=E - 1)

            def round_w1(t, c, e):
                cols = slice(c * FF // 2, (c + 1) * FF // 2)
                if not isinstance(t, int) or t > 0:
                    act.wait_ge(h_psum, 4 * t + 2 * c - 2)
                copy(w1_hi[:, :, cols].unsqueeze(1), w1_sb[:, bass.ds(e, 1), :, cols]).then_inc(w1_hi_ready, 1)

            def round_w2(t, c, e):
                rows = slice(c * FB // 2, (c + 1) * FB // 2)
                if not isinstance(t, int) or t > 0:
                    act.wait_ge(h_used, 4 * t + 2 * c - 2)
                copy(w2_hi[:, rows, :].unsqueeze(1), w2_sb[:, bass.ds(e, 1), rows, :]).then_inc(w2_hi_ready, 1)

            def round_x(t, par):
                act.wait_ge(xt_psum, t + 1)
                if not isinstance(t, int) or t > 1:
                    act.wait_ge(h_psum, 4 * t - 4)
                copy(xt_hi[:, par, :, :], xt_bank[par][:, :].rearrange("p (b n) -> p b n", b=DB))\
                    .then_inc(x_hi_ready, 1)

            def bias_relu(t, b, e):
                act.wait_ge(h_psum, 4 * t + b + 1)
                if not (isinstance(t, int) and t == 0 and b < 2):
                    act.wait_ge(h_lo_ready, 4 * t + b - 1)
                for i in range(2):
                    fb = 2 * b + i
                    act.activation(h_full[:, b % 2, i * TILE:(i + 1) * TILE], h_bank[b][:, i * TILE:(i + 1) * TILE],
                                   ACT.Relu, bias=b1_cols[:, bass.ds(e * FB + fb, 1)])\
                        .then_inc(h_full_ready, 1)

            def weigh(t, par):
                act.wait_ge(h_used, 4 * t + 4)
                if not isinstance(t, int) or t > 1:
                    act.wait_ge(added, 32 * t - 32)
                for h in range(2):
                    act.activation(y_sb[:, par, h, :], y_bank[h][:, 0:D], ACT.Copy,
                                   scale=slot_weight[:, bass.ds(2 * t + h, 1)]).then_inc(y_ready, 1)

            e_first = expert_of(0)
            round_w1(0, 0, e_first)
            round_w1(0, 1, e_first)
            act.wait_ge(slots_psum, 1)
            copy(slots_t[:, :], attn_bank[0][0:2 * SLOTS, 0:P]).then_inc(slots_ready, 1)

            def step(t, par):
                static = isinstance(t, int)
                if not static or t >= 1:
                    weigh(t - 1, 1 - par)
                if not static or 0 <= t < PAIR_TILES:
                    if static and t == 0:
                        act.wait_ge(w2_in, 16 * E)
                    e = expert_of(t)
                    round_w2(t, 0, e)
                    round_w2(t, 1, e)
                hidden = not static or 0 <= t + 1 < PAIR_TILES
                ahead = not static or t + 2 < PAIR_TILES
                e_next = expert_of(t + 1) if hidden else None
                split_w1 = ahead and not (static and t == -2)
                x_first = static and t == -1
                e_ahead = expert_of(t + 2) if split_w1 else None
                if x_first:
                    round_x(t + 2, par)
                if hidden:
                    bias_relu(t + 1, 0, e_next)
                if split_w1:
                    round_w1(t + 2, 0, e_ahead)
                if hidden:
                    bias_relu(t + 1, 1, e_next)
                if split_w1:
                    round_w1(t + 2, 1, e_ahead)
                if ahead and not x_first:
                    round_x(t + 2, par)
                if hidden:
                    bias_relu(t + 1, 2, e_next)
                    bias_relu(t + 1, 3, e_next)

            act.wait_ge(out_init, 16 * XG)
            for t in range(-2, 2):
                step(t, t % 2)
            with act.Fori(1, PAIR_TILES // 2 - 1) as k:
                for par in range(2):
                    step(2 * k + par, par)
            for t in range(2 * (PAIR_TILES // 2 - 1), PAIR_TILES + 1):
                step(t, t % 2)

        @block.vector
        def _(vec):
            steps = [0]

            def after(instruction):
                instruction.then_inc(route, 1)
                steps[0] += 1
                vec.wait_ge(route, steps[0])

            def row_moments(stage, ts):
                for t in range(T)[ts]:
                    vec.wait_ge(ln_step, stage * T + t + 1)
                    vec.bn_aggr(moments[:, t, :], stats[:, t, :]).then_inc(ln_done, 1)
                vec.wait_ge(ln_done, stage * T + ts.stop)
                vec.tensor_scalar(newton[:, ts], moments[:, ts, 1], LN_EPS, None, ALU.add).then_inc(ln_var, 1)

            def inverse_root(n, ts):
                vec.wait_ge(ln_std, n)
                after(vec.reciprocal(rstd[:, ts], spread[:, ts]))
                after(vec.tensor_tensor(spread[:, ts], rstd[:, ts], rstd[:, ts], ALU.mult))
                after(vec.tensor_tensor(spread[:, ts], spread[:, ts], newton[:, ts], ALU.mult))
                after(vec.tensor_scalar(spread[:, ts], spread[:, ts], -0.5, 1.5, ALU.mult, ALU.add))
                after(vec.tensor_tensor(rstd[:, ts], rstd[:, ts], spread[:, ts], ALU.mult))
                vec.scalar_tensor_tensor(centre[:, ts], moments[:, ts, 0], -1.0, rstd[:, ts], ALU.mult, ALU.mult)\
                    .then_inc(centre_ready, 1)

            def normalise(t, dst):
                vec.tensor_scalar(dst[:, t, :], x_sb[:, t, :], moments[:, t, 0:1], rstd[:, t:t + 1],
                                  ALU.subtract, ALU.mult).then_inc(xn_even, 1)

            def statistics(t):
                vec.bn_stats(stats[:, bass.ds(t, 1), :], x_sb[:, bass.ds(t, 1), :]).then_inc(ln_step, 1)

            for g in range(XG):
                vec.wait_ge(x_in[g], 16)
                for t in range(g * T // XG, (g + 1) * T // XG):
                    statistics(t)
            row_moments(0, slice(0, T))
            inverse_root(1, slice(0, T))
            for t in range(0, T, 2):
                normalise(t, xn)
            vec.wait_ge(small_in, 16 * SMALL)
            for b in range(2 * DB):
                dst = fc_ext[:, b, D:D + 1] if b < DB else c2_cols[:, b - DB:b - DB + 1]
                vec.tensor_tensor_reduce(products[:, b, :], gnn_ws[:, b, :], aw_rows[:, :], 1.0, 0.0,
                                         ALU.mult, ALU.add, dst).then_inc(proj_step, 1)
            vec.wait_ge(proj_step, 2 * DB)
            vec.wait_ge(consts, CONSTS)
            for b in range(DB):
                vec.tensor_scalar(c2_wide[:, b, :], ones[:, :], c2_cols[:, b:b + 1], None, ALU.mult)\
                    .then_inc(c_ready, 1)
            for unit in range(1, DB * QUADS, 2):
                evict_turned(vec, 0, unit, vec.tensor_copy, xt_odd, xn_t)
            vec.tensor_copy(ones_r[:, :], ones[0:FCK, :]).then_inc(one_rows, 1)
            vec.tensor_copy(fcb_parts[:, :], fcb_raw[:, :]).then_inc(bias_hi, 1)
            vec.wait_ge(bias_hi, 1)
            vec.tensor_tensor(fcb_parts[32:FCK, :], fcb_raw[32:FCK, :], fcb_parts[32:FCK, :].bitcast(F32),
                              ALU.subtract).then_inc(bias_ready, 1)

            def mask(t, par, turn):
                vec.wait_ge(adj_in[par], 16 * turn + 16)
                vec.tensor_scalar(adj_sb[:, par, :], adj_sb[:, par, :], 0.0, MASKED, ALU.is_le, ALU.mult)\
                    .then_inc(mask_ready, 1)

            def masked(t):
                vec.wait_ge(mask_ready, t + 1)
                if not isinstance(t, int) or t > 1:
                    vec.wait_ge(probs_ready, 2 * t - 2)

            def spread_s2(t, par):
                vec.tensor_tensor_reduce(z[:, par, :], adj_sb[:, par, :], s2_rows[:, :], 1.0, -3.0e38,
                                         ALU.add, ALU.max, z_max[:, par:par + 1]).then_inc(z_ready, 1)

            def rest_turned(t, q):
                vec.wait_ge(pt_hi_ready, 4 * t + q + 1)
                vec.tensor_tensor(pt_lo[:, q, :], turn_bank[q][:, :], pt_hi[:, q, :].bitcast(F32), ALU.subtract)\
                    .then_inc(pt_lo_ready, 1)

            def finish_rows(t, par):
                vec.wait_ge(sum_ready, t + 1)
                vec.reciprocal(row_rcp[:, bass.ds(t, 1)], row_sum[:, bass.ds(t, 1)]).then_inc(rcp_ready, 1)
                vec.wait_ge(attn_psum, t + 1)
                vec.wait_ge(rcp_ready, t + 1)
                vec.scalar_tensor_tensor(x_sb[:, bass.ds(t, 1), :], attn_bank[par][:, 0:D].unsqueeze(1),
                                         row_rcp[:, bass.ds(t, 1)], x_sb[:, bass.ds(t, 1), :],
                                         ALU.mult, ALU.add).then_inc(x1_ready, 1)

            def attention(t, par, half):
                static = isinstance(t, int)
                here = not static or t >= 0
                following = not static or t + 1 < T
                ahead = not static or t + 3 < T
                if here:
                    rest_turned(t, 2)
                if not static or t > 0:
                    finish_rows(t - 1, 1 - par)
                if ahead:
                    mask(t + 3, 1 - par, half + (3 + par) // 2)
                    masked(t + 3)
                if not static or t > 0:
                    vec.wait_ge(x1_ready, t)
                    statistics(t - 1)
                if here:
                    rest_turned(t, 3)
                if following:
                    rest_turned(t + 1, 0)
                if ahead:
                    spread_s2(t + 3, 1 - par)
                if following:
                    rest_turned(t + 1, 1)

            def rest_value(t):
                vec.wait_ge(v_hi_ready, t + 1)
                vec.tensor_scalar(s1_pos[:, t:t + 1], value_bank[t % 4][:, D:D + 1], ab_col[:, :], 1 - SLOPE,
                                  ALU.add, ALU.mult).then_inc(s1_ready, 1)
                vec.tensor_tensor(v_lo[:, t, :], value_bank[t % 4][:, 0:D], v_hi[:, t, :].bitcast(F32),
                                  ALU.subtract).then_inc(v_ready, 1)

            for t in range(2):
                mask(t, t, 0)
            after(vec.tensor_reduce(same_expert[:, :], ident[:, :].rearrange("p (t e) -> p e t", e=E), AXIS, ALU.add))
            after(vec.tensor_tensor(earlier[:, :, :], below[:, :].rearrange("p (t e) -> p t e", e=E),
                                    same_expert[:, :].unsqueeze(1).to_broadcast([P, T, E]), ALU.mult))
            vec.wait_ge(late_in, 16 * LATE)
            vec.tensor_copy(b2_parts[:, :], b2_rows[:, :]).then_inc(b2_hi, 1)
            vec.wait_ge(b2_hi, 1)
            vec.tensor_tensor(b2_parts[32:B2K, :], b2_rows[32:B2K, :], b2_parts[32:B2K, :].bitcast(F32),
                              ALU.subtract).then_inc(b2_lo, 1)
            vec.wait_ge(s2_ready, QUADS)
            masked(0)
            spread_s2(0, 0)
            for t in range(0, 4):
                rest_value(t)
            spread_s2(1, 1)
            for t in range(4, 8):
                rest_value(t)
            mask(2, 0, 1)
            for t in range(8, 12):
                rest_value(t)
            masked(2)
            spread_s2(2, 0)
            rest_value(12)
            rest_turned(0, 0)
            rest_value(13)
            rest_turned(0, 1)
            for t in range(14, T):
                rest_value(t)
            for t in range(0, 2):
                attention(t, t % 2, t // 2)
            with vec.Fori(1, T // 2 - 2) as k:
                for par in range(2):
                    attention(2 * k + par, par, k)
            for t in range(T - 4, T - 1):
                attention(t, t % 2, t // 2)
            row_moments(1, EARLY_ROWS)
            rest_turned(T - 1, 2)
            inverse_root(2, EARLY_ROWS)
            rest_turned(T - 1, 3)
            finish_rows(T - 2, 0)
            vec.wait_ge(probs_ready, 2 * T)
            for t in range(0, T - 2, 2):
                normalise(t, xn2)
            vec.wait_ge(x1_ready, T - 1)
            statistics(T - 2)
            finish_rows(T - 1, 1)
            vec.wait_ge(x1_ready, T)
            statistics(T - 1)
            row_moments(1, LATE_ROWS)
            inverse_root(3, LATE_ROWS)
            normalise(T - 2, xn2)
            vec.wait_ge(xt_odd, QUADS + 1)
            for unit in range(3, DB * QUADS, 2):
                evict_turned(vec, 1, unit, vec.tensor_copy, xt_odd, xn2_t)

            def grid(ap, axis):
                return ap.unsqueeze(axis).to_broadcast([P, T, E])

            vec.wait_ge(out_init, 16 * XG)
            vec.wait_ge(logits_psum, 1)
            after(vec.tensor_tensor(logits[:, :, :], attn_bank[0][:, 0:TE].rearrange("p (t e) -> p t e", e=E),
                                    grid(gate_bs[:, :], 1), ALU.add))
            after(vec.tensor_reduce(norm[:, :], logits[:, :, :], AXIS, ALU.max))
            vec.tensor_tensor(logits[:, :, :], logits[:, :, :], grid(norm[:, :], 2), ALU.subtract)\
                .then_inc(logits_shifted, 1)
            vec.wait_ge(exp_ready, 1)
            after(vec.tensor_reduce(norm[:, :], gates2[:, :, :], AXIS, ALU.add))
            after(vec.reciprocal(norm[:, :], norm[:, :]))
            after(vec.tensor_tensor(gates[:, :, :], gates2[:, :, :], grid(norm[:, :], 2), ALU.mult))

            def choose(k, src, hot):
                after(vec.tensor_reduce(top[:, k, :], src, AXIS, ALU.max))
                after(vec.tensor_tensor(cand[:, :, :], src, grid(top[:, k, :], 2), ALU.is_equal))
                after(vec.tensor_tensor(cand[:, :, :], cand[:, :, :], grid(id_less[:, :], 1), ALU.mult))
                after(vec.tensor_reduce(top_id[:, k, :], cand[:, :, :], AXIS, ALU.min))
                after(vec.tensor_tensor(hot, grid(id_less[:, :], 1), grid(top_id[:, k, :], 2), ALU.is_equal))

            choose(0, gates[:, :, :], hots[:, 0, :, :])
            after(vec.scalar_tensor_tensor(gates2[:, :, :], hots[:, 0, :, :], -2.0, gates[:, :, :], ALU.mult, ALU.add))
            choose(1, gates2[:, :, :], hots[:, 1, :, :])
            vec.tensor_tensor(chosen[:, :, :], hots[:, 0, :, :], hots[:, 1, :, :], ALU.add).then_inc(chosen_ready, 1)
            after(vec.tensor_tensor(norm[:, :], top[:, 0, :], top[:, 1, :], ALU.add))
            after(vec.tensor_scalar(norm[:, :], norm[:, :], GATE_EPS, None, ALU.add))
            after(vec.reciprocal(norm[:, :], norm[:, :]))
            after(vec.tensor_tensor(top_w[:, :, :], top[:, :, :],
                                    norm[:, :].unsqueeze(1).to_broadcast([P, TOPK, T]), ALU.mult))

            vec.wait_ge(position_psum, 1)
            after(vec.tensor_tensor(cmp[:, :, :], attn_bank[1][:, TE:TE + E].unsqueeze(2).to_broadcast([P, E, E]),
                                    tile_limits[:, :].unsqueeze(1).to_broadcast([P, E, E]), ALU.is_gt))
            after(vec.tensor_reduce(tiles_of[:, :], cmp[:, :, :], AXIS, ALU.add))
            after(vec.tensor_tensor_scan(tiles_end[:, :], ones[:, 0:E], tiles_of[:, :], 0.0, ALU.mult, ALU.add))
            after(vec.tensor_tensor(base_tile[:, :], tiles_end[:, :], tiles_of[:, :], ALU.subtract))
            after(vec.scalar_tensor_tensor(position[:, :, :], grid(base_tile[:, :], 1), float(TILE),
                                           attn_bank[1][:, 0:TE].rearrange("p (t e) -> p t e", e=E),
                                           ALU.mult, ALU.add))
            after(vec.tensor_tensor(picked[:, :, :, :],
                                    position[:, :, :].unsqueeze(1).to_broadcast([P, TOPK, T, E]),
                                    hots[:, :, :, :], ALU.mult))
            after(vec.tensor_reduce(pos[:, :, :], picked[:, :, :, :], AXIS, ALU.add))
            after(vec.tensor_copy(pos_int[:, :, :], pos[:, :, :]))
            vec.tensor_scalar(part_int[:, 0, :, :], pos_int[:, :, :], P - 1, None, ALU.bitwise_and).then_inc(route, 1)
            steps[0] += 1
            after(vec.tensor_scalar(part_int[:, 1, :, :], pos_int[:, :, :], P.bit_length() - 1, None,
                                    ALU.logical_shift_right))
            after(vec.tensor_copy(part[:, :, :, :], part_int[:, :, :, :]))
            kt = TOPK * T

            def pairs(ap, n):
                return ap.rearrange("p k t -> p (k t)").unsqueeze(2).to_broadcast([P, kt, n])

            for g in range(HOTS):
                ks = slice(g * kt // HOTS, (g + 1) * kt // HOTS)
                vec.tensor_tensor(in_slot[:, ks, :], column[:, 0:SLOTS].unsqueeze(1).to_broadcast([P, kt // HOTS, SLOTS]),
                                  pairs(part[:, 1, :, :], SLOTS)[:, ks, :], ALU.is_equal).then_inc(slots_hot, 1)
                vec.tensor_tensor(in_row[:, ks, :], column[:, :].unsqueeze(1).to_broadcast([P, kt // HOTS, P]),
                                  pairs(part[:, 0, :, :], P)[:, ks, :], ALU.is_equal).then_inc(rows_hot, 1)
            after(vec.tensor_tensor(ended[:, :, :],
                                    tiles_end[:, 0:E - 1].unsqueeze(1).to_broadcast([P, PAIR_TILES, E - 1]),
                                    column[:, 0:PAIR_TILES].unsqueeze(2).to_broadcast([P, PAIR_TILES, E - 1]),
                                    ALU.is_le))
            after(vec.tensor_reduce(ended_sum[:, :], ended[:, :, :], AXIS, ALU.add))
            vec.tensor_copy(tile_expert[:, :], ended_sum[0:1, :]).then_inc(experts_known, 1)
            after(vec.tensor_scalar(row_expert[32:64, :], row_expert[32:64, :], -32.0, None, ALU.add))
            after(vec.tensor_scalar(b2_choice[:, :], ended_sum[0:B2K, :], row_expert[0:B2K, :], None, ALU.is_equal))

            vec.wait_ge(experts_known, 1)

            def expert_of(t):
                return vec.value_load(tile_expert[0:1, bass.ds(t, 1)], min_val=0, max_val=E - 1)

            def rest_w1(t, c, e):
                cols = slice(c * FF // 2, (c + 1) * FF // 2)
                vec.wait_ge(w1_hi_ready, 2 * t + c + 1)
                vec.tensor_tensor(w1_lo[:, :, cols].unsqueeze(1), w1_sb[:, bass.ds(e, 1), :, cols],
                                  w1_hi[:, :, cols].bitcast(F32).unsqueeze(1), ALU.subtract).then_inc(w1_lo_ready, 1)

            e_first = expert_of(0)
            rest_w1(0, 0, e_first)

            vec.wait_ge(slots_turned, 1)
            slot_token = attn_bank[1][:, 0:SLOTS]
            vec.tensor_scalar(gather_idx[:, :], slot_token, -1.0, 0.0, ALU.add, ALU.max).then_inc(tables, 1)
            after(vec.tensor_scalar(slot_empty[:, :], slot_token, 0.0, NO_TOKEN, ALU.is_equal, ALU.mult))
            vec.scalar_tensor_tensor(add_idx[:, :], slot_token, -1.0, slot_empty[:, :], ALU.add, ALU.add)\
                .then_inc(tables, 1)
            vec.tensor_copy(slot_weight[:, :], attn_bank[1][:, SLOTS:2 * SLOTS]).then_inc(tables, 1)
            rest_w1(0, 1, e_first)

            def rest_w2(t, c, e):
                rows = slice(c * FB // 2, (c + 1) * FB // 2)
                vec.wait_ge(w2_hi_ready, 2 * t + c + 1)
                vec.tensor_tensor(w2_lo[:, rows, :].unsqueeze(1), w2_sb[:, bass.ds(e, 1), rows, :],
                                  w2_hi[:, rows, :].bitcast(F32).unsqueeze(1), ALU.subtract).then_inc(w2_lo_ready, 1)

            def rest_x(t, par):
                vec.wait_ge(x_hi_ready, t + 1)
                vec.tensor_tensor(xt_lo[:, par, :, :], xt_bank[par][:, :].rearrange("p (b n) -> p b n", b=DB),
                                  xt_hi[:, par, :, :].bitcast(F32), ALU.subtract).then_inc(x_lo_ready, 1)

            def split_hidden(t, b):
                hi = h_hi[:, 2 * b:2 * b + 2, :]
                full = h_full[:, b % 2, :].rearrange("p (i n) -> p i n", i=2)
                vec.wait_ge(h_full_ready, 8 * t + 2 * b + 2)
                if not isinstance(t, int) or t > 0:
                    vec.wait_ge(h_used, 4 * t + b - 3)
                vec.tensor_copy(hi, full).then_inc(h_hi_ready, 1)
                vec.wait_ge(h_hi_ready, 4 * t + b + 1)
                vec.tensor_tensor(h_lo[:, 2 * b:2 * b + 2, :], full, hi.bitcast(F32), ALU.subtract)\
                    .then_inc(h_lo_ready, 1)

            def select_bias(t):
                if not isinstance(t, int) or t > 0:
                    vec.wait_ge(h_used, 4 * t)
                vec.tensor_scalar(b2_select[:, :], ones[0:B2K, :], b2_choice[:, bass.ds(t, 1)], None, ALU.mult)\
                    .then_inc(b2_selected, 1)

            def step(t, par):
                static = isinstance(t, int)
                if not static or 0 <= t < PAIR_TILES:
                    select_bias(t)
                    e = expert_of(t)
                    rest_w2(t, 0, e)
                    rest_w2(t, 1, e)
                hidden = not static or 0 <= t + 1 < PAIR_TILES
                ahead = not static or t + 2 < PAIR_TILES
                split_w1 = ahead and not (static and t == -2)
                x_first = static and t == -1
                e_ahead = expert_of(t + 2) if split_w1 else None
                if x_first:
                    rest_x(t + 2, par)
                if split_w1:
                    rest_w1(t + 2, 0, e_ahead)
                if hidden:
                    split_hidden(t + 1, 0)
                if split_w1:
                    rest_w1(t + 2, 1, e_ahead)
                if ahead and not x_first:
                    rest_x(t + 2, par)
                if hidden:
                    split_hidden(t + 1, 1)
                    split_hidden(t + 1, 2)
                    split_hidden(t + 1, 3)

            for t in range(-2, 2):
                step(t, t % 2)
            with vec.Fori(1, PAIR_TILES // 2 - 1) as k:
                for par in range(2):
                    step(2 * k + par, par)
            for t in range(2 * (PAIR_TILES // 2 - 1), PAIR_TILES):
                step(t, t % 2)

        @block.tensor
        def _(pe):
            def turn_rows(stage, src, unit):
                g, b = unit // DB, unit % DB
                if b == 0:
                    pe.wait_ge(xn_even, stage * T // 2 + 2 * g + 2)
                    pe.wait_ge(xn_odd, stage * T // 2 + 2 * g + 2)
                if unit >= 4:
                    pe.wait_ge(xt_odd if b else xt_even, stage * QUADS + unit // 2 - 1)
                for j in range(JQ):
                    mm = pe.transpose(turn_bank[unit % 4][:, j * P:(j + 1) * P],
                                      src[:, JQ * g + j, b * P:(b + 1) * P], ident[:, :])
                mm.then_inc(xt_turned, 1)

            def keep_busy(n):
                for _ in range(n):
                    pe.matmul(turn_bank[0][:, 0:P], ident[:, :], ones[:, :], start=True, stop=True)

            pe.wait_ge(consts, CONSTS)
            keep_busy(WARM_START)
            for unit in range(DB * QUADS):
                turn_rows(0, xn, unit)
            pe.wait_ge(c_ready, DB)
            for c in range(QUADS):
                pe.wait_ge(xt_even, c + 1)
                pe.wait_ge(xt_odd, c + 1)
                if c >= 2:
                    pe.wait_ge(s2_ready, c - 1)
                for b in range(DB):
                    mm = pe.matmul(wide_bank[c % 2][:, :], c2_wide[:, b, :], xn_t[:, b, c * BANK:(c + 1) * BANK],
                                   start=(b == 0), stop=(b == DB - 1))
                mm.then_inc(s2_psum, 1)

            def value(t):
                if 2 <= t < 4:
                    pe.wait_ge(s2_ready, t + 1)
                if t >= 4:
                    pe.wait_ge(v_ready, t - 3)
                for b in range(DB):
                    pe.matmul(value_bank[t % 4][:, 0:D + 1], xn_t[:, b, t * P:(t + 1) * P], fc_ext[:, b, :],
                              start=(b == 0), stop=False)
                pe.matmul(value_bank[t % 4][:, 0:D], ones_r[:, :], fcb_parts[:, :], start=False, stop=True)\
                    .then_inc(v_psum, 1)

            def turn(t, par, q):
                if q % 2 == 0:
                    pe.wait_ge(probs_ready, 2 * t + q // 2 + 1)
                if not isinstance(t, int) or t > 0:
                    pe.wait_ge(pt_lo_ready, 4 * t + q - 3)
                for j in range(JQ):
                    c = (JQ * q + j) * P
                    mm = pe.transpose(turn_bank[q][:, j * P:(j + 1) * P], probs[:, par, c:c + P], ident[:, :])
                mm.then_inc(turned, 1)

            def attend(t, par, q):
                if q == 0 and (not isinstance(t, int) or t > 1):
                    pe.wait_ge(x1_ready, t - 1)
                pe.wait_ge(pt_lo_ready, 4 * t + q + 1)
                for j in range(JQ):
                    block_j = JQ * q + j
                    cols = slice(j * P, (j + 1) * P)
                    passes = ((pt_hi, v_hi), (pt_hi, v_lo), (pt_lo, v_hi))
                    for n, (left, right) in enumerate(passes):
                        mm = pe.matmul(attn_bank[par][:, 0:D], left[:, q, cols], right[:, block_j, :],
                                       start=(block_j == 0 and n == 0), stop=(block_j == T - 1 and n == 2))
                if q == QUADS - 1:
                    mm.then_inc(attn_psum, 1)

            def attention(t, par):
                for q in range(QUADS):
                    attend(t, par, q)
                    if not isinstance(t, int) or t + 1 < T:
                        turn(t + 1, 1 - par, q)

            pe.wait_ge(one_rows, 1)
            pe.wait_ge(bias_ready, 1)
            for t in range(T - 4):
                value(t)
            for q in range(QUADS):
                turn(0, 0, q)
            for t in range(T - 4, T):
                value(t)
            pe.wait_ge(v_ready, T)
            for t in range(0, 2):
                attention(t, t % 2)
            with pe.Fori(1, T // 2 - 2) as k:
                for par in range(2):
                    attention(2 * k + par, par)
            for t in range(T - 4, T):
                attention(t, t % 2)

            def gate(g):
                pe.wait_ge(xt_even, QUADS + g + 1)
                pe.wait_ge(xt_odd, QUADS + g + 1)
                if g >= 2:
                    pe.wait_ge(gate_ready, g - 1)
                for b in range(DB):
                    mm = pe.matmul(wide_bank[g % 2][0:E, :], gate_ws[:, b, :], xn2_t[:, b, g * BANK:(g + 1) * BANK],
                                   start=(b == 0), stop=(b == DB - 1))
                mm.then_inc(gate_psum, 1)

            pe.wait_ge(late_in, 16 * LATE)
            for g in range(QUADS):
                for b in range(DB):
                    turn_rows(1, xn2, DB * g + b)
                if g > 0:
                    gate(g - 1)
            gate(QUADS - 1)
            pe.wait_ge(x1_ready, T - 1)
            for t in range(T):
                if t % JQ == 0:
                    pe.wait_ge(gate_ready, t // JQ + 1)
                mm = pe.transpose(attn_bank[0][:, t * E:(t + 1) * E], logits_t[:, t * P:(t + 1) * P],
                                  ident[0:E, 0:E])
            mm.then_inc(logits_psum, 1)
            pe.transpose(wide_bank[1][:, 0:E * FB], b1_raw[:, :], ident[0:E * FB, 0:E * FB]).then_inc(b1_turned, 1)
            keep_busy(WARM_CHOICE)
            pe.wait_ge(chosen_ready, 1)
            hot = chosen[:, :, :].rearrange("p t e -> p (t e)")
            pe.matmul(wide_bank[0][:, 0:P], hot, ones[:, :], start=True, stop=True).then_inc(totals_psum, 1)
            pe.matmul(attn_bank[1][:, 0:TE], below[:, :], hot, start=True, stop=False)
            pe.wait_ge(totals_ready, 1)
            pe.matmul(attn_bank[1][:, 0:TE], totals[:, :], earlier[:, :, :].rearrange("p t e -> p (t e)"),
                      start=False, stop=True)
            pe.matmul(attn_bank[1][:, TE:TE + E], totals[:, :], same_expert[:, :], start=True, stop=True)\
                .then_inc(position_psum, 1)
            keep_busy(WARM_RANK)
            for i in range(TOPK * T):
                if i % (TOPK * T // HOTS) == 0:
                    g = i // (TOPK * T // HOTS)
                    pe.wait_ge(rows_hot, g + 1)
                    pe.wait_ge(vals_ready, 2 * g + 2)
                mm = pe.matmul(attn_bank[0][0:2 * SLOTS, 0:P], slot_vals[:, i, :, :].rearrange("p v s -> p (v s)"),
                               in_row[:, i, :], start=(i == 0), stop=(i == TOPK * T - 1))
            mm.then_inc(slots_psum, 1)
            pe.wait_ge(slots_ready, 1)
            pe.transpose(attn_bank[1][:, 0:2 * SLOTS], slots_t[:, :], ident[0:2 * SLOTS, 0:2 * SLOTS])\
                .then_inc(slots_turned, 1)
            keep_busy(WARM_GATHER)

            def turn_x(t, par, half):
                pe.wait_ge(rows_in[par], 32 * half + 32)
                if not isinstance(t, int) or t > 1:
                    pe.wait_ge(x_lo_ready, t - 1)
                for b in range(DB):
                    for h in range(2):
                        mm = pe.transpose(xt_bank[par][:, b * TILE + h * P:b * TILE + (h + 1) * P],
                                          x_rows[:, par, h, b * P:(b + 1) * P], ident[:, :])
                mm.then_inc(xt_psum, 1)

            def first_layer(t, par):
                pe.wait_ge(x_lo_ready, t + 1)
                for b in range(HBANKS):
                    if b % 2 == 0:
                        pe.wait_ge(w1_lo_ready, 2 * t + b // 2 + 1)
                    if not isinstance(t, int) or t > 0:
                        pe.wait_ge(h_full_ready, 8 * t + 2 * b - 6)
                    for i in range(2):
                        cols = slice((2 * b + i) * P, (2 * b + i + 1) * P)
                        passes = [(left, right, d) for d in range(DB)
                                  for left, right in ((w1_hi, xt_hi), (w1_hi, xt_lo), (w1_lo, xt_hi))]
                        for n, (left, right, d) in enumerate(passes):
                            mm = pe.matmul(h_bank[b][:, i * TILE:(i + 1) * TILE], left[:, d, cols],
                                           right[:, par, d, :], start=(n == 0), stop=(n == len(passes) - 1))
                    mm.then_inc(h_psum, 1)

            def second_layer(t):
                if not isinstance(t, int) or t > 0:
                    pe.wait_ge(y_ready, 2 * t)
                pe.wait_ge(b2_selected, t + 1)
                for h in range(2):
                    pe.matmul(y_bank[h][:, 0:D], b2_select[:, :], b2_parts[:, :], start=True, stop=False)
                for b in range(HBANKS):
                    pe.wait_ge(h_lo_ready, 4 * t + b + 1)
                    if b % 2 == 0:
                        pe.wait_ge(w2_lo_ready, 2 * t + b // 2 + 1)
                    for fb in (2 * b, 2 * b + 1):
                        for h in range(2):
                            rows = slice(h * P, (h + 1) * P)
                            for left, right in ((h_hi, w2_hi), (h_hi, w2_lo), (h_lo, w2_hi)):
                                mm = pe.matmul(y_bank[h][:, 0:D], left[:, fb, rows], right[:, fb, :], start=False,
                                               stop=(fb == FB - 1 and left is h_lo))
                    mm.then_inc(h_used, 1)

            def step(t, par, half):
                static = isinstance(t, int)
                if not static or t + 2 < PAIR_TILES:
                    turn_x(t + 2, par, half + 1)
                if not static or 0 <= t + 1 < PAIR_TILES:
                    first_layer(t + 1, 1 - par)
                if not static or t >= 0:
                    second_layer(t)

            pe.wait_ge(b2_lo, 1)
            pe.wait_ge(b1_ready, 1)
            for t in range(-2, 2):
                step(t, t % 2, t // 2)
            with pe.Fori(1, PAIR_TILES // 2 - 1) as k:
                for par in range(2):
                    step(2 * k + par, par, k)
            for t in range(2 * (PAIR_TILES // 2 - 1), PAIR_TILES):
                step(t, t % 2, t // 2)


_INS = ["x", "adj", "L0_gnn_W", "L0_gnn_a_w", "L0_gnn_a_b", "L0_gnn_fc_w", "L0_gnn_fc_b", "L0_ffn_Wg",
        "L0_ffn_bg", "L0_ffn_W1", "L0_ffn_b1", "L0_ffn_W2", "L0_ffn_b2"]


def kernel(**inputs):
    import numpy as np
    import concourse.bacc as bacc
    from concourse.bass_utils import run_bass_kernel_spmd

    nc = bacc.Bacc("TRN2", target_bir_lowering=False, num_devices=1)
    arrays, args = {}, []
    for name in _INS:
        a = np.ascontiguousarray(inputs[name]).reshape(np.shape(inputs[name]) or (1,))
        arrays[name] = a
        args.append(nc.dram_tensor(name, a.shape, mybir.dt.from_np(a.dtype), kind="ExternalInput").ap())
    shape = arrays["x"].shape
    args.append(nc.dram_tensor("out", shape, F32, kind="ExternalOutput").ap())
    graph_attention_experts(nc, *args)
    return run_bass_kernel_spmd(nc, [arrays], core_ids=[0]).results[0]["out"]
```

```python
from contextlib import ExitStack

import concourse.bass as bass
from concourse import mybir

F32 = mybir.dt.float32
F32R = mybir.dt.float32r
I32 = mybir.dt.int32
ALU = mybir.AluOpType
ACT = mybir.ActivationFunctionType
AXIS = mybir.AxisListType.X

P = 128
SLOPE = 0.2
MASKED = -9000000000000000.0
LN_EPS = 1e-05
GATE_EPS = 0.01
BANK = 512


def graph_attention_experts(nc, x, adj, gnn_w, a_w, a_b, fc_w, fc_b, gate_w, gate_b, w1, b1, w2, b2, out):
    N, D = x.shape
    E, _, FF = w1.shape
    T = N // P
    DB = D // P
    FB = FF // P
    QUADS = N // BANK
    JQ = BANK // P
    TOPK = 2
    PAIRS = TOPK * N
    TILE = 2 * P
    SLOTS = (PAIRS - E) // P + E
    HALF = E - 1
    FULL = (SLOTS - HALF) // 2
    TILES = FULL + HALF
    TE = T * E
    NO_TOKEN = 2.0 * N
    HBANKS = FB // 2
    B2K = 32 + E
    FCK = 33
    EARLY_ROWS, LATE_ROWS = slice(0, T - 2), slice(T - 2, T)
    HOTS = 4
    WARM_START, WARM_CHOICE, WARM_RANK, WARM_GATHER = 38, 26, 22, 24
    CONSTS = 10
    assert D == 256 and N == 2048 and FB == 8 and TE == P and SLOTS == 2 * FULL + HALF

    ctx = ExitStack()
    with ctx:
        def sb(name, shape, dt=F32):
            return ctx.enter_context(nc.sbuf_tensor(name, shape, dt))

        def sem(name):
            return ctx.enter_context(nc.semaphore(name))

        ident = sb("ident", [P, P])
        ones = sb("ones", [P, P])
        below = sb("below", [P, P])
        same_expert = sb("same_expert", [P, E])
        earlier = sb("earlier", [P, T, E])
        column = sb("column", [P, P])
        minus_one = sb("minus_one", [P, 1])
        table_scratch = sb("table_scratch", [P, 1])
        token = sb("token", [P, T])
        id_less = sb("id_less", [P, E])
        block_limits = sb("block_limits", [P, T])
        cum_blocks = sb("cum_blocks", [P, E + 1])
        cum_pairs = sb("cum_pairs", [P, E + 1])
        stats = sb("stats", [P, T, 6])
        moments = sb("moments", [P, T, 2])
        spread = sb("spread", [P, T])
        rstd = sb("rstd", [P, T])
        newton = sb("newton", [P, T])
        centre = sb("centre", [P, T])
        s1_pos = sb("s1_pos", [P, T])
        z_max = sb("z_max", [P, 2])
        relu_max = sb("relu_max", [P, 2])
        e_max = sb("e_max", [P, 2])
        neg_max = sb("neg_max", [P, 2])
        half_sums = sb("half_sums", [P, T, 2])
        row_sum = sb("row_sum", [P, T])
        row_rcp = sb("row_rcp", [P, T])
        ab_col = sb("ab_col", [P, 1])
        gate_ws = sb("gate_ws", [P, DB, E])
        gate_bs = sb("gate_bs", [P, E])
        b1_cols = sb("b1_cols", [P, E * FB])
        b2_parts = sb("b2_parts", [B2K, D], F32R)
        row_expert = sb("row_expert", [P, 1])
        b2_choice = sb("b2_choice", [B2K, TILES])
        b2_select = sb("b2_select", [B2K, P], F32R)
        tile_expert = sb("tile_expert", [1, TILES], I32)
        gather_idx = sb("gather_idx", [P, SLOTS], I32)
        add_idx = sb("add_idx", [P, SLOTS], I32)
        slot_weight = sb("slot_weight", [P, SLOTS])
        gather_now = sb("gather_now", [P, 2, 2], I32)
        add_now = sb("add_now", [P, 2, 2], I32)

        base = (nc.sbuf_base + 31) // 32 * 32

        def at(name, offset, shape, dt=F32):
            return nc.alloc_sbuf_tensor_at(name, shape, dt, offset=base + offset)

        K = 1024
        w1_sb = at("w1_sb", 0, [P, E, DB, FF])
        LOW = E * DB * FF * 4
        w2_sb = at("w2_sb", LOW, [P, E, FB, D])
        A = LOW + E * FB * D * 4
        B, C, X, Z = A + 16 * K, A + 32 * K, A + 48 * K, A + 64 * K
        v_hi = at("v_hi", LOW, [P, T, D], F32R)
        v_lo = at("v_lo", LOW + 16 * K, [P, T, D], F32R)
        s2_rows = at("s2_rows", LOW + 32 * K, [P, N])
        adj_sb = at("adj_sb", LOW + 40 * K, [P, 2, N])
        relu_part = at("relu_part", LOW + 56 * K, [P, N])
        z = at("z", A, [P, 2, N])
        probs = at("probs", B, [P, 2, N])
        pt_hi = at("pt_hi", C, [P, QUADS, BANK], F32R)
        pt_lo = at("pt_lo", C + 8 * K, [P, QUADS, BANK], F32R)
        x_sb = at("x_sb", X, [P, T, D])
        xn_t = at("xn_t", 32 * K, [P, DB, N])
        early = [48 * K]

        def spare(name, shape, dt=F32):
            size = 4
            for n in shape[1:]:
                size *= n
            offset = early[0]
            early[0] = offset + (size + 31) // 32 * 32
            assert early[0] <= LOW
            return at(name, offset, shape, dt)

        fc_ext = spare("fc_ext", [P, DB, D + 1])
        gnn_ws = spare("gnn_ws", [P, 2 * DB, D])
        aw_rows = spare("aw_rows", [P, D])
        products = spare("products", [P, 2 * DB, D])
        c2_cols = spare("c2_cols", [P, DB])
        c2_wide = spare("c2_wide", [P, DB, P])
        fcb_raw = spare("fcb_raw", [FCK, D])
        fcb_parts = spare("fcb_parts", [FCK, D], F32R)
        ones_r = spare("ones_r", [FCK, P], F32R)
        b2_rows = at("b2_rows", Z + 3 * K, [B2K, D])
        b1_raw = at("b1_raw", Z + 2 * K, [E * FB, P])
        xn = at("xn", B, [P, T, D])
        xn2 = at("xn2", A, [P, T, D])
        xn2_t = at("xn2_t", B, [P, DB, N])
        logits_t = at("logits_t", C, [E, N])
        rt = [X]

        def routing(name, shape, dt=F32):
            size = 4
            for n in shape[1:]:
                size *= n
            offset = rt[0]
            rt[0] = offset + (size + 31) // 32 * 32
            assert rt[0] <= Z
            return at(name, offset, shape, dt)

        logits = routing("logits", [P, T, E])
        gates = routing("gates", [P, T, E])
        gates2 = routing("gates2", [P, T, E])
        hots = routing("hots", [P, TOPK, T, E])
        cand = routing("cand", [P, T, E])
        chosen = routing("chosen", [P, T, E])
        picked = routing("picked", [P, TOPK, T, E])
        position = routing("position", [P, T, E])
        totals = routing("totals", [P, P])
        cmp = routing("cmp", [P, E, T])
        late = routing("late", [P, T, E])
        top = routing("top", [P, TOPK, T])
        top_id = routing("top_id", [P, TOPK, T])
        top_w = routing("top_w", [P, TOPK, T])
        norm = routing("norm", [P, T])
        blocks_of = routing("blocks_of", [P, E])
        pairs_of = routing("pairs_of", [P, E])
        kept = routing("kept", [P, E])
        left_before = routing("left_before", [P, E])
        left_end = routing("left_end", [P, E])
        shift = routing("shift", [P, E])
        over = routing("over", [P, TOPK, T])
        pos = routing("pos", [P, TOPK, T])
        pos_int = routing("pos_int", [P, TOPK, T], I32)
        part_int = routing("part_int", [P, 2, TOPK, T], I32)
        part = routing("part", [P, 2, TOPK, T])
        ended = routing("ended", [P, TILES, E - 1])
        ended_sum = routing("ended_sum", [P, TILES])
        slots_t = routing("slots_t", [2 * SLOTS, P])
        slot_empty = routing("slot_empty", [P, SLOTS])
        in_row = at("in_row", B, [P, TOPK * T, P])
        in_slot = at("in_slot", Z, [P, TOPK * T, SLOTS])
        slot_vals = at("slot_vals", A, [P, TOPK * T, 2, SLOTS])
        w2_hi = at("w2_hi", A, [P, FB, D], F32R)
        w2_lo = at("w2_lo", A + 8 * K, [P, FB, D], F32R)
        h_hi = at("h_hi", B, [P, FB, TILE], F32R)
        h_lo = at("h_lo", B + 8 * K, [P, FB, TILE], F32R)
        w1_hi = at("w1_hi", C, [P, DB, FF], F32R)
        w1_lo = at("w1_lo", C + 8 * K, [P, DB, FF], F32R)
        w1_full = at("w1_full", C, [P, DB, FF])
        xt_hi = at("xt_hi", X, [P, 2, DB, TILE], F32R)
        xt_lo = at("xt_lo", X + 4 * K, [P, 2, DB, TILE], F32R)
        xt_full = at("xt_full", X, [P, 2, DB, TILE])
        h_full = at("h_full", X + 8 * K, [P, 2, BANK])
        y_sb = at("y_sb", X + 12 * K, [P, 2, 2, D])
        x_rows = at("x_rows", Z, [P, 2, 2, D])

        bank = [ctx.enter_context(nc.psum_tensor(f"bank{i}", [P, BANK], F32)) for i in range(8)]
        turn_bank, attn_bank, wide_bank, value_bank = bank[0:4], bank[4:6], bank[6:8], bank[4:8]
        h_bank, y_bank, xt_bank = bank[0:4], bank[4:6], bank[6:8]

        xn2_dram = nc.dram_tensor("xn2_dram", [N, D], F32).ap()

        x_in = [sem(f"x_in{g}") for g in range(4)]; small_in = sem("small_in"); late_in = sem("late_in")
        adj_in = [sem("adj_in0"), sem("adj_in1")]
        w1_in = sem("w1_in"); w2_in = sem("w2_in"); xn2_out = sem("xn2_out"); out_init = sem("out_init")
        rows_in = [sem("rows_in0"), sem("rows_in1")]; added = sem("added")
        consts = sem("consts"); pool_step = sem("pool_step")
        proj_step = sem("proj_step"); c_ready = sem("c_ready")
        ln_var = sem("ln_var"); ln_std = sem("ln_std"); ln_step = sem("ln_step"); ln_done = sem("ln_done"); xn_odd = sem("xn_odd"); xn_even = sem("xn_even"); centre_ready = sem("centre_ready")
        xt_turned = sem("xt_turned"); xt_even = sem("xt_even"); xt_odd = sem("xt_odd")
        s2_psum = sem("s2_psum"); s2_ready = sem("s2_ready")
        bias_zero = sem("bias_zero"); bias_hi = sem("bias_hi"); bias_ready = sem("bias_ready")
        v_psum = sem("v_psum"); v_hi_ready = sem("v_hi_ready"); v_ready = sem("v_ready")
        b1_turned = sem("b1_turned"); b1_ready = sem("b1_ready")
        s1_ready = sem("s1_ready"); preloaded = sem("preloaded")
        mask_ready = sem("mask_ready"); z_ready = sem("z_ready"); relu_ready = sem("relu_ready")
        e_max_ready = sem("e_max_ready"); e_ready = sem("e_ready"); probs_ready = sem("probs_ready"); sum_ready = sem("sum_ready")
        turned = sem("turned"); pt_hi_ready = sem("pt_hi_ready"); pt_lo_ready = sem("pt_lo_ready")
        attn_psum = sem("attn_psum"); rcp_ready = sem("rcp_ready"); x1_ready = sem("x1_ready")
        logits_psum = sem("logits_psum"); gate_psum = sem("gate_psum"); gate_ready = sem("gate_ready"); route = sem("route"); exp_ready = sem("exp_ready")
        logits_shifted = sem("logits_shifted"); weights_ready = sem("weights_ready")
        chosen_ready = sem("chosen_ready"); totals_psum = sem("totals_psum"); totals_ready = sem("totals_ready")
        position_psum = sem("position_psum"); slots_hot = sem("slots_hot"); rows_hot = sem("rows_hot"); pos_ready = sem("pos_ready"); vals_ready = sem("vals_ready"); slots_psum = sem("slots_psum"); slots_ready = sem("slots_ready"); slots_turned = sem("slots_turned")
        neg_max_ready = sem("neg_max_ready"); b2_zero = sem("b2_zero"); b2_hi = sem("b2_hi"); b2_lo = sem("b2_lo")
        b2_selected = sem("b2_selected"); routed_b1 = sem("routed_b1")
        tables = sem("tables"); experts_known = sem("experts_known"); one_rows = sem("one_rows")
        pool_passed = sem("pool_passed")
        gather_cols = sem("gather_cols"); add_cols = sem("add_cols")
        xt_psum = sem("xt_psum"); x_hi_ready = sem("x_hi_ready"); x_lo_ready = sem("x_lo_ready")
        w1_hi_ready = sem("w1_hi_ready"); w1_lo_ready = sem("w1_lo_ready")
        w2_hi_ready = sem("w2_hi_ready"); w2_lo_ready = sem("w2_lo_ready")
        h_psum = sem("h_psum"); h_full_ready = sem("h_full_ready")
        h_hi_ready = sem("h_hi_ready"); h_lo_ready = sem("h_lo_ready"); h_used = sem("h_used")
        y_ready = sem("y_ready")

        adj_tiles = adj.rearrange("(t p) j -> p t j", p=P)
        x_tiles = x.rearrange("(t p) d -> p t d", p=P)
        out_tiles = out.rearrange("(t p) d -> p t d", p=P)
        xn2_tiles = xn2_dram.rearrange("(t p) d -> p t d", p=P)
        w1_view = w1.rearrange("e (b p) f -> p e b f", p=P)
        w2_view = w2.rearrange("e (b p) d -> p e b d", p=P)

        XG = 4
        SMALL = 6
        LATE = 5

        def half_tile(t):
            return isinstance(t, int) and t >= FULL

        def done(t, full, half):
            return full * t if not isinstance(t, int) or t <= FULL else full * FULL + half * (t - FULL)

        def per_expert(ap, n=T):
            return ap.unsqueeze(2).to_broadcast([P, n, E])

        block = ctx.enter_context(nc.Block())

        @block.sync
        def _(sp):
            for g in range(XG):
                ts = slice(g * T // XG, (g + 1) * T // XG)
                sp.dma_start(x_sb[:, ts, :], x_tiles[:, ts, :]).then_inc(x_in[g], 16)
            sp.dma_start(gnn_ws[:, :, :], gnn_w.rearrange("(b p) f -> p b f", p=P)).then_inc(small_in, 16)
            sp.dma_start(aw_rows[:, :], a_w.unsqueeze(0).to_broadcast([P, D])).then_inc(small_in, 16)
            sp.dma_start(fc_ext[:, :, 0:D], fc_w.rearrange("(b p) f -> p b f", p=P)).then_inc(small_in, 16)
            sp.dma_start(ab_col[:, :], a_b.unsqueeze(0).to_broadcast([P, 1])).then_inc(small_in, 16)
            sp.wait_ge(bias_zero, 1)
            sp.dma_start(fcb_raw[0:1, :], fc_b.unsqueeze(0)).then_inc(small_in, 16)
            sp.dma_start(fcb_raw[32:33, :], fc_b.unsqueeze(0)).then_inc(small_in, 16)
            for t in range(2):
                sp.dma_start(adj_sb[:, t, :], adj_tiles[:, t, :]).then_inc(adj_in[t], 16)
            sp.dma_start(b1_raw[:, :], b1.rearrange("e (b p) -> (e b) p", p=P)).then_inc(late_in, 16)
            sp.wait_ge(b2_zero, 1)
            sp.dma_start(b2_rows[0:E, :], b2).then_inc(late_in, 16)
            sp.dma_start(b2_rows[32:B2K, :], b2).then_inc(late_in, 16)
            sp.dma_start(gate_ws[:, :, :], gate_w.rearrange("(b p) e -> p b e", p=P)).then_inc(late_in, 16)
            sp.dma_start(gate_bs[:, :], gate_b.unsqueeze(0).to_broadcast([P, E])).then_inc(late_in, 16)

            def load_w1(t, e, half):
                sp.dma_start(w1_sb[:, e, half, :], w1_view[:, e, half, :]).then_inc(w1_in, 16)

            with sp.Fori(0, T // 2 - 1) as k:
                for par in range(2):
                    sp.wait_ge(z_ready, 2 * k + par + 1)
                    sp.dma_start(adj_sb[:, par, :], adj_tiles[:, bass.ds(2 * k + par + 2, 1), :])\
                        .then_inc(adj_in[par], 16)
                    sp.dma_start(w1_sb[:, bass.ds(k, 1), par, :], w1_view[:, bass.ds(k, 1), par, :])\
                        .then_inc(w1_in, 16)
            for half in range(DB):
                sp.dma_start(w1_sb[:, E - 1, half, :], w1_view[:, E - 1, half, :]).then_inc(w1_in, 16)
            for g in range(XG):
                ts = slice(g * T // XG, (g + 1) * T // XG)
                sp.wait_ge(x1_ready, (g + 1) * T // XG)
                sp.dma_start(out_tiles[:, ts, :], x_sb[:, ts, :]).then_inc(out_init, 16)
            sp.wait_ge(attn_psum, T)
            sp.wait_ge(e_ready, 2 * T)
            sp.wait_ge(z_ready, T)
            for g in range(XG):
                ts = slice(g * T // XG, (g + 1) * T // XG)
                sp.wait_ge(xn_even, T // 2 + 2 * g + 2)
                sp.wait_ge(xn_odd, T // 2 + 2 * g + 2)
                sp.dma_start(xn2_tiles[:, ts, :], xn2[:, ts, :]).then_inc(xn2_out, 16)
            for e in range(E):
                sp.dma_start(w2_sb[:, e, :, :], w2_view[:, e, :, :]).then_inc(w2_in, 16)
            sp.wait_ge(out_init, 16 * XG)
            sp.wait_ge(added, done(TILES, 32, 16))

        @block.gpsimd
        def _(pool):
            steps = [0]

            def after(instruction):
                instruction.then_inc(pool_step, 1)
                steps[0] += 1
                pool.wait_ge(pool_step, steps[0])

            pool.memset(ident[:, :], 0.0).then_inc(pool_step, 1)
            pool.memset(ones[:, :], 1.0).then_inc(pool_step, 1)
            pool.memset(fcb_raw[:, :], 0.0).then_inc(bias_zero, 1)
            pool.wait_ge(pool_step, 2)
            steps[0] = 2
            pool.affine_select(out=ident[:, :], in_=ident[:, :], compare_op=ALU.not_equal, fill=1.0, base=0,
                               pattern=[[-1, P]], channel_multiplier=1).then_inc(consts, 1)
            pool.affine_select(out=below[:, :], in_=ones[:, :], compare_op=ALU.is_gt, fill=0.0, base=0,
                               pattern=[[1, P]], channel_multiplier=-1).then_inc(consts, 1)
            pool.iota(column[:, :], [[1, P]], base=0, channel_multiplier=0,
                      allow_small_or_imprecise_dtypes=True).then_inc(consts, 1)
            pool.iota(token[:, :], [[P, T]], base=1, channel_multiplier=1,
                      allow_small_or_imprecise_dtypes=True).then_inc(consts, 1)
            pool.iota(id_less[:, :], [[1, E]], base=-E, channel_multiplier=0,
                      allow_small_or_imprecise_dtypes=True).then_inc(consts, 1)
            pool.iota(block_limits[:, :], [[P, T]], base=0, channel_multiplier=0,
                      allow_small_or_imprecise_dtypes=True).then_inc(consts, 1)

            pool.iota(row_expert[:, :], [[0, 1]], base=0, channel_multiplier=1,
                      allow_small_or_imprecise_dtypes=True).then_inc(consts, 1)
            pool.memset(minus_one[:, :], -1.0).then_inc(consts, 1)
            pool.memset(cum_blocks[:, 0:1], 0.0).then_inc(consts, 1)
            pool.memset(cum_pairs[:, 0:1], 0.0).then_inc(consts, 1)
            pool.memset(b2_rows[:, :], 0.0).then_inc(b2_zero, 1)

            pool.wait_ge(consts, CONSTS)

            def total(t):
                pool.wait_ge(probs_ready, 2 * t + 2)
                pool.tensor_tensor(row_sum[:, bass.ds(t, 1)], half_sums[:, bass.ds(t, 1), 0],
                                   half_sums[:, bass.ds(t, 1), 1], ALU.add).then_inc(sum_ready, 1)

            def leaky(t, par):
                pool.wait_ge(relu_ready, 3 * t + 1)
                pool.tensor_tensor(e_max[:, par:par + 1], z_max[:, par:par + 1],
                                   relu_max[:, par:par + 1], ALU.add).then_inc(e_max_ready, 1)
                pool.wait_ge(e_max_ready, t + 1)
                pool.tensor_tensor(neg_max[:, par:par + 1], e_max[:, par:par + 1], minus_one[:, :], ALU.mult)\
                    .then_inc(neg_max_ready, 1)
                for half in range(2):
                    cols = slice(half * N // 2, (half + 1) * N // 2)
                    pool.wait_ge(relu_ready, 3 * t + 2 + half)
                    pool.tensor_tensor(z[:, par, cols], z[:, par, cols], relu_part[:, cols], ALU.add)\
                        .then_inc(e_ready, 1)

            leaky(0, 0)
            leaky(1, 1)
            with pool.Fori(1, T // 2) as k:
                for par in range(2):
                    total(2 * k + par - 2)
                    leaky(2 * k + par, par)
            total(T - 2)
            total(T - 1)

            kt = TOPK * T
            top_w_pairs = top_w[:, :, :].rearrange("p k t -> p (k t)").unsqueeze(2).to_broadcast([P, kt, SLOTS])
            pool.wait_ge(xn2_out, 16 * XG)
            for g in range(HOTS):
                ks = slice(g * kt // HOTS, (g + 1) * kt // HOTS)
                ts = slice(g * kt // HOTS % T, g * kt // HOTS % T + kt // HOTS)
                pool.wait_ge(slots_hot, g + 1)
                pool.tensor_tensor(slot_vals[:, ks, 0, :], in_slot[:, ks, :],
                                   token[:, ts].unsqueeze(2).to_broadcast([P, kt // HOTS, SLOTS]), ALU.mult)\
                    .then_inc(vals_ready, 1)
                pool.tensor_tensor(slot_vals[:, ks, 1, :], in_slot[:, ks, :], top_w_pairs[:, ks, :], ALU.mult)\
                    .then_inc(vals_ready, 1)

            pool.wait_ge(tables, 1)
            pool.wait_ge(slots_psum, 1)

            def gather(t, par):
                n, col = (1, done(t, 2, 1)) if half_tile(t) else (2, 2 * t)
                pool.tensor_copy(gather_now[:, par, 0:n], gather_idx[:, bass.ds(col, n)]).then_inc(gather_cols, 1)
                pool.wait_ge(xn2_out, 16 * XG)
                pool.wait_ge(gather_cols, t + 1)
                pool.sem_inc(pool_passed, 1)
                for h in range(n):
                    pool.indirect_dma_start(
                        out=x_rows[:, par, h, :], out_offset=None, in_=xn2_dram,
                        in_offset=bass.IndirectOffsetOnAxis(ap=gather_now[:, par, h:h + 1], axis=0))\
                        .then_inc(rows_in[par], 16)

            def add(t, par):
                n, col = (1, done(t, 2, 1)) if half_tile(t) else (2, 2 * t)
                pool.tensor_copy(add_now[:, par, 0:n], add_idx[:, bass.ds(col, n)]).then_inc(add_cols, 1)
                pool.wait_ge(add_cols, t + 1)
                pool.wait_ge(y_ready, done(t, 2, 1) + n)
                pool.wait_ge(out_init, 16 * XG)
                if not isinstance(t, int) or t > 0:
                    pool.wait_ge(added, done(t, 32, 16))
                    pool.sem_inc(pool_passed, 1)
                for h in range(n):
                    pool.indirect_dma_start(
                        out=out, out_offset=bass.IndirectOffsetOnAxis(ap=add_now[:, par, h:h + 1], axis=0),
                        in_=y_sb[:, par, h, :], in_offset=None, bounds_check=N - 1, oob_is_err=False,
                        compute_op=ALU.add).then_inc(added, 16)

            def step(t, par):
                if not isinstance(t, int) or t + 3 < TILES:
                    if not isinstance(t, int) or t + 3 >= 2:
                        pool.wait_ge(xt_psum, t + 2)
                    gather(t + 3, 1 - par)
                if not isinstance(t, int) or t >= 1:
                    add(t - 1, 1 - par)

            gather(0, 0)
            gather(1, 1)
            pool.wait_ge(tables, 3)
            step(-1, 1)
            for t in range(0, 2):
                step(t, t % 2)
            with pool.Fori(1, FULL // 2 - 2) as k:
                for par in range(2):
                    step(2 * k + par, par)
            for t in range(2 * (FULL // 2 - 2), TILES + 1):
                step(t, t % 2)

        def evict_turned(eng, stage, unit, copy, done, dst):
            g, b = unit // DB, unit % DB
            eng.wait_ge(xt_turned, stage * DB * QUADS + unit + 1)
            copy(dst[:, b, g * BANK:(g + 1) * BANK], turn_bank[unit % 4][:, :]).then_inc(done, 1)

        @block.scalar
        def _(act):
            def copy(dst, src):
                return act.activation(dst, src, ACT.Copy)

            def square_root(n, ts):
                act.wait_ge(ln_var, n)
                act.activation(spread[:, ts], newton[:, ts], ACT.Sqrt).then_inc(ln_std, 1)

            def preload(func, n):
                act.wait_ge(preloaded, n)
                act.activation(table_scratch[:, :], minus_one[:, :] if func == ACT.Exp else ones[:, 0:1], func)\
                    .then_inc(preloaded, 1)

            def normalise(t, dst, done):
                act.activation(dst[:, t, :], x_sb[:, t, :], ACT.Identity, scale=rstd[:, t:t + 1],
                               bias=centre[:, t:t + 1]).then_inc(done, 1)

            def relu_row(t, par):
                act.wait_ge(z_ready, t + 1)
                act.activation(relu_max[:, par:par + 1], z_max[:, par:par + 1], ACT.Relu,
                               scale=(1 - SLOPE) / SLOPE, bias=s1_pos[:, bass.ds(t, 1)]).then_inc(relu_ready, 1)

            def relu(t, par, half):
                cols = slice(half * N // 2, (half + 1) * N // 2)
                act.activation(relu_part[:, cols], z[:, par, cols], ACT.Relu, scale=(1 - SLOPE) / SLOPE,
                               bias=s1_pos[:, bass.ds(t, 1)]).then_inc(relu_ready, 1)

            def exponent(t, par, half):
                cols = slice(half * N // 2, (half + 1) * N // 2)
                act.wait_ge(e_ready, 2 * t + half + 1)
                if half == 0:
                    act.wait_ge(neg_max_ready, t + 1)
                if not isinstance(t, int) or t > 1:
                    act.wait_ge(turned, 4 * t + 2 * half - 6)
                act.activation(probs[:, par, cols], z[:, par, cols], ACT.Exp, bias=neg_max[:, par:par + 1],
                               accum_out=half_sums[:, bass.ds(t, 1), half]).then_inc(probs_ready, 1)

            def round_turned(t, q):
                act.wait_ge(turned, 4 * t + q + 1)
                copy(pt_hi[:, q, :], turn_bank[q][:, :]).then_inc(pt_hi_ready, 1)

            def attention(t, par):
                static = isinstance(t, int)
                here = not static or t >= 0
                following = not static or t + 1 < T
                ahead = not static or t + 2 < T
                if following:
                    exponent(t + 1, 1 - par, 0)
                if here:
                    round_turned(t, 2)
                if ahead:
                    relu_row(t + 2, par)
                    relu(t + 2, par, 0)
                if here:
                    round_turned(t, 3)
                if following:
                    exponent(t + 1, 1 - par, 1)
                if following:
                    round_turned(t + 1, 0)
                if ahead:
                    relu(t + 2, par, 1)
                if following:
                    round_turned(t + 1, 1)

            square_root(1, slice(0, T))
            act.wait_ge(centre_ready, 1)
            for t in range(1, T, 2):
                normalise(t, xn, xn_odd)
            for unit in range(0, DB * QUADS, 2):
                evict_turned(act, 0, unit, copy, xt_even, xn_t)
            preload(ACT.Exp, 0)
            for c in range(QUADS):
                act.wait_ge(s2_psum, c + 1)
                act.activation(s2_rows[:, c * BANK:(c + 1) * BANK], wide_bank[c % 2][:, :], ACT.Copy, scale=SLOPE)\
                    .then_inc(s2_ready, 1)

            def round_value(t):
                act.wait_ge(v_psum, t + 1)
                copy(v_hi[:, t, :], value_bank[t % 4][:, 0:D]).then_inc(v_hi_ready, 1)

            for t in range(0, 2):
                round_value(t)
            act.wait_ge(s1_ready, 1)
            relu_row(0, 0)
            relu(0, 0, 0)
            for t in range(2, 4):
                round_value(t)
            relu(0, 0, 1)
            for t in range(4, 8):
                round_value(t)
            exponent(0, 0, 0)
            act.wait_ge(s1_ready, 2)
            relu_row(1, 1)
            relu(1, 1, 0)
            for t in range(8, 10):
                round_value(t)
            exponent(0, 0, 1)
            for t in range(10, 12):
                round_value(t)
            relu(1, 1, 1)
            round_value(12)
            round_turned(0, 0)
            round_value(13)
            round_turned(0, 1)
            for t in range(14, T):
                round_value(t)

            act.wait_ge(s1_ready, T)
            for t in range(0, 2):
                attention(t, t % 2)
            with act.Fori(1, T // 2 - 2) as k:
                for par in range(2):
                    attention(2 * k + par, par)
            for t in range(T - 4, T - 1):
                attention(t, t % 2)
            square_root(2, EARLY_ROWS)
            attention(T - 1, 1)
            act.wait_ge(centre_ready, 2)
            for t in range(1, T - 2, 2):
                normalise(t, xn2, xn_odd)
            square_root(3, LATE_ROWS)
            evict_turned(act, 1, 0, copy, xt_even, xn2_t)
            evict_turned(act, 1, 1, copy, xt_odd, xn2_t)
            act.wait_ge(centre_ready, 3)
            normalise(T - 1, xn2, xn_odd)
            def gate_rows(g):
                act.wait_ge(gate_psum, g + 1)
                copy(logits_t[:, g * BANK:(g + 1) * BANK], wide_bank[g % 2][0:E, :]).then_inc(gate_ready, 1)

            for g in range(1, QUADS):
                evict_turned(act, 1, DB * g, copy, xt_even, xn2_t)
                gate_rows(g - 1)
            gate_rows(QUADS - 1)
            preload(ACT.Exp, 1)

            act.wait_ge(logits_shifted, 1)
            act.activation(gates2[:, :, :], logits[:, :, :], ACT.Exp).then_inc(exp_ready, 1)
            act.wait_ge(totals_psum, 1)
            copy(totals[:, :], wide_bank[0][:, 0:P]).then_inc(totals_ready, 1)
            act.wait_ge(b1_turned, 1)
            copy(b1_cols[:, :], wide_bank[1][:, 0:E * FB]).then_inc(b1_ready, 1)

            act.wait_ge(experts_known, 1)
            act.wait_ge(w1_in, 16 * DB * E)
            act.wait_ge(b1_ready, 1)

            def expert_of(t):
                return act.value_load(tile_expert[0:1, bass.ds(t, 1)], min_val=0, max_val=E - 1)

            def round_w1(t, c, e):
                cols = slice(c * FF // 2, (c + 1) * FF // 2)
                if half_tile(t - 1):
                    act.wait_ge(h_psum, done(t - 1, 4, 2) + c + 1)
                elif not isinstance(t, int) or t > 0:
                    act.wait_ge(h_psum, 4 * t + 2 * c - 2)
                dst = w1_full if half_tile(t) else w1_hi
                copy(dst[:, :, cols].unsqueeze(1), w1_sb[:, bass.ds(e, 1), :, cols]).then_inc(w1_hi_ready, 1)

            def round_w2(t, c, e):
                rows = slice(c * FB // 2, (c + 1) * FB // 2)
                if half_tile(t - 1):
                    act.wait_ge(h_used, done(t - 1, 4, 2) + c + 1)
                elif not isinstance(t, int) or t > 0:
                    act.wait_ge(h_used, 4 * t + 2 * c - 2)
                copy(w2_hi[:, rows, :].unsqueeze(1), w2_sb[:, bass.ds(e, 1), rows, :]).then_inc(w2_hi_ready, 1)

            def round_x(t, par):
                n = P if half_tile(t) else TILE
                act.wait_ge(xt_psum, t + 1)
                if not isinstance(t, int) or t > 1:
                    act.wait_ge(h_psum, done(t - 1, 4, 2))
                dst = xt_full if half_tile(t) else xt_hi
                copy(dst[:, par, :, 0:n], xt_bank[par][:, 0:DB * n].rearrange("p (b n) -> p b n", b=DB))\
                    .then_inc(x_hi_ready, 1)

            def bias_relu(t, b, e):
                k, n, m = (2 * (t % 2) + b, P, 4) if half_tile(t) else (b, TILE, 2)
                banks_before = done(t, 4, 2) + b
                act.wait_ge(h_psum, banks_before + 1)
                if not isinstance(t, int) or banks_before >= 2:
                    act.wait_ge(h_lo_ready, banks_before - 1)
                for i in range(m):
                    act.activation(h_full[:, b % 2, i * n:(i + 1) * n], h_bank[k][:, i * n:(i + 1) * n],
                                   ACT.Relu, bias=b1_cols[:, bass.ds(e * FB + m * b + i, 1)])\
                        .then_inc(h_full_ready, 1)

            def weigh(t, par):
                n, col = (1, done(t, 2, 1)) if half_tile(t) else (2, 2 * t)
                act.wait_ge(h_used, done(t + 1, 4, 2))
                if not isinstance(t, int) or t > 1:
                    act.wait_ge(added, done(t - 1, 32, 16))
                for h in range(n):
                    act.activation(y_sb[:, par, h, :], y_bank[par if half_tile(t) else h][:, 0:D], ACT.Copy,
                                   scale=slot_weight[:, bass.ds(col + h, 1)]).then_inc(y_ready, 1)

            e_first = expert_of(0)
            round_w1(0, 0, e_first)
            round_w1(0, 1, e_first)
            act.wait_ge(slots_psum, 1)
            copy(slots_t[:, :], attn_bank[0][0:2 * SLOTS, 0:P]).then_inc(slots_ready, 1)

            def step(t, par):
                static = isinstance(t, int)
                if not static or t >= 1:
                    weigh(t - 1, 1 - par)
                if not static or 0 <= t < TILES:
                    if static and t == 0:
                        act.wait_ge(w2_in, 16 * E)
                    e = expert_of(t)
                    round_w2(t, 0, e)
                    round_w2(t, 1, e)
                hidden = not static or 0 <= t + 1 < TILES
                ahead = not static or t + 2 < TILES
                e_next = expert_of(t + 1) if hidden else None
                split_w1 = ahead and not (static and t == -2)
                x_first = static and t == -1
                e_ahead = expert_of(t + 2) if split_w1 else None
                if x_first:
                    round_x(t + 2, par)
                if hidden:
                    bias_relu(t + 1, 0, e_next)
                if split_w1:
                    round_w1(t + 2, 0, e_ahead)
                if hidden:
                    bias_relu(t + 1, 1, e_next)
                if split_w1:
                    round_w1(t + 2, 1, e_ahead)
                if ahead and not x_first:
                    round_x(t + 2, par)
                if hidden and not half_tile(t + 1):
                    bias_relu(t + 1, 2, e_next)
                    bias_relu(t + 1, 3, e_next)

            act.wait_ge(out_init, 16 * XG)
            for t in range(-2, 2):
                step(t, t % 2)
            with act.Fori(1, FULL // 2 - 1) as k:
                for par in range(2):
                    step(2 * k + par, par)
            for t in range(2 * (FULL // 2 - 1), TILES + 1):
                step(t, t % 2)

        @block.vector
        def _(vec):
            steps = [0]

            def after(instruction):
                instruction.then_inc(route, 1)
                steps[0] += 1
                vec.wait_ge(route, steps[0])

            def count(instruction):
                instruction.then_inc(route, 1)
                steps[0] += 1

            def row_moments(stage, ts):
                for t in range(T)[ts]:
                    vec.wait_ge(ln_step, stage * T + t + 1)
                    vec.bn_aggr(moments[:, t, :], stats[:, t, :]).then_inc(ln_done, 1)
                vec.wait_ge(ln_done, stage * T + ts.stop)
                vec.tensor_scalar(newton[:, ts], moments[:, ts, 1], LN_EPS, None, ALU.add).then_inc(ln_var, 1)

            def inverse_root(n, ts):
                vec.wait_ge(ln_std, n)
                after(vec.reciprocal(rstd[:, ts], spread[:, ts]))
                after(vec.tensor_tensor(spread[:, ts], rstd[:, ts], rstd[:, ts], ALU.mult))
                after(vec.tensor_tensor(spread[:, ts], spread[:, ts], newton[:, ts], ALU.mult))
                after(vec.tensor_scalar(spread[:, ts], spread[:, ts], -0.5, 1.5, ALU.mult, ALU.add))
                after(vec.tensor_tensor(rstd[:, ts], rstd[:, ts], spread[:, ts], ALU.mult))
                vec.scalar_tensor_tensor(centre[:, ts], moments[:, ts, 0], -1.0, rstd[:, ts], ALU.mult, ALU.mult)\
                    .then_inc(centre_ready, 1)

            def normalise(t, dst):
                vec.tensor_scalar(dst[:, t, :], x_sb[:, t, :], moments[:, t, 0:1], rstd[:, t:t + 1],
                                  ALU.subtract, ALU.mult).then_inc(xn_even, 1)

            def statistics(t):
                vec.bn_stats(stats[:, bass.ds(t, 1), :], x_sb[:, bass.ds(t, 1), :]).then_inc(ln_step, 1)

            for g in range(XG):
                vec.wait_ge(x_in[g], 16)
                for t in range(g * T // XG, (g + 1) * T // XG):
                    statistics(t)
            row_moments(0, slice(0, T))
            inverse_root(1, slice(0, T))
            for t in range(0, T, 2):
                normalise(t, xn)
            vec.wait_ge(small_in, 16 * SMALL)
            for b in range(2 * DB):
                dst = fc_ext[:, b, D:D + 1] if b < DB else c2_cols[:, b - DB:b - DB + 1]
                vec.tensor_tensor_reduce(products[:, b, :], gnn_ws[:, b, :], aw_rows[:, :], 1.0, 0.0,
                                         ALU.mult, ALU.add, dst).then_inc(proj_step, 1)
            vec.wait_ge(proj_step, 2 * DB)
            vec.wait_ge(consts, CONSTS)
            for b in range(DB):
                vec.tensor_scalar(c2_wide[:, b, :], ones[:, :], c2_cols[:, b:b + 1], None, ALU.mult)\
                    .then_inc(c_ready, 1)
            for unit in range(1, DB * QUADS, 2):
                evict_turned(vec, 0, unit, vec.tensor_copy, xt_odd, xn_t)
            vec.tensor_copy(ones_r[:, :], ones[0:FCK, :]).then_inc(one_rows, 1)
            vec.tensor_copy(fcb_parts[:, :], fcb_raw[:, :]).then_inc(bias_hi, 1)
            vec.wait_ge(bias_hi, 1)
            vec.tensor_tensor(fcb_parts[32:FCK, :], fcb_raw[32:FCK, :], fcb_parts[32:FCK, :].bitcast(F32),
                              ALU.subtract).then_inc(bias_ready, 1)

            def mask(t, par, turn):
                vec.wait_ge(adj_in[par], 16 * turn + 16)
                vec.tensor_scalar(adj_sb[:, par, :], adj_sb[:, par, :], 0.0, MASKED, ALU.is_le, ALU.mult)\
                    .then_inc(mask_ready, 1)

            def masked(t):
                vec.wait_ge(mask_ready, t + 1)
                if not isinstance(t, int) or t > 1:
                    vec.wait_ge(probs_ready, 2 * t - 2)

            def spread_s2(t, par):
                vec.tensor_tensor_reduce(z[:, par, :], adj_sb[:, par, :], s2_rows[:, :], 1.0, -3.0e38,
                                         ALU.add, ALU.max, z_max[:, par:par + 1]).then_inc(z_ready, 1)

            def rest_turned(t, q):
                vec.wait_ge(pt_hi_ready, 4 * t + q + 1)
                vec.tensor_tensor(pt_lo[:, q, :], turn_bank[q][:, :], pt_hi[:, q, :].bitcast(F32), ALU.subtract)\
                    .then_inc(pt_lo_ready, 1)

            def finish_rows(t, par):
                vec.wait_ge(sum_ready, t + 1)
                vec.reciprocal(row_rcp[:, bass.ds(t, 1)], row_sum[:, bass.ds(t, 1)]).then_inc(rcp_ready, 1)
                vec.wait_ge(attn_psum, t + 1)
                vec.wait_ge(rcp_ready, t + 1)
                vec.scalar_tensor_tensor(x_sb[:, bass.ds(t, 1), :], attn_bank[par][:, 0:D].unsqueeze(1),
                                         row_rcp[:, bass.ds(t, 1)], x_sb[:, bass.ds(t, 1), :],
                                         ALU.mult, ALU.add).then_inc(x1_ready, 1)

            def attention(t, par, half):
                static = isinstance(t, int)
                here = not static or t >= 0
                following = not static or t + 1 < T
                ahead = not static or t + 3 < T
                if here:
                    rest_turned(t, 2)
                if not static or t > 0:
                    finish_rows(t - 1, 1 - par)
                if ahead:
                    mask(t + 3, 1 - par, half + (3 + par) // 2)
                    masked(t + 3)
                if not static or t > 0:
                    vec.wait_ge(x1_ready, t)
                    statistics(t - 1)
                if here:
                    rest_turned(t, 3)
                if following:
                    rest_turned(t + 1, 0)
                if ahead:
                    spread_s2(t + 3, 1 - par)
                if following:
                    rest_turned(t + 1, 1)

            def rest_value(t):
                vec.wait_ge(v_hi_ready, t + 1)
                vec.tensor_scalar(s1_pos[:, t:t + 1], value_bank[t % 4][:, D:D + 1], ab_col[:, :], 1 - SLOPE,
                                  ALU.add, ALU.mult).then_inc(s1_ready, 1)
                vec.tensor_tensor(v_lo[:, t, :], value_bank[t % 4][:, 0:D], v_hi[:, t, :].bitcast(F32),
                                  ALU.subtract).then_inc(v_ready, 1)

            for t in range(2):
                mask(t, t, 0)
            after(vec.tensor_reduce(same_expert[:, :], ident[:, :].rearrange("p (t e) -> p e t", e=E), AXIS, ALU.add))
            after(vec.tensor_tensor(earlier[:, :, :], below[:, :].rearrange("p (t e) -> p t e", e=E),
                                    same_expert[:, :].unsqueeze(1).to_broadcast([P, T, E]), ALU.mult))
            vec.wait_ge(late_in, 16 * LATE)
            vec.tensor_copy(b2_parts[:, :], b2_rows[:, :]).then_inc(b2_hi, 1)
            vec.wait_ge(b2_hi, 1)
            vec.tensor_tensor(b2_parts[32:B2K, :], b2_rows[32:B2K, :], b2_parts[32:B2K, :].bitcast(F32),
                              ALU.subtract).then_inc(b2_lo, 1)
            vec.wait_ge(s2_ready, QUADS)
            masked(0)
            spread_s2(0, 0)
            for t in range(0, 4):
                rest_value(t)
            spread_s2(1, 1)
            for t in range(4, 8):
                rest_value(t)
            mask(2, 0, 1)
            for t in range(8, 12):
                rest_value(t)
            masked(2)
            spread_s2(2, 0)
            rest_value(12)
            rest_turned(0, 0)
            rest_value(13)
            rest_turned(0, 1)
            for t in range(14, T):
                rest_value(t)
            for t in range(0, 2):
                attention(t, t % 2, t // 2)
            with vec.Fori(1, T // 2 - 2) as k:
                for par in range(2):
                    attention(2 * k + par, par, k)
            for t in range(T - 4, T - 1):
                attention(t, t % 2, t // 2)
            row_moments(1, EARLY_ROWS)
            rest_turned(T - 1, 2)
            inverse_root(2, EARLY_ROWS)
            rest_turned(T - 1, 3)
            finish_rows(T - 2, 0)
            vec.wait_ge(probs_ready, 2 * T)
            for t in range(0, T - 2, 2):
                normalise(t, xn2)
            vec.wait_ge(x1_ready, T - 1)
            statistics(T - 2)
            finish_rows(T - 1, 1)
            vec.wait_ge(x1_ready, T)
            statistics(T - 1)
            row_moments(1, LATE_ROWS)
            inverse_root(3, LATE_ROWS)
            normalise(T - 2, xn2)
            vec.wait_ge(xt_odd, QUADS + 1)
            for unit in range(3, DB * QUADS, 2):
                evict_turned(vec, 1, unit, vec.tensor_copy, xt_odd, xn2_t)

            def grid(ap, axis):
                return ap.unsqueeze(axis).to_broadcast([P, T, E])

            vec.wait_ge(out_init, 16 * XG)
            vec.wait_ge(logits_psum, 1)
            after(vec.tensor_tensor(logits[:, :, :], attn_bank[0][:, 0:TE].rearrange("p (t e) -> p t e", e=E),
                                    grid(gate_bs[:, :], 1), ALU.add))
            after(vec.tensor_reduce(norm[:, :], logits[:, :, :], AXIS, ALU.max))
            vec.tensor_tensor(logits[:, :, :], logits[:, :, :], grid(norm[:, :], 2), ALU.subtract)\
                .then_inc(logits_shifted, 1)
            vec.wait_ge(exp_ready, 1)
            after(vec.tensor_reduce(norm[:, :], gates2[:, :, :], AXIS, ALU.add))
            after(vec.reciprocal(norm[:, :], norm[:, :]))
            after(vec.tensor_tensor(gates[:, :, :], gates2[:, :, :], grid(norm[:, :], 2), ALU.mult))

            def choose(k, src, hot):
                after(vec.tensor_reduce(top[:, k, :], src, AXIS, ALU.max))
                after(vec.tensor_tensor(cand[:, :, :], src, grid(top[:, k, :], 2), ALU.is_equal))
                after(vec.tensor_tensor(cand[:, :, :], cand[:, :, :], grid(id_less[:, :], 1), ALU.mult))
                after(vec.tensor_reduce(top_id[:, k, :], cand[:, :, :], AXIS, ALU.min))
                after(vec.tensor_tensor(hot, grid(id_less[:, :], 1), grid(top_id[:, k, :], 2), ALU.is_equal))

            choose(0, gates[:, :, :], hots[:, 0, :, :])
            after(vec.scalar_tensor_tensor(gates2[:, :, :], hots[:, 0, :, :], -2.0, gates[:, :, :], ALU.mult, ALU.add))
            choose(1, gates2[:, :, :], hots[:, 1, :, :])
            vec.tensor_tensor(chosen[:, :, :], hots[:, 0, :, :], hots[:, 1, :, :], ALU.add).then_inc(chosen_ready, 1)
            after(vec.tensor_tensor(norm[:, :], top[:, 0, :], top[:, 1, :], ALU.add))
            after(vec.tensor_scalar(norm[:, :], norm[:, :], GATE_EPS, None, ALU.add))
            after(vec.reciprocal(norm[:, :], norm[:, :]))
            after(vec.tensor_tensor(top_w[:, :, :], top[:, :, :],
                                    norm[:, :].unsqueeze(1).to_broadcast([P, TOPK, T]), ALU.mult))

            vec.wait_ge(position_psum, 1)
            after(vec.tensor_tensor(cmp[:, :, :], attn_bank[1][:, TE:TE + E].unsqueeze(2).to_broadcast([P, E, T]),
                                    block_limits[:, :].unsqueeze(1).to_broadcast([P, E, T]), ALU.is_gt))
            count(vec.tensor_reduce(blocks_of[:, :], cmp[:, :, :], AXIS, ALU.add))
            after(vec.tensor_reduce(pairs_of[:, :], cmp[:, :, 1::2], AXIS, ALU.add))
            count(vec.tensor_tensor_scan(cum_blocks[:, 1:], ones[:, 0:E], blocks_of[:, :], 0.0, ALU.mult, ALU.add))
            after(vec.tensor_tensor_scan(cum_pairs[:, 1:], ones[:, 0:E], pairs_of[:, :], 0.0, ALU.mult, ALU.add))
            after(vec.tensor_scalar(cum_pairs[:, 1:], cum_pairs[:, 1:], float(FULL), None, ALU.min))
            count(vec.tensor_tensor(kept[:, :], cum_pairs[:, 1:], cum_pairs[:, 0:E], ALU.subtract))
            count(vec.scalar_tensor_tensor(left_end[:, :], cum_pairs[:, 1:], -2.0, cum_blocks[:, 1:],
                                           ALU.mult, ALU.add))
            after(vec.scalar_tensor_tensor(left_before[:, :], cum_pairs[:, 0:E], -2.0, cum_blocks[:, 0:E],
                                           ALU.mult, ALU.add))
            count(vec.scalar_tensor_tensor(shift[:, :], cum_pairs[:, 1:], -2.0, left_before[:, :],
                                           ALU.mult, ALU.add))
            rank = attn_bank[1][:, 0:TE].rearrange("p (t e) -> p t e", e=E)
            after(vec.scalar_tensor_tensor(late[:, :, :], grid(kept[:, :], 1), float(TILE), rank,
                                           ALU.mult, ALU.is_le))
            after(vec.scalar_tensor_tensor(late[:, :, :], grid(shift[:, :], 1), 2.0 * FULL, late[:, :, :],
                                           ALU.add, ALU.mult))
            after(vec.scalar_tensor_tensor(late[:, :, :], grid(cum_pairs[:, 0:E], 1), 2.0, late[:, :, :],
                                           ALU.mult, ALU.add))
            after(vec.scalar_tensor_tensor(position[:, :, :], late[:, :, :], float(P), rank, ALU.mult, ALU.add))
            after(vec.tensor_tensor(picked[:, :, :, :],
                                    position[:, :, :].unsqueeze(1).to_broadcast([P, TOPK, T, E]),
                                    hots[:, :, :, :], ALU.mult))
            after(vec.tensor_reduce(pos[:, :, :], picked[:, :, :, :], AXIS, ALU.add))
            after(vec.tensor_copy(pos_int[:, :, :], pos[:, :, :]))
            count(vec.tensor_scalar(part_int[:, 0, :, :], pos_int[:, :, :], P - 1, None, ALU.bitwise_and))
            after(vec.tensor_scalar(part_int[:, 1, :, :], pos_int[:, :, :], P.bit_length() - 1, None,
                                    ALU.logical_shift_right))
            after(vec.tensor_copy(part[:, :, :, :], part_int[:, :, :, :]))
            after(vec.tensor_scalar(over[:, :, :], part[:, 1, :, :], float(SLOTS), float(2 * FULL - 2 - SLOTS),
                                    ALU.is_ge, ALU.mult))
            after(vec.tensor_tensor(part[:, 1, :, :], part[:, 1, :, :], over[:, :, :], ALU.add))
            kt = TOPK * T

            def pairs(ap, n):
                return ap.rearrange("p k t -> p (k t)").unsqueeze(2).to_broadcast([P, kt, n])

            for g in range(HOTS):
                ks = slice(g * kt // HOTS, (g + 1) * kt // HOTS)
                vec.tensor_tensor(in_slot[:, ks, :], column[:, 0:SLOTS].unsqueeze(1).to_broadcast([P, kt // HOTS, SLOTS]),
                                  pairs(part[:, 1, :, :], SLOTS)[:, ks, :], ALU.is_equal).then_inc(slots_hot, 1)
                vec.tensor_tensor(in_row[:, ks, :], column[:, :].unsqueeze(1).to_broadcast([P, kt // HOTS, P]),
                                  pairs(part[:, 0, :, :], P)[:, ks, :], ALU.is_equal).then_inc(rows_hot, 1)
            for tiles, ends in ((slice(0, FULL), cum_pairs[:, 1:E]), (slice(FULL, TILES), left_end[:, 0:E - 1])):
                n = tiles.stop - tiles.start
                after(vec.tensor_tensor(ended[:, tiles, :], ends.unsqueeze(1).to_broadcast([P, n, E - 1]),
                                        column[:, 0:n].unsqueeze(2).to_broadcast([P, n, E - 1]), ALU.is_le))
            after(vec.tensor_reduce(ended_sum[:, :], ended[:, :, :], AXIS, ALU.add))
            vec.tensor_copy(tile_expert[:, :], ended_sum[0:1, :]).then_inc(experts_known, 1)
            after(vec.tensor_scalar(row_expert[32:64, :], row_expert[32:64, :], -32.0, None, ALU.add))
            after(vec.tensor_scalar(b2_choice[:, :], ended_sum[0:B2K, :], row_expert[0:B2K, :], None, ALU.is_equal))

            vec.wait_ge(experts_known, 1)

            def expert_of(t):
                return vec.value_load(tile_expert[0:1, bass.ds(t, 1)], min_val=0, max_val=E - 1)

            def rest_w1(t, c, e):
                cols = slice(c * FF // 2, (c + 1) * FF // 2)
                vec.wait_ge(w1_hi_ready, 2 * t + c + 1)
                vec.tensor_tensor(w1_lo[:, :, cols].unsqueeze(1), w1_sb[:, bass.ds(e, 1), :, cols],
                                  w1_hi[:, :, cols].bitcast(F32).unsqueeze(1), ALU.subtract).then_inc(w1_lo_ready, 1)

            e_first = expert_of(0)
            rest_w1(0, 0, e_first)

            vec.wait_ge(slots_turned, 1)
            slot_token = attn_bank[1][:, 0:SLOTS]
            vec.tensor_scalar(gather_idx[:, :], slot_token, -1.0, 0.0, ALU.add, ALU.max).then_inc(tables, 1)
            after(vec.tensor_scalar(slot_empty[:, :], slot_token, 0.0, NO_TOKEN, ALU.is_equal, ALU.mult))
            vec.scalar_tensor_tensor(add_idx[:, :], slot_token, -1.0, slot_empty[:, :], ALU.add, ALU.add)\
                .then_inc(tables, 1)
            vec.tensor_copy(slot_weight[:, :], attn_bank[1][:, SLOTS:2 * SLOTS]).then_inc(tables, 1)
            rest_w1(0, 1, e_first)

            def rest_w2(t, c, e):
                rows = slice(c * FB // 2, (c + 1) * FB // 2)
                vec.wait_ge(w2_hi_ready, 2 * t + c + 1)
                vec.tensor_tensor(w2_lo[:, rows, :].unsqueeze(1), w2_sb[:, bass.ds(e, 1), rows, :],
                                  w2_hi[:, rows, :].bitcast(F32).unsqueeze(1), ALU.subtract).then_inc(w2_lo_ready, 1)

            def rest_x(t, par):
                vec.wait_ge(x_hi_ready, t + 1)
                vec.tensor_tensor(xt_lo[:, par, :, :], xt_bank[par][:, :].rearrange("p (b n) -> p b n", b=DB),
                                  xt_hi[:, par, :, :].bitcast(F32), ALU.subtract).then_inc(x_lo_ready, 1)

            def split_hidden(t, b):
                half = half_tile(t)
                blocks = slice(4 * b, 4 * b + 4) if half else slice(2 * b, 2 * b + 2)
                n = P if half else TILE
                hi = h_hi[:, blocks, 0:n]
                full = h_full[:, b % 2, :].rearrange("p (i n) -> p i n", n=n)
                vec.wait_ge(h_full_ready, 8 * t + (4 * b + 4 if half else 2 * b + 2))
                if not isinstance(t, int) or t > 0:
                    vec.wait_ge(h_used, done(t - 1, 4, 2) + (2 * b + 2 if half and t == FULL else b + 1))
                vec.tensor_copy(hi, full).then_inc(h_hi_ready, 1)
                vec.wait_ge(h_hi_ready, done(t, 4, 2) + b + 1)
                vec.tensor_tensor(h_lo[:, blocks, 0:n], full, hi.bitcast(F32), ALU.subtract)\
                    .then_inc(h_lo_ready, 1)

            def select_bias(t):
                if not isinstance(t, int) or t > 0:
                    vec.wait_ge(h_used, done(t, 4, 2))
                vec.tensor_scalar(b2_select[:, :], ones[0:B2K, :], b2_choice[:, bass.ds(t, 1)], None, ALU.mult)\
                    .then_inc(b2_selected, 1)

            def step(t, par):
                static = isinstance(t, int)
                if not static or 0 <= t < TILES:
                    select_bias(t)
                    e = expert_of(t)
                    rest_w2(t, 0, e)
                    rest_w2(t, 1, e)
                hidden = not static or 0 <= t + 1 < TILES
                ahead = not static or t + 2 < TILES
                ahead = ahead and not half_tile(t + 2)
                split_w1 = ahead and not (static and t == -2)
                x_first = static and t == -1
                e_ahead = expert_of(t + 2) if split_w1 else None
                if x_first:
                    rest_x(t + 2, par)
                if split_w1:
                    rest_w1(t + 2, 0, e_ahead)
                if hidden:
                    split_hidden(t + 1, 0)
                if split_w1:
                    rest_w1(t + 2, 1, e_ahead)
                if ahead and not x_first:
                    rest_x(t + 2, par)
                if hidden:
                    split_hidden(t + 1, 1)
                if hidden and not half_tile(t + 1):
                    split_hidden(t + 1, 2)
                    split_hidden(t + 1, 3)

            for t in range(-2, 2):
                step(t, t % 2)
            with vec.Fori(1, FULL // 2 - 1) as k:
                for par in range(2):
                    step(2 * k + par, par)
            for t in range(2 * (FULL // 2 - 1), TILES):
                step(t, t % 2)

        @block.tensor
        def _(pe):
            def turn_rows(stage, src, unit):
                g, b = unit // DB, unit % DB
                if b == 0:
                    pe.wait_ge(xn_even, stage * T // 2 + 2 * g + 2)
                    pe.wait_ge(xn_odd, stage * T // 2 + 2 * g + 2)
                if unit >= 4:
                    pe.wait_ge(xt_odd if b else xt_even, stage * QUADS + unit // 2 - 1)
                for j in range(JQ):
                    mm = pe.transpose(turn_bank[unit % 4][:, j * P:(j + 1) * P],
                                      src[:, JQ * g + j, b * P:(b + 1) * P], ident[:, :])
                mm.then_inc(xt_turned, 1)

            def keep_busy(n):
                for _ in range(n):
                    pe.matmul(turn_bank[0][:, 0:P], ident[:, :], ones[:, :], start=True, stop=True)

            pe.wait_ge(consts, CONSTS)
            keep_busy(WARM_START)
            for unit in range(DB * QUADS):
                turn_rows(0, xn, unit)
            pe.wait_ge(c_ready, DB)
            for c in range(QUADS):
                pe.wait_ge(xt_even, c + 1)
                pe.wait_ge(xt_odd, c + 1)
                if c >= 2:
                    pe.wait_ge(s2_ready, c - 1)
                for b in range(DB):
                    mm = pe.matmul(wide_bank[c % 2][:, :], c2_wide[:, b, :], xn_t[:, b, c * BANK:(c + 1) * BANK],
                                   start=(b == 0), stop=(b == DB - 1))
                mm.then_inc(s2_psum, 1)

            def value(t):
                if 2 <= t < 4:
                    pe.wait_ge(s2_ready, t + 1)
                if t >= 4:
                    pe.wait_ge(v_ready, t - 3)
                for b in range(DB):
                    pe.matmul(value_bank[t % 4][:, 0:D + 1], xn_t[:, b, t * P:(t + 1) * P], fc_ext[:, b, :],
                              start=(b == 0), stop=False)
                pe.matmul(value_bank[t % 4][:, 0:D], ones_r[:, :], fcb_parts[:, :], start=False, stop=True)\
                    .then_inc(v_psum, 1)

            def turn(t, par, q):
                if q % 2 == 0:
                    pe.wait_ge(probs_ready, 2 * t + q // 2 + 1)
                if not isinstance(t, int) or t > 0:
                    pe.wait_ge(pt_lo_ready, 4 * t + q - 3)
                for j in range(JQ):
                    c = (JQ * q + j) * P
                    mm = pe.transpose(turn_bank[q][:, j * P:(j + 1) * P], probs[:, par, c:c + P], ident[:, :])
                mm.then_inc(turned, 1)

            def attend(t, par, q):
                if q == 0 and (not isinstance(t, int) or t > 1):
                    pe.wait_ge(x1_ready, t - 1)
                pe.wait_ge(pt_lo_ready, 4 * t + q + 1)
                for j in range(JQ):
                    block_j = JQ * q + j
                    cols = slice(j * P, (j + 1) * P)
                    passes = ((pt_hi, v_hi), (pt_hi, v_lo), (pt_lo, v_hi))
                    for n, (left, right) in enumerate(passes):
                        mm = pe.matmul(attn_bank[par][:, 0:D], left[:, q, cols], right[:, block_j, :],
                                       start=(block_j == 0 and n == 0), stop=(block_j == T - 1 and n == 2))
                if q == QUADS - 1:
                    mm.then_inc(attn_psum, 1)

            def attention(t, par):
                for q in range(QUADS):
                    attend(t, par, q)
                    if not isinstance(t, int) or t + 1 < T:
                        turn(t + 1, 1 - par, q)

            pe.wait_ge(one_rows, 1)
            pe.wait_ge(bias_ready, 1)
            for t in range(T - 4):
                value(t)
            for q in range(QUADS):
                turn(0, 0, q)
            for t in range(T - 4, T):
                value(t)
            pe.wait_ge(v_ready, T)
            for t in range(0, 2):
                attention(t, t % 2)
            with pe.Fori(1, T // 2 - 2) as k:
                for par in range(2):
                    attention(2 * k + par, par)
            for t in range(T - 4, T):
                attention(t, t % 2)

            def gate(g):
                pe.wait_ge(xt_even, QUADS + g + 1)
                pe.wait_ge(xt_odd, QUADS + g + 1)
                if g >= 2:
                    pe.wait_ge(gate_ready, g - 1)
                for b in range(DB):
                    mm = pe.matmul(wide_bank[g % 2][0:E, :], gate_ws[:, b, :], xn2_t[:, b, g * BANK:(g + 1) * BANK],
                                   start=(b == 0), stop=(b == DB - 1))
                mm.then_inc(gate_psum, 1)

            pe.wait_ge(late_in, 16 * LATE)
            for g in range(QUADS):
                for b in range(DB):
                    turn_rows(1, xn2, DB * g + b)
                if g > 0:
                    gate(g - 1)
            gate(QUADS - 1)
            pe.wait_ge(x1_ready, T - 1)
            for t in range(T):
                if t % JQ == 0:
                    pe.wait_ge(gate_ready, t // JQ + 1)
                mm = pe.transpose(attn_bank[0][:, t * E:(t + 1) * E], logits_t[:, t * P:(t + 1) * P],
                                  ident[0:E, 0:E])
            mm.then_inc(logits_psum, 1)
            pe.transpose(wide_bank[1][:, 0:E * FB], b1_raw[:, :], ident[0:E * FB, 0:E * FB]).then_inc(b1_turned, 1)
            keep_busy(WARM_CHOICE)
            pe.wait_ge(chosen_ready, 1)
            hot = chosen[:, :, :].rearrange("p t e -> p (t e)")
            pe.matmul(wide_bank[0][:, 0:P], hot, ones[:, :], start=True, stop=True).then_inc(totals_psum, 1)
            pe.matmul(attn_bank[1][:, 0:TE], below[:, :], hot, start=True, stop=False)
            pe.wait_ge(totals_ready, 1)
            pe.matmul(attn_bank[1][:, 0:TE], totals[:, :], earlier[:, :, :].rearrange("p t e -> p (t e)"),
                      start=False, stop=True)
            pe.matmul(attn_bank[1][:, TE:TE + E], totals[:, :], same_expert[:, :], start=True, stop=True)\
                .then_inc(position_psum, 1)
            keep_busy(WARM_RANK)
            for i in range(TOPK * T):
                if i % (TOPK * T // HOTS) == 0:
                    g = i // (TOPK * T // HOTS)
                    pe.wait_ge(rows_hot, g + 1)
                    pe.wait_ge(vals_ready, 2 * g + 2)
                mm = pe.matmul(attn_bank[0][0:2 * SLOTS, 0:P], slot_vals[:, i, :, :].rearrange("p v s -> p (v s)"),
                               in_row[:, i, :], start=(i == 0), stop=(i == TOPK * T - 1))
            mm.then_inc(slots_psum, 1)
            pe.wait_ge(slots_ready, 1)
            pe.transpose(attn_bank[1][:, 0:2 * SLOTS], slots_t[:, :], ident[0:2 * SLOTS, 0:2 * SLOTS])\
                .then_inc(slots_turned, 1)
            keep_busy(WARM_GATHER)

            def turn_x(t, par, turn):
                half = half_tile(t)
                if half:
                    pe.wait_ge(rows_in[par], 16 * FULL + 16 * ((t - FULL) // 2 + 1))
                else:
                    pe.wait_ge(rows_in[par], 32 * turn + 32)
                if not isinstance(t, int) or t > 1:
                    if half_tile(t - 2):
                        pe.wait_ge(x_hi_ready, t - 1)
                    else:
                        pe.wait_ge(x_lo_ready, t - 1)
                n = 1 if half else 2
                for b in range(DB):
                    for h in range(n):
                        at_col = (b * n + h) * P
                        mm = pe.transpose(xt_bank[par][:, at_col:at_col + P],
                                          x_rows[:, par, h, b * P:(b + 1) * P], ident[:, :])
                mm.then_inc(xt_psum, 1)

            def first_layer(t, par):
                pe.wait_ge(x_lo_ready, t + 1)
                for b in range(HBANKS):
                    if b % 2 == 0:
                        pe.wait_ge(w1_lo_ready, 2 * t + b // 2 + 1)
                    if not isinstance(t, int) or t > 0:
                        pe.wait_ge(h_full_ready, 8 * t + 2 * b - 6)
                    for i in range(2):
                        cols = slice((2 * b + i) * P, (2 * b + i + 1) * P)
                        passes = [(left, right, d) for d in range(DB)
                                  for left, right in ((w1_hi, xt_hi), (w1_hi, xt_lo), (w1_lo, xt_hi))]
                        for n, (left, right, d) in enumerate(passes):
                            mm = pe.matmul(h_bank[b][:, i * TILE:(i + 1) * TILE], left[:, d, cols],
                                           right[:, par, d, :], start=(n == 0), stop=(n == len(passes) - 1))
                    mm.then_inc(h_psum, 1)

            def first_layer_half(t, par):
                pe.wait_ge(x_hi_ready, t + 1)
                for b in range(2):
                    k = 2 * (t % 2) + b
                    pe.wait_ge(w1_hi_ready, 2 * t + b + 1)
                    if t < FULL + 2:
                        pe.wait_ge(h_full_ready, 8 * (FULL - 1) + 2 * k + 2)
                    else:
                        pe.wait_ge(h_full_ready, 8 * (t - 2) + 4 * b + 4)
                    for i in range(4):
                        cols = slice((4 * b + i) * P, (4 * b + i + 1) * P)
                        for d in range(DB):
                            mm = pe.matmul(h_bank[k][:, i * P:(i + 1) * P], w1_full[:, d, cols],
                                           xt_full[:, par, d, 0:P], start=(d == 0), stop=(d == DB - 1))
                    mm.then_inc(h_psum, 1)

            def second_layer(t, par):
                half = half_tile(t)
                if half:
                    pe.wait_ge(y_ready, done(max(t - 1, FULL), 2, 1))
                elif not isinstance(t, int) or t > 0:
                    pe.wait_ge(y_ready, 2 * t)
                banks = [(0, y_bank[par])] if half else [(0, y_bank[0]), (1, y_bank[1])]
                pe.wait_ge(b2_selected, t + 1)
                for h, y in banks:
                    pe.matmul(y[:, 0:D], b2_select[:, :], b2_parts[:, :], start=True, stop=False)
                for b in range(2 if half else HBANKS):
                    pe.wait_ge(h_lo_ready, done(t, 4, 2) + b + 1)
                    if half or b % 2 == 0:
                        pe.wait_ge(w2_lo_ready, 2 * t + (b if half else b // 2) + 1)
                    for fb in range(4 * b, 4 * b + 4) if half else range(2 * b, 2 * b + 2):
                        for h, y in banks:
                            rows = slice(h * P, (h + 1) * P)
                            for left, right in ((h_hi, w2_hi), (h_hi, w2_lo), (h_lo, w2_hi)):
                                mm = pe.matmul(y[:, 0:D], left[:, fb, rows], right[:, fb, :], start=False,
                                               stop=(fb == FB - 1 and left is h_lo))
                    mm.then_inc(h_used, 1)

            def step(t, par, half):
                static = isinstance(t, int)
                if not static or t + 2 < TILES:
                    turn_x(t + 2, par, half + 1)
                if not static or 0 <= t + 1 < TILES:
                    if half_tile(t + 1):
                        first_layer_half(t + 1, 1 - par)
                    else:
                        first_layer(t + 1, 1 - par)
                if not static or t >= 0:
                    second_layer(t, par)

            pe.wait_ge(b2_lo, 1)
            pe.wait_ge(b1_ready, 1)
            for t in range(-2, 2):
                step(t, t % 2, t // 2)
            with pe.Fori(1, FULL // 2 - 1) as k:
                for par in range(2):
                    step(2 * k + par, par, k)
            for t in range(2 * (FULL // 2 - 1), TILES):
                step(t, t % 2, t // 2)


_INS = ["x", "adj", "L0_gnn_W", "L0_gnn_a_w", "L0_gnn_a_b", "L0_gnn_fc_w", "L0_gnn_fc_b", "L0_ffn_Wg",
        "L0_ffn_bg", "L0_ffn_W1", "L0_ffn_b1", "L0_ffn_W2", "L0_ffn_b2"]


def kernel(**inputs):
    import numpy as np
    import concourse.bacc as bacc
    from concourse.bass_utils import run_bass_kernel_spmd

    nc = bacc.Bacc("TRN2", target_bir_lowering=False, num_devices=1)
    arrays, args = {}, []
    for name in _INS:
        a = np.ascontiguousarray(inputs[name]).reshape(np.shape(inputs[name]) or (1,))
        arrays[name] = a
        args.append(nc.dram_tensor(name, a.shape, mybir.dt.from_np(a.dtype), kind="ExternalInput").ap())
    shape = arrays["x"].shape
    args.append(nc.dram_tensor("out", shape, F32, kind="ExternalOutput").ap())
    graph_attention_experts(nc, *args)
    return run_bass_kernel_spmd(nc, [arrays], core_ids=[0]).results[0]["out"]
```

```python
from contextlib import ExitStack

import concourse.bass as bass
from concourse import mybir

F32 = mybir.dt.float32
F32R = mybir.dt.float32r
I32 = mybir.dt.int32
ALU = mybir.AluOpType
ACT = mybir.ActivationFunctionType
AXIS = mybir.AxisListType.X

P = 128
SLOPE = 0.2
MASKED = -9000000000000000.0
LN_EPS = 1e-05
GATE_EPS = 0.01
FAR_BELOW = -1.0e30
BANK = 512


def graph_attention_experts(nc, x, adj, gnn_w, a_w, a_b, fc_w, fc_b, gate_w, gate_b, w1, b1, w2, b2, out):
    N, D = x.shape
    E, _, FF = w1.shape
    T = N // P
    DB = D // P
    FB = FF // P
    QUADS = N // BANK
    JQ = BANK // P
    TOPK = 2
    PAIRS = TOPK * N
    TILE = 2 * P
    SLOTS = (PAIRS - E) // P + E
    HALF = E - 1
    FULL = (SLOTS - HALF) // 2
    TILES = FULL + HALF
    TE = T * E
    NO_TOKEN = 2.0 * N
    HBANKS = FB // 2
    B2K = 32 + E
    FCK = 33
    DX = D + 2
    EARLY_ROWS, LATE_ROWS = slice(0, T - 2), slice(T - 2, T)
    HOTS = 8
    WARM_START, WARM_SPLIT, WARM_NORM, WARM_CHOICE, WARM_RANK, WARM_GATHER = 42, 4, 6, 20, 33, 24
    CONSTS = 11
    assert D == 256 and N == 2048 and FB == 8 and TE == P and SLOTS == 2 * FULL + HALF

    ctx = ExitStack()
    with ctx:
        def sb(name, shape, dt=F32):
            return ctx.enter_context(nc.sbuf_tensor(name, shape, dt))

        def sem(name):
            return ctx.enter_context(nc.semaphore(name))

        ident = sb("ident", [P, P])
        ones = sb("ones", [P, P])
        below = sb("below", [P, P])
        same_expert = sb("same_expert", [P, E])
        earlier = sb("earlier", [P, T, E])
        column = sb("column", [P, P])
        minus_one = sb("minus_one", [P, 1])
        table_scratch = sb("table_scratch", [P, 1])
        token = sb("token", [P, T])
        id_less = sb("id_less", [P, E])
        block_limits = sb("block_limits", [P, T])
        cum_blocks = sb("cum_blocks", [P, E + 1])
        cum_pairs = sb("cum_pairs", [P, E + 1])
        stats = sb("stats", [P, T, 6])
        moments = sb("moments", [P, T, 2])
        spread = sb("spread", [P, T])
        rstd = sb("rstd", [P, T])
        newton = sb("newton", [P, T])
        centre = sb("centre", [P, T])
        s1_pos = sb("s1_pos", [P, T])
        z_max = sb("z_max", [P, 2])
        relu_max = sb("relu_max", [P, 2])
        e_max = sb("e_max", [P, 2])
        neg_max = sb("neg_max", [P, 2])
        half_sums = sb("half_sums", [P, T, 2])
        row_sum = sb("row_sum", [P, T])
        row_rcp = sb("row_rcp", [P, T])
        ab_col = sb("ab_col", [P, 1])
        gate_ws = sb("gate_ws", [P, DB, E])
        gate_bs = sb("gate_bs", [P, E])
        b1_cols = sb("b1_cols", [P, E * FB])
        b2_parts = sb("b2_parts", [B2K, D], F32R)
        row_expert = sb("row_expert", [P, 1])
        b2_choice = sb("b2_choice", [B2K, TILES])
        b2_select = sb("b2_select", [B2K, P], F32R)
        tile_expert = sb("tile_expert", [1, TILES], I32)
        gather_idx = sb("gather_idx", [P, SLOTS], I32)
        add_idx = sb("add_idx", [P, SLOTS], I32)
        slot_weight = sb("slot_weight", [P, SLOTS])
        gather_now = sb("gather_now", [P, 2, 2], I32)
        add_now = sb("add_now", [P, 2, 2], I32)

        base = (nc.sbuf_base + 31) // 32 * 32

        def at(name, offset, shape, dt=F32):
            return nc.alloc_sbuf_tensor_at(name, shape, dt, offset=base + offset)

        K = 1024
        w1_sb = at("w1_sb", 0, [P, E, DB, FF])
        LOW = E * DB * FF * 4
        w2_sb = at("w2_sb", LOW, [P, E, FB, D])
        A = LOW + E * FB * D * 4
        B, C, X, Z = A + 16 * K, A + 32 * K, A + 48 * K, A + 64 * K
        v_hi = at("v_hi", LOW, [P, T, D], F32R)
        v_lo = at("v_lo", LOW + 16 * K, [P, T, D], F32R)
        s2_rows = at("s2_rows", LOW + 32 * K, [P, N])
        adj_sb = at("adj_sb", LOW + 40 * K, [P, 2, N])
        relu_part = at("relu_part", LOW + 56 * K, [P, N])
        z = at("z", A, [P, 2, N])
        probs = at("probs", B, [P, 2, N])
        pt_hi = at("pt_hi", C, [P, QUADS, BANK], F32R)
        pt_lo = at("pt_lo", C + 8 * K, [P, QUADS, BANK], F32R)
        x_sb = at("x_sb", X, [P, T, D])
        xn_t_hi = at("xn_t_hi", 16 * K, [P, DB, N], F32R)
        xn_t_lo = at("xn_t_lo", 32 * K, [P, DB, N], F32R)
        early = [48 * K, A]

        def spare(name, shape, dt=F32, where=0):
            size = 4
            for n in shape[1:]:
                size *= n
            offset = early[where]
            early[where] = offset + (size + 31) // 32 * 32
            assert early[where] <= (LOW, B)[where]
            return at(name, offset, shape, dt)

        fc_ext = spare("fc_ext", [P, DB, DX])
        fc_hi = spare("fc_hi", [P, DB, DX], F32R)
        fc_lo = spare("fc_lo", [P, DB, DX], F32R)
        c2_cols = spare("c2_cols", [P, DB])
        c2_wide = spare("c2_wide", [P, DB, P])
        c2_hi = spare("c2_hi", [P, DB, P], F32R)
        c2_lo = spare("c2_lo", [P, DB, P], F32R)
        fcb_raw = spare("fcb_raw", [FCK, D])
        fcb_parts = spare("fcb_parts", [FCK, D], F32R)
        ones_r = spare("ones_r", [FCK, P], F32R)
        gnn_ws = spare("gnn_ws", [P, 2 * DB, D], F32, 1)
        aw_rows = spare("aw_rows", [P, D], F32, 1)
        products = spare("products", [P, 2 * DB, D], F32, 1)
        b2_rows = at("b2_rows", Z + 3 * K, [B2K, D])
        b1_raw = at("b1_raw", Z + 2 * K, [E * FB, P])
        xn = at("xn", B, [P, T, D])
        xn2 = at("xn2", A, [P, T, D])
        xn2_t = at("xn2_t", B, [P, DB, N])
        logits_t = at("logits_t", C, [E, N])
        rt = [X]

        def routing(name, shape, dt=F32):
            size = 4
            for n in shape[1:]:
                size *= n
            offset = rt[0]
            rt[0] = offset + (size + 31) // 32 * 32
            assert rt[0] <= Z
            return at(name, offset, shape, dt)

        logits = routing("logits", [P, T, E])
        gates = routing("gates", [P, T, E])
        shifted = routing("shifted", [P, T, E])
        others = routing("others", [P, T, E])
        top_less = routing("top_less", [P, TOPK, T])
        top_exp = routing("top_exp", [P, TOPK, T])
        hots = routing("hots", [P, TOPK, T, E])
        cand = routing("cand", [P, T, E])
        chosen = routing("chosen", [P, T, E])
        picked = routing("picked", [P, TOPK, T, E])
        position = routing("position", [P, T, E])
        totals = routing("totals", [P, P])
        cmp = routing("cmp", [P, E, T])
        late = routing("late", [P, T, E])
        top = routing("top", [P, TOPK, T])
        top_id = routing("top_id", [P, TOPK, T])
        top_w = routing("top_w", [P, TOPK, T])
        norm = routing("norm", [P, T])
        blocks_of = routing("blocks_of", [P, E])
        pairs_of = routing("pairs_of", [P, E])
        kept = routing("kept", [P, E])
        left_before = routing("left_before", [P, E])
        left_end = routing("left_end", [P, E])
        shift = routing("shift", [P, E])
        over = routing("over", [P, TOPK, T])
        pos = routing("pos", [P, TOPK, T])
        pos_int = routing("pos_int", [P, TOPK, T], I32)
        part_int = routing("part_int", [P, 2, TOPK, T], I32)
        part = routing("part", [P, 2, TOPK, T])
        ended = routing("ended", [P, TILES, E - 1])
        ended_sum = routing("ended_sum", [P, TILES])
        slots_t = routing("slots_t", [2 * SLOTS, P])
        slot_empty = routing("slot_empty", [P, SLOTS])
        in_row = at("in_row", B, [P, TOPK * T, P])
        in_slot = at("in_slot", Z, [P, TOPK * T, SLOTS])
        slot_vals = at("slot_vals", A, [P, TOPK * T, 2, SLOTS])
        w2_hi = at("w2_hi", A, [P, FB, D], F32R)
        w2_lo = at("w2_lo", A + 8 * K, [P, FB, D], F32R)
        h_hi = at("h_hi", B, [P, FB, TILE], F32R)
        h_lo = at("h_lo", B + 8 * K, [P, FB, TILE], F32R)
        w1_hi = at("w1_hi", C, [P, DB, FF], F32R)
        w1_lo = at("w1_lo", C + 8 * K, [P, DB, FF], F32R)
        last_hi = at("last_hi", C, [P, FB, D], F32R)
        last_lo = at("last_lo", C + 8 * K, [P, FB, D], F32R)
        w1_full = at("w1_full", C, [P, DB, FF])
        xt_hi = at("xt_hi", X, [P, 2, DB, TILE], F32R)
        xt_lo = at("xt_lo", X + 4 * K, [P, 2, DB, TILE], F32R)
        xt_full = at("xt_full", X, [P, 2, DB, TILE])
        h_full = at("h_full", X + 8 * K, [P, 2, BANK])
        y_sb = at("y_sb", X + 12 * K, [P, 2, 2, D])
        x_rows = at("x_rows", Z, [P, 2, 2, D])

        bank = [ctx.enter_context(nc.psum_tensor(f"bank{i}", [P, BANK], F32)) for i in range(8)]
        turn_bank, attn_bank, wide_bank, value_bank = bank[0:4], bank[4:6], bank[6:8], bank[4:8]
        early_bank = bank[0:6]
        h_bank, y_bank, xt_bank = bank[0:4], bank[4:6], bank[6:8]

        xn2_dram = nc.dram_tensor("xn2_dram", [N, D], F32).ap()

        x_in = [sem(f"x_in{g}") for g in range(4)]; small_in = sem("small_in"); late_in = sem("late_in")
        adj_in = [sem("adj_in0"), sem("adj_in1")]
        w1_in = sem("w1_in"); w2_in = sem("w2_in"); xn2_out = sem("xn2_out"); out_init = sem("out_init")
        rows_in = [sem("rows_in0"), sem("rows_in1")]; added = sem("added")
        consts = sem("consts"); pool_step = sem("pool_step")
        proj_step = sem("proj_step"); c_ready = sem("c_ready")
        ln_var = sem("ln_var"); ln_std = sem("ln_std"); ln_step = sem("ln_step"); ln_done = sem("ln_done")
        xn_odd = sem("xn_odd"); xn_even = sem("xn_even"); centre_ready = sem("centre_ready")
        xt_turned = sem("xt_turned"); xt_even = sem("xt_even"); xt_odd = sem("xt_odd")
        xn_t_rounded = sem("xn_t_rounded"); xn_t_ready = sem("xn_t_ready")
        fc_rounded = sem("fc_rounded"); c2_rounded = sem("c2_rounded"); fc_ready = sem("fc_ready")
        c2_ready = sem("c2_ready")
        s2_psum = sem("s2_psum"); s2_ready = sem("s2_ready")
        bias_zero = sem("bias_zero"); bias_hi = sem("bias_hi"); bias_ready = sem("bias_ready")
        v_psum = sem("v_psum"); v_hi_ready = sem("v_hi_ready"); v_ready = sem("v_ready")
        b1_turned = sem("b1_turned"); b1_ready = sem("b1_ready")
        s1_ready = sem("s1_ready"); preloaded = sem("preloaded")
        mask_ready = sem("mask_ready"); z_ready = sem("z_ready"); relu_ready = sem("relu_ready")
        e_max_ready = sem("e_max_ready"); e_ready = sem("e_ready"); probs_ready = sem("probs_ready")
        sum_ready = sem("sum_ready")
        turned = sem("turned"); pt_hi_ready = sem("pt_hi_ready"); pt_lo_ready = sem("pt_lo_ready")
        attn_psum = sem("attn_psum"); rcp_ready = sem("rcp_ready"); x1_ready = sem("x1_ready")
        logits_psum = sem("logits_psum"); gate_psum = sem("gate_psum"); gate_ready = sem("gate_ready")
        route = sem("route"); exp_ready = sem("exp_ready")
        logits_shifted = sem("logits_shifted")
        chosen_ready = sem("chosen_ready"); totals_psum = sem("totals_psum"); totals_ready = sem("totals_ready")
        position_psum = sem("position_psum"); slots_hot = sem("slots_hot"); rows_hot = sem("rows_hot")
        vals_ready = sem("vals_ready"); slots_psum = sem("slots_psum"); slots_ready = sem("slots_ready")
        slots_turned = sem("slots_turned")
        neg_max_ready = sem("neg_max_ready"); b2_zero = sem("b2_zero"); b2_hi = sem("b2_hi"); b2_lo = sem("b2_lo")
        b2_selected = sem("b2_selected")
        tables = sem("tables"); experts_known = sem("experts_known"); one_rows = sem("one_rows")
        pool_passed = sem("pool_passed")
        gather_cols = sem("gather_cols"); add_cols = sem("add_cols")
        xt_psum = sem("xt_psum"); x_hi_ready = sem("x_hi_ready"); x_lo_ready = sem("x_lo_ready")
        w1_hi_ready = sem("w1_hi_ready"); w1_lo_ready = sem("w1_lo_ready")
        w2_hi_ready = sem("w2_hi_ready"); w2_lo_ready = sem("w2_lo_ready")
        h_psum = sem("h_psum"); h_full_ready = sem("h_full_ready")
        h_hi_ready = sem("h_hi_ready"); h_lo_ready = sem("h_lo_ready"); h_used = sem("h_used")
        y_ready = sem("y_ready")

        adj_tiles = adj.rearrange("(t p) j -> p t j", p=P)
        x_tiles = x.rearrange("(t p) d -> p t d", p=P)
        out_tiles = out.rearrange("(t p) d -> p t d", p=P)
        xn2_tiles = xn2_dram.rearrange("(t p) d -> p t d", p=P)
        w1_view = w1.rearrange("e (b p) f -> p e b f", p=P)
        w2_view = w2.rearrange("e (b p) d -> p e b d", p=P)

        XG = 4
        SMALL = 6
        LATE = 5

        def half_tile(t):
            return isinstance(t, int) and t >= FULL

        def second_parts(t):
            return (last_hi, last_lo) if isinstance(t, int) and t == TILES - 1 else (w2_hi, w2_lo)

        def done(t, full, half):
            return full * t if not isinstance(t, int) or t <= FULL else full * FULL + half * (t - FULL)

        block = ctx.enter_context(nc.Block())

        @block.sync
        def _(sp):
            for g in range(XG):
                ts = slice(g * T // XG, (g + 1) * T // XG)
                sp.dma_start(x_sb[:, ts, :], x_tiles[:, ts, :]).then_inc(x_in[g], 16)
            sp.dma_start(gnn_ws[:, :, :], gnn_w.rearrange("(b p) f -> p b f", p=P)).then_inc(small_in, 16)
            sp.dma_start(aw_rows[:, :], a_w.unsqueeze(0).to_broadcast([P, D])).then_inc(small_in, 16)
            sp.dma_start(fc_ext[:, :, 0:D], fc_w.rearrange("(b p) f -> p b f", p=P)).then_inc(small_in, 16)
            sp.dma_start(ab_col[:, :], a_b.unsqueeze(0).to_broadcast([P, 1])).then_inc(small_in, 16)
            sp.wait_ge(bias_zero, 1)
            sp.dma_start(fcb_raw[0:1, :], fc_b.unsqueeze(0)).then_inc(small_in, 16)
            sp.dma_start(fcb_raw[32:33, :], fc_b.unsqueeze(0)).then_inc(small_in, 16)
            for t in range(2):
                sp.dma_start(adj_sb[:, t, :], adj_tiles[:, t, :]).then_inc(adj_in[t], 16)
            sp.dma_start(b1_raw[:, :], b1.rearrange("e (b p) -> (e b) p", p=P)).then_inc(late_in, 16)
            sp.wait_ge(b2_zero, 1)
            sp.dma_start(b2_rows[0:E, :], b2).then_inc(late_in, 16)
            sp.dma_start(b2_rows[32:B2K, :], b2).then_inc(late_in, 16)
            sp.dma_start(gate_ws[:, :, :], gate_w.rearrange("(b p) e -> p b e", p=P)).then_inc(late_in, 16)
            sp.dma_start(gate_bs[:, :], gate_b.unsqueeze(0).to_broadcast([P, E])).then_inc(late_in, 16)

            with sp.Fori(0, T // 2 - 1) as k:
                for par in range(2):
                    sp.wait_ge(z_ready, 2 * k + par + 1)
                    sp.dma_start(adj_sb[:, par, :], adj_tiles[:, bass.ds(2 * k + par + 2, 1), :])\
                        .then_inc(adj_in[par], 16)
                    sp.dma_start(w1_sb[:, bass.ds(k, 1), par, :], w1_view[:, bass.ds(k, 1), par, :])\
                        .then_inc(w1_in, 16)
            for half in range(DB):
                sp.dma_start(w1_sb[:, E - 1, half, :], w1_view[:, E - 1, half, :]).then_inc(w1_in, 16)
            for g in range(XG):
                ts = slice(g * T // XG, (g + 1) * T // XG)
                sp.wait_ge(x1_ready, (g + 1) * T // XG)
                sp.dma_start(out_tiles[:, ts, :], x_sb[:, ts, :]).then_inc(out_init, 16)
            sp.wait_ge(attn_psum, T)
            sp.wait_ge(e_ready, 2 * T)
            sp.wait_ge(z_ready, T)
            for g in range(XG):
                ts = slice(g * T // XG, (g + 1) * T // XG)
                sp.wait_ge(xn_even, T // 2 + 2 * g + 2)
                sp.wait_ge(xn_odd, T // 2 + 2 * g + 2)
                sp.dma_start(xn2_tiles[:, ts, :], xn2[:, ts, :]).then_inc(xn2_out, 16)
            for e in range(E):
                sp.dma_start(w2_sb[:, e, :, :], w2_view[:, e, :, :]).then_inc(w2_in, 16)
            sp.wait_ge(out_init, 16 * XG)
            sp.wait_ge(added, done(TILES, 32, 16))

        @block.gpsimd
        def _(pool):
            steps = [0]

            def after(instruction):
                instruction.then_inc(pool_step, 1)
                steps[0] += 1
                pool.wait_ge(pool_step, steps[0])

            pool.memset(ident[:, :], 0.0).then_inc(pool_step, 1)
            pool.memset(ones[:, :], 1.0).then_inc(pool_step, 1)
            pool.memset(fcb_raw[:, :], 0.0).then_inc(bias_zero, 1)
            pool.memset(fc_ext[:, :, D + 1:DX], 0.0).then_inc(consts, 1)
            pool.wait_ge(pool_step, 2)
            steps[0] = 2
            pool.affine_select(out=ident[:, :], in_=ident[:, :], compare_op=ALU.not_equal, fill=1.0, base=0,
                               pattern=[[-1, P]], channel_multiplier=1).then_inc(consts, 1)
            pool.affine_select(out=below[:, :], in_=ones[:, :], compare_op=ALU.is_gt, fill=0.0, base=0,
                               pattern=[[1, P]], channel_multiplier=-1).then_inc(consts, 1)
            pool.iota(column[:, :], [[1, P]], base=0, channel_multiplier=0,
                      allow_small_or_imprecise_dtypes=True).then_inc(consts, 1)
            pool.iota(token[:, :], [[P, T]], base=1, channel_multiplier=1,
                      allow_small_or_imprecise_dtypes=True).then_inc(consts, 1)
            pool.iota(id_less[:, :], [[1, E]], base=-E, channel_multiplier=0,
                      allow_small_or_imprecise_dtypes=True).then_inc(consts, 1)
            pool.iota(block_limits[:, :], [[P, T]], base=0, channel_multiplier=0,
                      allow_small_or_imprecise_dtypes=True).then_inc(consts, 1)

            pool.iota(row_expert[:, :], [[0, 1]], base=0, channel_multiplier=1,
                      allow_small_or_imprecise_dtypes=True).then_inc(consts, 1)
            pool.memset(minus_one[:, :], -1.0).then_inc(consts, 1)
            pool.memset(cum_blocks[:, 0:1], 0.0).then_inc(consts, 1)
            pool.memset(cum_pairs[:, 0:1], 0.0).then_inc(consts, 1)
            pool.memset(b2_rows[:, :], 0.0).then_inc(b2_zero, 1)

            pool.wait_ge(consts, CONSTS)
            pool.tensor_copy(ones_r[:, :], ones[0:FCK, :]).then_inc(one_rows, 1)
            pool.wait_ge(small_in, 16 * SMALL)
            pool.wait_ge(one_rows, 1)
            pool.tensor_copy(fcb_parts[:, :], fcb_raw[:, :]).then_inc(bias_hi, 1)
            pool.wait_ge(bias_hi, 1)
            pool.tensor_tensor(fcb_parts[32:FCK, :], fcb_raw[32:FCK, :], fcb_parts[32:FCK, :].bitcast(F32),
                               ALU.subtract).then_inc(bias_ready, 1)
            pool.wait_ge(bias_ready, 1)
            pool.wait_ge(proj_step, 2 * DB)
            pool.tensor_copy(fc_hi[:, :, :], fc_ext[:, :, :]).then_inc(fc_rounded, 1)
            pool.wait_ge(fc_rounded, 1)
            pool.tensor_tensor(fc_lo[:, :, :], fc_ext[:, :, :], fc_hi[:, :, :].bitcast(F32), ALU.subtract)\
                .then_inc(fc_ready, 1)
            pool.wait_ge(fc_ready, 1)
            pool.wait_ge(late_in, 16 * LATE)
            pool.tensor_copy(b2_parts[:, :], b2_rows[:, :]).then_inc(b2_hi, 1)
            pool.wait_ge(b2_hi, 1)
            pool.tensor_tensor(b2_parts[32:B2K, :], b2_rows[32:B2K, :], b2_parts[32:B2K, :].bitcast(F32),
                               ALU.subtract).then_inc(b2_lo, 1)
            pool.wait_ge(b2_lo, 1)

            def total(t):
                pool.wait_ge(probs_ready, 2 * t + 2)
                pool.tensor_tensor(row_sum[:, bass.ds(t, 1)], half_sums[:, bass.ds(t, 1), 0],
                                   half_sums[:, bass.ds(t, 1), 1], ALU.add).then_inc(sum_ready, 1)

            def leaky(t, par):
                pool.wait_ge(relu_ready, 3 * t + 1)
                pool.tensor_tensor(e_max[:, par:par + 1], z_max[:, par:par + 1],
                                   relu_max[:, par:par + 1], ALU.add).then_inc(e_max_ready, 1)
                pool.wait_ge(e_max_ready, t + 1)
                pool.tensor_tensor(neg_max[:, par:par + 1], e_max[:, par:par + 1], minus_one[:, :], ALU.mult)\
                    .then_inc(neg_max_ready, 1)
                for half in range(2):
                    cols = slice(half * N // 2, (half + 1) * N // 2)
                    pool.wait_ge(relu_ready, 3 * t + 2 + half)
                    pool.tensor_tensor(z[:, par, cols], z[:, par, cols], relu_part[:, cols], ALU.add)\
                        .then_inc(e_ready, 1)

            leaky(0, 0)
            leaky(1, 1)
            with pool.Fori(1, T // 2) as k:
                for par in range(2):
                    total(2 * k + par - 2)
                    leaky(2 * k + par, par)
            total(T - 2)
            total(T - 1)

            kt = TOPK * T
            top_w_pairs = top_w[:, :, :].rearrange("p k t -> p (k t)").unsqueeze(2).to_broadcast([P, kt, SLOTS])
            pool.wait_ge(xn2_out, 16 * XG)
            for g in range(HOTS):
                ks = slice(g * kt // HOTS, (g + 1) * kt // HOTS)
                ts = slice(g * kt // HOTS % T, g * kt // HOTS % T + kt // HOTS)
                pool.wait_ge(slots_hot, g + 1)
                pool.tensor_tensor(slot_vals[:, ks, 0, :], in_slot[:, ks, :],
                                   token[:, ts].unsqueeze(2).to_broadcast([P, kt // HOTS, SLOTS]), ALU.mult)\
                    .then_inc(vals_ready, 1)
                pool.tensor_tensor(slot_vals[:, ks, 1, :], in_slot[:, ks, :], top_w_pairs[:, ks, :], ALU.mult)\
                    .then_inc(vals_ready, 1)

            pool.wait_ge(tables, 1)
            pool.wait_ge(slots_psum, 1)

            def gather(t, par):
                n, col = (1, done(t, 2, 1)) if half_tile(t) else (2, 2 * t)
                pool.tensor_copy(gather_now[:, par, 0:n], gather_idx[:, bass.ds(col, n)]).then_inc(gather_cols, 1)
                pool.wait_ge(xn2_out, 16 * XG)
                pool.wait_ge(gather_cols, t + 1)
                pool.sem_inc(pool_passed, 1)
                for h in range(n):
                    pool.indirect_dma_start(
                        out=x_rows[:, par, h, :], out_offset=None, in_=xn2_dram,
                        in_offset=bass.IndirectOffsetOnAxis(ap=gather_now[:, par, h:h + 1], axis=0))\
                        .then_inc(rows_in[par], 16)

            def add(t, par):
                n, col = (1, done(t, 2, 1)) if half_tile(t) else (2, 2 * t)
                pool.tensor_copy(add_now[:, par, 0:n], add_idx[:, bass.ds(col, n)]).then_inc(add_cols, 1)
                pool.wait_ge(add_cols, t + 1)
                pool.wait_ge(y_ready, done(t, 2, 1) + n)
                pool.wait_ge(out_init, 16 * XG)
                if not isinstance(t, int) or t > 0:
                    pool.wait_ge(added, done(t, 32, 16))
                    pool.sem_inc(pool_passed, 1)
                for h in range(n):
                    pool.indirect_dma_start(
                        out=out, out_offset=bass.IndirectOffsetOnAxis(ap=add_now[:, par, h:h + 1], axis=0),
                        in_=y_sb[:, par, h, :], in_offset=None, bounds_check=N - 1, oob_is_err=False,
                        compute_op=ALU.add).then_inc(added, 16)

            def step(t, par):
                if not isinstance(t, int) or t + 3 < TILES:
                    if not isinstance(t, int) or t + 3 >= 2:
                        pool.wait_ge(xt_psum, t + 2)
                    gather(t + 3, 1 - par)
                if not isinstance(t, int) or t >= 1:
                    add(t - 1, 1 - par)

            gather(0, 0)
            gather(1, 1)
            pool.wait_ge(tables, 3)
            step(-1, 1)
            for t in range(0, 2):
                step(t, t % 2)
            with pool.Fori(1, FULL // 2 - 2) as k:
                for par in range(2):
                    step(2 * k + par, par)
            for t in range(2 * (FULL // 2 - 2), TILES + 1):
                step(t, t % 2)

        def evict_turned(eng, unit, copy, done):
            g, b = unit // DB, unit % DB
            eng.wait_ge(xt_turned, DB * QUADS + unit + 1)
            copy(xn2_t[:, b, g * BANK:(g + 1) * BANK], turn_bank[unit % 4][:, :]).then_inc(done, 1)

        @block.scalar
        def _(act):
            def copy(dst, src):
                return act.activation(dst, src, ACT.Copy)

            def square_root(n, ts):
                act.wait_ge(ln_var, n)
                act.activation(spread[:, ts], newton[:, ts], ACT.Sqrt).then_inc(ln_std, 1)

            def preload(func, n):
                if n > 0:
                    act.wait_ge(preloaded, n)
                act.activation(table_scratch[:, :], minus_one[:, :] if func == ACT.Exp else ones[:, 0:1], func)\
                    .then_inc(preloaded, 1)

            def normalise(t, dst, done):
                act.activation(dst[:, t, :], x_sb[:, t, :], ACT.Identity, scale=rstd[:, t:t + 1],
                               bias=centre[:, t:t + 1]).then_inc(done, 1)

            def relu_row(t, par):
                act.wait_ge(z_ready, t + 1)
                act.activation(relu_max[:, par:par + 1], z_max[:, par:par + 1], ACT.Relu,
                               scale=(1 - SLOPE) / SLOPE, bias=s1_pos[:, bass.ds(t, 1)]).then_inc(relu_ready, 1)

            def relu(t, par, half):
                cols = slice(half * N // 2, (half + 1) * N // 2)
                act.activation(relu_part[:, cols], z[:, par, cols], ACT.Relu, scale=(1 - SLOPE) / SLOPE,
                               bias=s1_pos[:, bass.ds(t, 1)]).then_inc(relu_ready, 1)

            def exponent(t, par, half):
                cols = slice(half * N // 2, (half + 1) * N // 2)
                act.wait_ge(e_ready, 2 * t + half + 1)
                if half == 0:
                    act.wait_ge(neg_max_ready, t + 1)
                if not isinstance(t, int) or t > 1:
                    act.wait_ge(turned, 4 * t + 2 * half - 6)
                act.activation(probs[:, par, cols], z[:, par, cols], ACT.Exp, bias=neg_max[:, par:par + 1],
                               accum_out=half_sums[:, bass.ds(t, 1), half]).then_inc(probs_ready, 1)

            def round_turned(t, q):
                act.wait_ge(turned, 4 * t + q + 1)
                copy(pt_hi[:, q, :], turn_bank[q][:, :]).then_inc(pt_hi_ready, 1)

            def attention(t, par):
                static = isinstance(t, int)
                here = not static or t >= 0
                following = not static or t + 1 < T
                ahead = not static or t + 2 < T
                if following:
                    exponent(t + 1, 1 - par, 0)
                if here:
                    round_turned(t, 2)
                if ahead:
                    relu_row(t + 2, par)
                    relu(t + 2, par, 0)
                if here:
                    round_turned(t, 3)
                if following:
                    exponent(t + 1, 1 - par, 1)
                if following:
                    round_turned(t + 1, 0)
                if ahead:
                    relu(t + 2, par, 1)
                if following:
                    round_turned(t + 1, 1)

            square_root(1, slice(0, T))
            act.wait_ge(centre_ready, 1)
            for t in range(1, T, 2):
                normalise(t, xn, xn_odd)
            for unit in range(DB * QUADS):
                act.wait_ge(xt_turned, unit + 1)
                copy(xn_t_hi[:, unit % DB, unit // DB * BANK:(unit // DB + 1) * BANK], early_bank[unit % 6][:, :])\
                    .then_inc(xn_t_rounded, 1)
            for c in range(QUADS):
                if c == 2:
                    preload(ACT.Exp, 0)
                act.wait_ge(s2_psum, c + 1)
                act.activation(s2_rows[:, c * BANK:(c + 1) * BANK], wide_bank[c % 2][:, :], ACT.Copy, scale=SLOPE)\
                    .then_inc(s2_ready, 1)

            def round_value(t):
                act.wait_ge(v_psum, t + 1)
                copy(v_hi[:, t, :], value_bank[t % 4][:, 0:D]).then_inc(v_hi_ready, 1)

            for t in range(0, 2):
                round_value(t)
            act.wait_ge(s1_ready, 1)
            relu_row(0, 0)
            relu(0, 0, 0)
            for t in range(2, 4):
                round_value(t)
            relu(0, 0, 1)
            for t in range(4, 8):
                round_value(t)
            exponent(0, 0, 0)
            act.wait_ge(s1_ready, 2)
            relu_row(1, 1)
            relu(1, 1, 0)
            for t in range(8, 10):
                round_value(t)
            exponent(0, 0, 1)
            for t in range(10, 12):
                round_value(t)
            relu(1, 1, 1)
            round_value(12)
            round_turned(0, 0)
            round_value(13)
            round_turned(0, 1)
            for t in range(14, T):
                round_value(t)

            act.wait_ge(s1_ready, T)
            for t in range(0, 2):
                attention(t, t % 2)
            with act.Fori(1, T // 2 - 2) as k:
                for par in range(2):
                    attention(2 * k + par, par)
            for t in range(T - 4, T - 1):
                attention(t, t % 2)
            square_root(2, EARLY_ROWS)
            attention(T - 1, 1)
            act.wait_ge(centre_ready, 2)
            for t in range(1, T - 2, 2):
                normalise(t, xn2, xn_odd)
            evict_turned(act, 0, copy, xt_even)
            square_root(3, LATE_ROWS)
            evict_turned(act, 1, copy, xt_odd)
            act.wait_ge(centre_ready, 3)
            normalise(T - 1, xn2, xn_odd)
            def gate_rows(g):
                act.wait_ge(gate_psum, g + 1)
                copy(logits_t[:, g * BANK:(g + 1) * BANK], wide_bank[g % 2][0:E, :]).then_inc(gate_ready, 1)

            for g in range(1, QUADS):
                evict_turned(act, DB * g, copy, xt_even)
                gate_rows(g - 1)
            gate_rows(QUADS - 1)
            preload(ACT.Exp, 1)

            act.wait_ge(logits_shifted, 1)
            act.activation(gates[:, :, :], shifted[:, :, :], ACT.Exp).then_inc(exp_ready, 1)
            act.wait_ge(logits_shifted, 2)
            act.activation(top_exp[:, :, :], top_less[:, :, :], ACT.Exp).then_inc(exp_ready, 1)
            act.wait_ge(totals_psum, 1)
            copy(totals[:, :], wide_bank[0][:, 0:P]).then_inc(totals_ready, 1)
            act.wait_ge(b1_turned, 1)
            copy(b1_cols[:, :], wide_bank[1][:, 0:E * FB]).then_inc(b1_ready, 1)

            act.wait_ge(experts_known, 1)
            act.wait_ge(w1_in, 16 * DB * E)
            act.wait_ge(b1_ready, 1)

            def expert_of(t):
                return act.value_load(tile_expert[0:1, bass.ds(t, 1)], min_val=0, max_val=E - 1)

            def round_w1(t, c, e):
                cols = slice(c * FF // 2, (c + 1) * FF // 2)
                if half_tile(t - 1):
                    act.wait_ge(h_psum, done(t - 1, 4, 2) + c + 1)
                elif not isinstance(t, int) or t > 0:
                    act.wait_ge(h_psum, 4 * t + 2 * c - 2)
                dst = w1_full if half_tile(t) else w1_hi
                copy(dst[:, :, cols].unsqueeze(1), w1_sb[:, bass.ds(e, 1), :, cols]).then_inc(w1_hi_ready, 1)

            def round_w2(t, c, e):
                rows = slice(c * FB // 2, (c + 1) * FB // 2)
                if isinstance(t, int) and t == TILES - 1:
                    act.wait_ge(h_psum, done(TILES, 4, 2))
                elif half_tile(t - 1):
                    act.wait_ge(h_used, done(t - 1, 4, 2) + c + 1)
                elif not isinstance(t, int) or t > 0:
                    act.wait_ge(h_used, 4 * t + 2 * c - 2)
                hi, _ = second_parts(t)
                copy(hi[:, rows, :].unsqueeze(1), w2_sb[:, bass.ds(e, 1), rows, :]).then_inc(w2_hi_ready, 1)

            def round_x(t, par):
                n = P if half_tile(t) else TILE
                act.wait_ge(xt_psum, t + 1)
                if not isinstance(t, int) or t > 1:
                    act.wait_ge(h_psum, done(t - 1, 4, 2))
                dst = xt_full if half_tile(t) else xt_hi
                copy(dst[:, par, :, 0:n], xt_bank[par][:, 0:DB * n].rearrange("p (b n) -> p b n", b=DB))\
                    .then_inc(x_hi_ready, 1)

            def bias_relu(t, b, e):
                k, n, m = (2 * (t % 2) + b, P, 4) if half_tile(t) else (b, TILE, 2)
                banks_before = done(t, 4, 2) + b
                act.wait_ge(h_psum, banks_before + 1)
                if not isinstance(t, int) or banks_before >= 2:
                    act.wait_ge(h_lo_ready, banks_before - 1)
                for i in range(m):
                    act.activation(h_full[:, b % 2, i * n:(i + 1) * n], h_bank[k][:, i * n:(i + 1) * n],
                                   ACT.Relu, bias=b1_cols[:, bass.ds(e * FB + m * b + i, 1)])\
                        .then_inc(h_full_ready, 1)

            def weigh(t, par):
                n, col = (1, done(t, 2, 1)) if half_tile(t) else (2, 2 * t)
                act.wait_ge(h_used, done(t + 1, 4, 2))
                if not isinstance(t, int) or t > 1:
                    act.wait_ge(added, done(t - 1, 32, 16))
                for h in range(n):
                    act.activation(y_sb[:, par, h, :], y_bank[par if half_tile(t) else h][:, 0:D], ACT.Copy,
                                   scale=slot_weight[:, bass.ds(col + h, 1)]).then_inc(y_ready, 1)

            act.wait_ge(slots_psum, 1)
            copy(slots_t[:, :], attn_bank[0][0:2 * SLOTS, 0:P]).then_inc(slots_ready, 1)
            e_first = expert_of(0)
            round_w1(0, 0, e_first)
            round_w1(0, 1, e_first)

            def step(t, par):
                static = isinstance(t, int)
                last = static and t == TILES - 1
                if (not static or t >= 1) and not last:
                    weigh(t - 1, 1 - par)
                if not static or 0 <= t < TILES:
                    if static and t == 0:
                        act.wait_ge(w2_in, 16 * E)
                    e = expert_of(t)
                    round_w2(t, 0, e)
                    round_w2(t, 1, e)
                if last:
                    weigh(t - 1, 1 - par)
                hidden = not static or 0 <= t + 1 < TILES
                ahead = not static or t + 2 < TILES
                e_next = expert_of(t + 1) if hidden else None
                split_w1 = ahead and not (static and t == -2)
                x_first = static and t == -1
                e_ahead = expert_of(t + 2) if split_w1 else None
                if x_first:
                    round_x(t + 2, par)
                if hidden:
                    bias_relu(t + 1, 0, e_next)
                if split_w1:
                    round_w1(t + 2, 0, e_ahead)
                if hidden:
                    bias_relu(t + 1, 1, e_next)
                if split_w1:
                    round_w1(t + 2, 1, e_ahead)
                if ahead and not x_first:
                    round_x(t + 2, par)
                if hidden and not half_tile(t + 1):
                    bias_relu(t + 1, 2, e_next)
                    bias_relu(t + 1, 3, e_next)

            act.wait_ge(out_init, 16 * XG)
            for t in range(-2, 2):
                step(t, t % 2)
            with act.Fori(1, FULL // 2 - 1) as k:
                for par in range(2):
                    step(2 * k + par, par)
            for t in range(2 * (FULL // 2 - 1), TILES + 1):
                step(t, t % 2)

        @block.vector
        def _(vec):
            steps = [0]

            def after(instruction):
                instruction.then_inc(route, 1)
                steps[0] += 1
                vec.wait_ge(route, steps[0])

            def count(instruction):
                instruction.then_inc(route, 1)
                steps[0] += 1

            def row_moments(stage, ts):
                for t in range(T)[ts]:
                    vec.wait_ge(ln_step, stage * T + t + 1)
                    vec.bn_aggr(moments[:, t, :], stats[:, t, :]).then_inc(ln_done, 1)
                vec.wait_ge(ln_done, stage * T + ts.stop)
                vec.tensor_scalar(newton[:, ts], moments[:, ts, 1], LN_EPS, None, ALU.add).then_inc(ln_var, 1)

            def inverse_root(n, ts):
                vec.wait_ge(ln_std, n)
                after(vec.reciprocal(rstd[:, ts], spread[:, ts]))
                after(vec.tensor_tensor(spread[:, ts], rstd[:, ts], rstd[:, ts], ALU.mult))
                after(vec.tensor_tensor(spread[:, ts], spread[:, ts], newton[:, ts], ALU.mult))
                after(vec.tensor_scalar(spread[:, ts], spread[:, ts], -0.5, 1.5, ALU.mult, ALU.add))
                after(vec.tensor_tensor(rstd[:, ts], rstd[:, ts], spread[:, ts], ALU.mult))
                vec.scalar_tensor_tensor(centre[:, ts], moments[:, ts, 0], -1.0, rstd[:, ts], ALU.mult, ALU.mult)\
                    .then_inc(centre_ready, 1)

            def normalise(t, dst):
                vec.tensor_scalar(dst[:, t, :], x_sb[:, t, :], moments[:, t, 0:1], rstd[:, t:t + 1],
                                  ALU.subtract, ALU.mult).then_inc(xn_even, 1)

            def statistics(t):
                vec.bn_stats(stats[:, bass.ds(t, 1), :], x_sb[:, bass.ds(t, 1), :]).then_inc(ln_step, 1)

            for g in range(XG):
                vec.wait_ge(x_in[g], 16)
                for t in range(g * T // XG, (g + 1) * T // XG):
                    statistics(t)
            row_moments(0, slice(0, T))
            inverse_root(1, slice(0, T))
            for t in range(0, T, 2):
                normalise(t, xn)
            vec.wait_ge(small_in, 16 * SMALL)
            for b in range(2 * DB):
                dst = fc_ext[:, b, D:D + 1] if b < DB else c2_cols[:, b - DB:b - DB + 1]
                vec.tensor_tensor_reduce(products[:, b, :], gnn_ws[:, b, :], aw_rows[:, :], 1.0, 0.0,
                                         ALU.mult, ALU.add, dst).then_inc(proj_step, 1)
            vec.wait_ge(proj_step, 2 * DB)
            vec.wait_ge(consts, CONSTS)
            for b in range(DB):
                vec.tensor_scalar(c2_wide[:, b, :], ones[:, :], c2_cols[:, b:b + 1], None, ALU.mult)\
                    .then_inc(c_ready, 1)
            vec.wait_ge(c_ready, DB)
            vec.tensor_copy(c2_hi[:, :, :], c2_wide[:, :, :]).then_inc(c2_rounded, 1)
            vec.wait_ge(c2_rounded, 1)
            vec.tensor_tensor(c2_lo[:, :, :], c2_wide[:, :, :], c2_hi[:, :, :].bitcast(F32), ALU.subtract)\
                .then_inc(c2_ready, 1)
            for unit in range(DB * QUADS):
                blocks = (slice(None), unit % DB, slice(unit // DB * BANK, (unit // DB + 1) * BANK))
                vec.wait_ge(xn_t_rounded, unit + 1)
                vec.tensor_tensor(xn_t_lo[blocks], early_bank[unit % 6][:, :], xn_t_hi[blocks].bitcast(F32),
                                  ALU.subtract).then_inc(xn_t_ready, 1)

            def mask(t, par, turn):
                vec.wait_ge(adj_in[par], 16 * turn + 16)
                vec.tensor_scalar(adj_sb[:, par, :], adj_sb[:, par, :], 0.0, MASKED, ALU.is_le, ALU.mult)\
                    .then_inc(mask_ready, 1)

            def masked(t):
                vec.wait_ge(mask_ready, t + 1)
                if not isinstance(t, int) or t > 1:
                    vec.wait_ge(probs_ready, 2 * t - 2)

            def spread_s2(t, par):
                vec.tensor_tensor_reduce(z[:, par, :], adj_sb[:, par, :], s2_rows[:, :], 1.0, -3.0e38,
                                         ALU.add, ALU.max, z_max[:, par:par + 1]).then_inc(z_ready, 1)

            def rest_turned(t, q):
                vec.wait_ge(pt_hi_ready, 4 * t + q + 1)
                vec.tensor_tensor(pt_lo[:, q, :], turn_bank[q][:, :], pt_hi[:, q, :].bitcast(F32), ALU.subtract)\
                    .then_inc(pt_lo_ready, 1)

            def finish_rows(t, par):
                vec.wait_ge(sum_ready, t + 1)
                vec.reciprocal(row_rcp[:, bass.ds(t, 1)], row_sum[:, bass.ds(t, 1)]).then_inc(rcp_ready, 1)
                vec.wait_ge(attn_psum, t + 1)
                vec.wait_ge(rcp_ready, t + 1)
                vec.scalar_tensor_tensor(x_sb[:, bass.ds(t, 1), :], attn_bank[par][:, 0:D].unsqueeze(1),
                                         row_rcp[:, bass.ds(t, 1)], x_sb[:, bass.ds(t, 1), :],
                                         ALU.mult, ALU.add).then_inc(x1_ready, 1)

            def attention(t, par, half):
                static = isinstance(t, int)
                here = not static or t >= 0
                following = not static or t + 1 < T
                ahead = not static or t + 3 < T
                if here:
                    rest_turned(t, 2)
                if not static or t > 0:
                    finish_rows(t - 1, 1 - par)
                if ahead:
                    mask(t + 3, 1 - par, half + (3 + par) // 2)
                    masked(t + 3)
                if not static or t > 0:
                    vec.wait_ge(x1_ready, t)
                    statistics(t - 1)
                if here:
                    rest_turned(t, 3)
                if following:
                    rest_turned(t + 1, 0)
                if ahead:
                    spread_s2(t + 3, 1 - par)
                if following:
                    rest_turned(t + 1, 1)

            def rest_value(t):
                vec.wait_ge(v_hi_ready, t + 1)
                vec.tensor_scalar(s1_pos[:, t:t + 1], value_bank[t % 4][:, D:D + 1], ab_col[:, :], 1 - SLOPE,
                                  ALU.add, ALU.mult).then_inc(s1_ready, 1)
                vec.tensor_tensor(v_lo[:, t, :], value_bank[t % 4][:, 0:D], v_hi[:, t, :].bitcast(F32),
                                  ALU.subtract).then_inc(v_ready, 1)

            for t in range(2):
                mask(t, t, 0)
            after(vec.tensor_reduce(same_expert[:, :], ident[:, :].rearrange("p (t e) -> p e t", e=E), AXIS, ALU.add))
            after(vec.tensor_tensor(earlier[:, :, :], below[:, :].rearrange("p (t e) -> p t e", e=E),
                                    same_expert[:, :].unsqueeze(1).to_broadcast([P, T, E]), ALU.mult))
            vec.wait_ge(s2_ready, QUADS)
            masked(0)
            spread_s2(0, 0)
            for t in range(0, 4):
                rest_value(t)
            spread_s2(1, 1)
            for t in range(4, 8):
                rest_value(t)
            mask(2, 0, 1)
            for t in range(8, 12):
                rest_value(t)
            masked(2)
            spread_s2(2, 0)
            rest_value(12)
            rest_turned(0, 0)
            rest_value(13)
            rest_turned(0, 1)
            for t in range(14, T):
                rest_value(t)
            for t in range(0, 2):
                attention(t, t % 2, t // 2)
            with vec.Fori(1, T // 2 - 2) as k:
                for par in range(2):
                    attention(2 * k + par, par, k)
            for t in range(T - 4, T - 1):
                attention(t, t % 2, t // 2)
            row_moments(1, EARLY_ROWS)
            rest_turned(T - 1, 2)
            inverse_root(2, EARLY_ROWS)
            rest_turned(T - 1, 3)
            finish_rows(T - 2, 0)
            vec.wait_ge(probs_ready, 2 * T)
            for t in range(0, T - 2, 2):
                normalise(t, xn2)
            vec.wait_ge(x1_ready, T - 1)
            statistics(T - 2)
            finish_rows(T - 1, 1)
            vec.wait_ge(x1_ready, T)
            statistics(T - 1)
            row_moments(1, LATE_ROWS)
            inverse_root(3, LATE_ROWS)
            normalise(T - 2, xn2)
            vec.wait_ge(xt_odd, 1)
            for unit in range(3, DB * QUADS, 2):
                evict_turned(vec, unit, vec.tensor_copy, xt_odd)

            def grid(ap, axis):
                return ap.unsqueeze(axis).to_broadcast([P, T, E])

            vec.wait_ge(out_init, 16 * XG)
            vec.wait_ge(logits_psum, 1)
            after(vec.tensor_tensor(logits[:, :, :], attn_bank[0][:, 0:TE].rearrange("p (t e) -> p t e", e=E),
                                    grid(gate_bs[:, :], 1), ALU.add))

            def choose(k, src, hot):
                after(vec.tensor_reduce(top[:, k, :], src, AXIS, ALU.max))
                if k == 0:
                    vec.tensor_tensor(shifted[:, :, :], logits[:, :, :], grid(top[:, 0, :], 2), ALU.subtract)\
                        .then_inc(logits_shifted, 1)
                after(vec.tensor_tensor(cand[:, :, :], src, grid(top[:, k, :], 2), ALU.is_equal))
                after(vec.tensor_tensor(cand[:, :, :], cand[:, :, :], grid(id_less[:, :], 1), ALU.mult))
                after(vec.tensor_reduce(top_id[:, k, :], cand[:, :, :], AXIS, ALU.min))
                after(vec.tensor_tensor(hot, grid(id_less[:, :], 1), grid(top_id[:, k, :], 2), ALU.is_equal))

            choose(0, logits[:, :, :], hots[:, 0, :, :])
            after(vec.scalar_tensor_tensor(others[:, :, :], hots[:, 0, :, :], FAR_BELOW, logits[:, :, :],
                                           ALU.mult, ALU.add))
            choose(1, others[:, :, :], hots[:, 1, :, :])
            vec.tensor_tensor(chosen[:, :, :], hots[:, 0, :, :], hots[:, 1, :, :], ALU.add).then_inc(chosen_ready, 1)
            vec.tensor_tensor(top_less[:, :, :], top[:, :, :], top[:, 0:1, :].to_broadcast([P, TOPK, T]), ALU.subtract)\
                .then_inc(logits_shifted, 1)
            vec.wait_ge(exp_ready, 1)
            after(vec.tensor_reduce(norm[:, :], gates[:, :, :], AXIS, ALU.add))
            vec.wait_ge(exp_ready, 2)
            after(vec.scalar_tensor_tensor(norm[:, :], norm[:, :], GATE_EPS, top_exp[:, 0, :], ALU.mult, ALU.add))
            after(vec.tensor_tensor(norm[:, :], norm[:, :], top_exp[:, 1, :], ALU.add))
            after(vec.reciprocal(norm[:, :], norm[:, :]))
            after(vec.tensor_tensor(top_w[:, :, :], top_exp[:, :, :],
                                    norm[:, :].unsqueeze(1).to_broadcast([P, TOPK, T]), ALU.mult))

            vec.wait_ge(position_psum, 1)
            after(vec.tensor_tensor(cmp[:, :, :], attn_bank[1][:, TE:TE + E].unsqueeze(2).to_broadcast([P, E, T]),
                                    block_limits[:, :].unsqueeze(1).to_broadcast([P, E, T]), ALU.is_gt))
            count(vec.tensor_reduce(blocks_of[:, :], cmp[:, :, :], AXIS, ALU.add))
            after(vec.tensor_reduce(pairs_of[:, :], cmp[:, :, 1::2], AXIS, ALU.add))
            count(vec.tensor_tensor_scan(cum_blocks[:, 1:], ones[:, 0:E], blocks_of[:, :], 0.0, ALU.mult, ALU.add))
            after(vec.tensor_tensor_scan(cum_pairs[:, 1:], ones[:, 0:E], pairs_of[:, :], 0.0, ALU.mult, ALU.add))
            after(vec.tensor_scalar(cum_pairs[:, 1:], cum_pairs[:, 1:], float(FULL), None, ALU.min))
            count(vec.tensor_tensor(kept[:, :], cum_pairs[:, 1:], cum_pairs[:, 0:E], ALU.subtract))
            count(vec.scalar_tensor_tensor(left_end[:, :], cum_pairs[:, 1:], -2.0, cum_blocks[:, 1:],
                                           ALU.mult, ALU.add))
            after(vec.scalar_tensor_tensor(left_before[:, :], cum_pairs[:, 0:E], -2.0, cum_blocks[:, 0:E],
                                           ALU.mult, ALU.add))
            count(vec.scalar_tensor_tensor(shift[:, :], cum_pairs[:, 1:], -2.0, left_before[:, :],
                                           ALU.mult, ALU.add))
            rank = attn_bank[1][:, 0:TE].rearrange("p (t e) -> p t e", e=E)
            after(vec.scalar_tensor_tensor(late[:, :, :], grid(kept[:, :], 1), float(TILE), rank,
                                           ALU.mult, ALU.is_le))
            after(vec.scalar_tensor_tensor(late[:, :, :], grid(shift[:, :], 1), 2.0 * FULL, late[:, :, :],
                                           ALU.add, ALU.mult))
            after(vec.scalar_tensor_tensor(late[:, :, :], grid(cum_pairs[:, 0:E], 1), 2.0, late[:, :, :],
                                           ALU.mult, ALU.add))
            after(vec.scalar_tensor_tensor(position[:, :, :], late[:, :, :], float(P), rank, ALU.mult, ALU.add))
            after(vec.tensor_tensor(picked[:, :, :, :],
                                    position[:, :, :].unsqueeze(1).to_broadcast([P, TOPK, T, E]),
                                    hots[:, :, :, :], ALU.mult))
            after(vec.tensor_reduce(pos[:, :, :], picked[:, :, :, :], AXIS, ALU.add))
            after(vec.tensor_copy(pos_int[:, :, :], pos[:, :, :]))
            count(vec.tensor_scalar(part_int[:, 0, :, :], pos_int[:, :, :], P - 1, None, ALU.bitwise_and))
            after(vec.tensor_scalar(part_int[:, 1, :, :], pos_int[:, :, :], P.bit_length() - 1, None,
                                    ALU.logical_shift_right))
            after(vec.tensor_copy(part[:, :, :, :], part_int[:, :, :, :]))
            after(vec.tensor_scalar(over[:, :, :], part[:, 1, :, :], float(SLOTS), float(2 * FULL - 2 - SLOTS),
                                    ALU.is_ge, ALU.mult))
            after(vec.tensor_tensor(part[:, 1, :, :], part[:, 1, :, :], over[:, :, :], ALU.add))
            kt = TOPK * T

            def pairs(ap, n):
                return ap.rearrange("p k t -> p (k t)").unsqueeze(2).to_broadcast([P, kt, n])

            for g in range(HOTS):
                ks = slice(g * kt // HOTS, (g + 1) * kt // HOTS)
                vec.tensor_tensor(in_slot[:, ks, :],
                                  column[:, 0:SLOTS].unsqueeze(1).to_broadcast([P, kt // HOTS, SLOTS]),
                                  pairs(part[:, 1, :, :], SLOTS)[:, ks, :], ALU.is_equal).then_inc(slots_hot, 1)
                vec.tensor_tensor(in_row[:, ks, :], column[:, :].unsqueeze(1).to_broadcast([P, kt // HOTS, P]),
                                  pairs(part[:, 0, :, :], P)[:, ks, :], ALU.is_equal).then_inc(rows_hot, 1)
            for tiles, ends in ((slice(0, FULL), cum_pairs[:, 1:E]), (slice(FULL, TILES), left_end[:, 0:E - 1])):
                n = tiles.stop - tiles.start
                after(vec.tensor_tensor(ended[:, tiles, :], ends.unsqueeze(1).to_broadcast([P, n, E - 1]),
                                        column[:, 0:n].unsqueeze(2).to_broadcast([P, n, E - 1]), ALU.is_le))
            after(vec.tensor_reduce(ended_sum[:, :], ended[:, :, :], AXIS, ALU.add))
            vec.tensor_copy(tile_expert[:, :], ended_sum[0:1, :]).then_inc(experts_known, 1)
            after(vec.tensor_scalar(row_expert[32:64, :], row_expert[32:64, :], -32.0, None, ALU.add))
            after(vec.tensor_scalar(b2_choice[:, :], ended_sum[0:B2K, :], row_expert[0:B2K, :], None, ALU.is_equal))

            vec.wait_ge(experts_known, 1)

            def expert_of(t):
                return vec.value_load(tile_expert[0:1, bass.ds(t, 1)], min_val=0, max_val=E - 1)

            def rest_w1(t, c, e):
                cols = slice(c * FF // 2, (c + 1) * FF // 2)
                vec.wait_ge(w1_hi_ready, 2 * t + c + 1)
                vec.tensor_tensor(w1_lo[:, :, cols].unsqueeze(1), w1_sb[:, bass.ds(e, 1), :, cols],
                                  w1_hi[:, :, cols].bitcast(F32).unsqueeze(1), ALU.subtract).then_inc(w1_lo_ready, 1)

            vec.wait_ge(slots_turned, 1)
            slot_token = attn_bank[1][:, 0:SLOTS]
            vec.tensor_scalar(gather_idx[:, :], slot_token, -1.0, 0.0, ALU.add, ALU.max).then_inc(tables, 1)
            after(vec.tensor_scalar(slot_empty[:, :], slot_token, 0.0, NO_TOKEN, ALU.is_equal, ALU.mult))
            vec.scalar_tensor_tensor(add_idx[:, :], slot_token, -1.0, slot_empty[:, :], ALU.add, ALU.add)\
                .then_inc(tables, 1)
            vec.tensor_copy(slot_weight[:, :], attn_bank[1][:, SLOTS:2 * SLOTS]).then_inc(tables, 1)
            e_first = expert_of(0)
            rest_w1(0, 0, e_first)
            rest_w1(0, 1, e_first)

            def rest_w2(t, c, e):
                rows = slice(c * FB // 2, (c + 1) * FB // 2)
                vec.wait_ge(w2_hi_ready, 2 * t + c + 1)
                hi, lo = second_parts(t)
                vec.tensor_tensor(lo[:, rows, :].unsqueeze(1), w2_sb[:, bass.ds(e, 1), rows, :],
                                  hi[:, rows, :].bitcast(F32).unsqueeze(1), ALU.subtract).then_inc(w2_lo_ready, 1)

            def rest_x(t, par):
                vec.wait_ge(x_hi_ready, t + 1)
                vec.tensor_tensor(xt_lo[:, par, :, :], xt_bank[par][:, :].rearrange("p (b n) -> p b n", b=DB),
                                  xt_hi[:, par, :, :].bitcast(F32), ALU.subtract).then_inc(x_lo_ready, 1)

            def split_hidden(t, b):
                half = half_tile(t)
                blocks = slice(4 * b, 4 * b + 4) if half else slice(2 * b, 2 * b + 2)
                cols = slice(t % 2 * P, t % 2 * P + P) if half else slice(0, TILE)
                n = cols.stop - cols.start
                hi = h_hi[:, blocks, cols]
                full = h_full[:, b % 2, :].rearrange("p (i n) -> p i n", n=n)
                vec.wait_ge(h_full_ready, 8 * t + (4 * b + 4 if half else 2 * b + 2))
                if not half:
                    if not isinstance(t, int) or t > 0:
                        vec.wait_ge(h_used, 4 * t + b - 3)
                elif t < FULL + 2:
                    vec.wait_ge(h_used, 4 * (FULL - 1) + 2 * b + 2)
                else:
                    vec.wait_ge(h_used, done(t - 2, 4, 2) + b + 1)
                vec.tensor_copy(hi, full).then_inc(h_hi_ready, 1)
                vec.wait_ge(h_hi_ready, done(t, 4, 2) + b + 1)
                vec.tensor_tensor(h_lo[:, blocks, cols], full, hi.bitcast(F32), ALU.subtract)\
                    .then_inc(h_lo_ready, 1)

            def select_bias(t):
                if not isinstance(t, int) or t > 0:
                    vec.wait_ge(h_used, done(t, 4, 2))
                vec.tensor_scalar(b2_select[:, :], ones[0:B2K, :], b2_choice[:, bass.ds(t, 1)], None, ALU.mult)\
                    .then_inc(b2_selected, 1)

            def step(t, par):
                static = isinstance(t, int)
                if not static or 0 <= t < TILES:
                    e = expert_of(t)
                    rest_w2(t, 0, e)
                    rest_w2(t, 1, e)
                    select_bias(t)
                hidden = not static or 0 <= t + 1 < TILES
                ahead = not static or t + 2 < TILES
                ahead = ahead and not half_tile(t + 2)
                split_w1 = ahead and not (static and t == -2)
                x_first = static and t == -1
                e_ahead = expert_of(t + 2) if split_w1 else None
                if x_first:
                    rest_x(t + 2, par)
                if split_w1:
                    rest_w1(t + 2, 0, e_ahead)
                if hidden:
                    split_hidden(t + 1, 0)
                if split_w1:
                    rest_w1(t + 2, 1, e_ahead)
                if ahead and not x_first:
                    rest_x(t + 2, par)
                if hidden:
                    split_hidden(t + 1, 1)
                if hidden and not half_tile(t + 1):
                    split_hidden(t + 1, 2)
                    split_hidden(t + 1, 3)

            for t in range(-2, 2):
                step(t, t % 2)
            with vec.Fori(1, FULL // 2 - 1) as k:
                for par in range(2):
                    step(2 * k + par, par)
            for t in range(2 * (FULL // 2 - 1), TILES):
                step(t, t % 2)

        @block.tensor
        def _(pe):
            def turn_rows(stage, unit):
                g, b = unit // DB, unit % DB
                src, banks = (xn2, turn_bank) if stage else (xn, early_bank)
                if b == 0:
                    pe.wait_ge(xn_even, stage * T // 2 + 2 * g + 2)
                    pe.wait_ge(xn_odd, stage * T // 2 + 2 * g + 2)
                if stage and unit >= 4:
                    pe.wait_ge(xt_odd if b else xt_even, unit // 2 - 1)
                elif unit >= 6:
                    pe.wait_ge(xn_t_ready, unit - 5)
                for j in range(JQ):
                    mm = pe.transpose(banks[unit % len(banks)][:, j * P:(j + 1) * P],
                                      src[:, JQ * g + j, b * P:(b + 1) * P], ident[:, :])
                mm.then_inc(xt_turned, 1)

            def keep_busy(n, spare_bank=turn_bank[0]):
                for _ in range(n):
                    pe.matmul(spare_bank[:, 0:P], ident[:, :], ones[:, :], start=True, stop=True)

            pe.wait_ge(consts, CONSTS)
            keep_busy(WARM_START)

            def spread_rows(c):
                pe.wait_ge(xn_t_ready, DB * c + DB)
                if c >= 2:
                    pe.wait_ge(s2_ready, c - 1)
                passes = [(left, right, b) for b in range(DB)
                          for left, right in ((c2_hi, xn_t_hi), (c2_hi, xn_t_lo), (c2_lo, xn_t_hi))]
                for n, (left, right, b) in enumerate(passes):
                    mm = pe.matmul(wide_bank[c % 2][:, :], left[:, b, :], right[:, b, c * BANK:(c + 1) * BANK],
                                   start=(n == 0), stop=(n == len(passes) - 1))
                mm.then_inc(s2_psum, 1)

            for unit in range(6):
                turn_rows(0, unit)
            keep_busy(WARM_SPLIT, wide_bank[0])
            pe.wait_ge(c2_ready, 1)
            spread_rows(0)
            for b in range(DB):
                turn_rows(0, 6 + b)
            for c in range(1, QUADS):
                spread_rows(c)

            def value(t):
                if 2 <= t < 4:
                    pe.wait_ge(s2_ready, t + 1)
                if t >= 4:
                    pe.wait_ge(v_ready, t - 3)
                passes = [(left, right, b) for b in range(DB)
                          for left, right in ((xn_t_hi, fc_hi), (xn_t_hi, fc_lo), (xn_t_lo, fc_hi))]
                for n, (left, right, b) in enumerate(passes):
                    pe.matmul(value_bank[t % 4][:, 0:DX], left[:, b, t * P:(t + 1) * P], right[:, b, :],
                              start=(n == 0), stop=False)
                pe.matmul(value_bank[t % 4][:, 0:D], ones_r[:, :], fcb_parts[:, :], start=False, stop=True)\
                    .then_inc(v_psum, 1)

            def turn(t, par, q):
                if q % 2 == 0:
                    pe.wait_ge(probs_ready, 2 * t + q // 2 + 1)
                if not isinstance(t, int) or t > 0:
                    pe.wait_ge(pt_lo_ready, 4 * t + q - 3)
                for j in range(JQ):
                    c = (JQ * q + j) * P
                    mm = pe.transpose(turn_bank[q][:, j * P:(j + 1) * P], probs[:, par, c:c + P], ident[:, :])
                mm.then_inc(turned, 1)

            def attend(t, par, q):
                if q == 0 and (not isinstance(t, int) or t > 1):
                    pe.wait_ge(x1_ready, t - 1)
                pe.wait_ge(pt_lo_ready, 4 * t + q + 1)
                for j in range(JQ):
                    block_j = JQ * q + j
                    cols = slice(j * P, (j + 1) * P)
                    passes = ((pt_hi, v_hi), (pt_hi, v_lo), (pt_lo, v_hi))
                    for n, (left, right) in enumerate(passes):
                        mm = pe.matmul(attn_bank[par][:, 0:D], left[:, q, cols], right[:, block_j, :],
                                       start=(block_j == 0 and n == 0), stop=(block_j == T - 1 and n == 2))
                if q == QUADS - 1:
                    mm.then_inc(attn_psum, 1)

            def attention(t, par):
                for q in range(QUADS):
                    attend(t, par, q)
                    if not isinstance(t, int) or t + 1 < T:
                        turn(t + 1, 1 - par, q)

            pe.wait_ge(fc_ready, 1)
            pe.wait_ge(one_rows, 1)
            pe.wait_ge(bias_ready, 1)
            for t in range(T - 4):
                value(t)
            for q in range(QUADS):
                turn(0, 0, q)
            for t in range(T - 4, T):
                value(t)
            pe.wait_ge(v_ready, T)
            for t in range(0, 2):
                attention(t, t % 2)
            with pe.Fori(1, T // 2 - 2) as k:
                for par in range(2):
                    attention(2 * k + par, par)
            for t in range(T - 4, T):
                attention(t, t % 2)

            def gate(g):
                pe.wait_ge(xt_even, g + 1)
                pe.wait_ge(xt_odd, g + 1)
                if g >= 2:
                    pe.wait_ge(gate_ready, g - 1)
                for b in range(DB):
                    mm = pe.matmul(wide_bank[g % 2][0:E, :], gate_ws[:, b, :], xn2_t[:, b, g * BANK:(g + 1) * BANK],
                                   start=(b == 0), stop=(b == DB - 1))
                mm.then_inc(gate_psum, 1)

            pe.wait_ge(late_in, 16 * LATE)
            pe.wait_ge(x1_ready, T - 1)
            for g in range(QUADS):
                for b in range(DB):
                    turn_rows(1, DB * g + b)
                if g == 1:
                    keep_busy(WARM_NORM, attn_bank[0])
                if g > 0:
                    gate(g - 1)
            gate(QUADS - 1)
            for t in range(T):
                if t % JQ == 0:
                    pe.wait_ge(gate_ready, t // JQ + 1)
                mm = pe.transpose(attn_bank[0][:, t * E:(t + 1) * E], logits_t[:, t * P:(t + 1) * P],
                                  ident[0:E, 0:E])
            mm.then_inc(logits_psum, 1)
            pe.transpose(wide_bank[1][:, 0:E * FB], b1_raw[:, :], ident[0:E * FB, 0:E * FB]).then_inc(b1_turned, 1)
            keep_busy(WARM_CHOICE)
            pe.wait_ge(chosen_ready, 1)
            hot = chosen[:, :, :].rearrange("p t e -> p (t e)")
            pe.matmul(wide_bank[0][:, 0:P], hot, ones[:, :], start=True, stop=True).then_inc(totals_psum, 1)
            pe.matmul(attn_bank[1][:, 0:TE], below[:, :], hot, start=True, stop=False)
            pe.wait_ge(totals_ready, 1)
            pe.matmul(attn_bank[1][:, 0:TE], totals[:, :], earlier[:, :, :].rearrange("p t e -> p (t e)"),
                      start=False, stop=True)
            pe.matmul(attn_bank[1][:, TE:TE + E], totals[:, :], same_expert[:, :], start=True, stop=True)\
                .then_inc(position_psum, 1)
            keep_busy(WARM_RANK)
            for i in range(TOPK * T):
                if i % (TOPK * T // HOTS) == 0:
                    g = i // (TOPK * T // HOTS)
                    pe.wait_ge(rows_hot, g + 1)
                    pe.wait_ge(vals_ready, 2 * g + 2)
                mm = pe.matmul(attn_bank[0][0:2 * SLOTS, 0:P], slot_vals[:, i, :, :].rearrange("p v s -> p (v s)"),
                               in_row[:, i, :], start=(i == 0), stop=(i == TOPK * T - 1))
            mm.then_inc(slots_psum, 1)
            pe.wait_ge(slots_ready, 1)
            pe.transpose(attn_bank[1][:, 0:2 * SLOTS], slots_t[:, :], ident[0:2 * SLOTS, 0:2 * SLOTS])\
                .then_inc(slots_turned, 1)
            keep_busy(WARM_GATHER)

            def turn_x(t, par, turn):
                half = half_tile(t)
                if half:
                    pe.wait_ge(rows_in[par], 16 * FULL + 16 * ((t - FULL) // 2 + 1))
                else:
                    pe.wait_ge(rows_in[par], 32 * turn + 32)
                if not isinstance(t, int) or t > 1:
                    if half_tile(t - 2):
                        pe.wait_ge(x_hi_ready, t - 1)
                    else:
                        pe.wait_ge(x_lo_ready, t - 1)
                n = 1 if half else 2
                for b in range(DB):
                    for h in range(n):
                        at_col = (b * n + h) * P
                        mm = pe.transpose(xt_bank[par][:, at_col:at_col + P],
                                          x_rows[:, par, h, b * P:(b + 1) * P], ident[:, :])
                mm.then_inc(xt_psum, 1)

            def first_layer(t, par):
                pe.wait_ge(x_lo_ready, t + 1)
                for b in range(HBANKS):
                    if b % 2 == 0:
                        pe.wait_ge(w1_lo_ready, 2 * t + b // 2 + 1)
                    if not isinstance(t, int) or t > 0:
                        pe.wait_ge(h_full_ready, 8 * t + 2 * b - 6)
                    for i in range(2):
                        cols = slice((2 * b + i) * P, (2 * b + i + 1) * P)
                        passes = [(left, right, d) for d in range(DB)
                                  for left, right in ((w1_hi, xt_hi), (w1_hi, xt_lo), (w1_lo, xt_hi))]
                        for n, (left, right, d) in enumerate(passes):
                            mm = pe.matmul(h_bank[b][:, i * TILE:(i + 1) * TILE], left[:, d, cols],
                                           right[:, par, d, :], start=(n == 0), stop=(n == len(passes) - 1))
                    mm.then_inc(h_psum, 1)

            def first_layer_half(t, par):
                pe.wait_ge(x_hi_ready, t + 1)
                for b in range(2):
                    k = 2 * (t % 2) + b
                    pe.wait_ge(w1_hi_ready, 2 * t + b + 1)
                    if t < FULL + 2:
                        pe.wait_ge(h_full_ready, 8 * (FULL - 1) + 2 * k + 2)
                    else:
                        pe.wait_ge(h_full_ready, 8 * (t - 2) + 4 * b + 4)
                    for i in range(4):
                        cols = slice((4 * b + i) * P, (4 * b + i + 1) * P)
                        for d in range(DB):
                            mm = pe.matmul(h_bank[k][:, i * P:(i + 1) * P], w1_full[:, d, cols],
                                           xt_full[:, par, d, 0:P], start=(d == 0), stop=(d == DB - 1))
                    mm.then_inc(h_psum, 1)

            def second_layer(t, par):
                half = half_tile(t)
                hi, lo = second_parts(t)
                if half:
                    pe.wait_ge(y_ready, done(max(t - 1, FULL), 2, 1))
                elif not isinstance(t, int) or t > 0:
                    pe.wait_ge(y_ready, 2 * t)
                banks = [(0, y_bank[par])] if half else [(0, y_bank[0]), (1, y_bank[1])]
                for b in range(2 if half else HBANKS):
                    pe.wait_ge(h_lo_ready, done(t, 4, 2) + b + 1)
                    if half or b % 2 == 0:
                        pe.wait_ge(w2_lo_ready, 2 * t + (b if half else b // 2) + 1)
                    for fb in range(4 * b, 4 * b + 4) if half else range(2 * b, 2 * b + 2):
                        for h, y in banks:
                            at_col = t % 2 * P if half else h * P
                            rows = slice(at_col, at_col + P)
                            for left, right in ((h_hi, hi), (h_hi, lo), (h_lo, hi)):
                                mm = pe.matmul(y[:, 0:D], left[:, fb, rows], right[:, fb, :],
                                               start=(fb == 0 and right is hi and left is h_hi), stop=False)
                    if b == (2 if half else HBANKS) - 1:
                        pe.wait_ge(b2_selected, t + 1)
                        for h, y in banks:
                            mm = pe.matmul(y[:, 0:D], b2_select[:, :], b2_parts[:, :], start=False, stop=True)
                    mm.then_inc(h_used, 1)

            def step(t, par, half):
                static = isinstance(t, int)
                if not static or t + 2 < TILES:
                    turn_x(t + 2, par, half + 1)
                if not static or 0 <= t + 1 < TILES:
                    if half_tile(t + 1):
                        first_layer_half(t + 1, 1 - par)
                    else:
                        first_layer(t + 1, 1 - par)
                if not static or t >= 0:
                    second_layer(t, par)

            pe.wait_ge(b2_lo, 1)
            pe.wait_ge(b1_ready, 1)
            for t in range(-2, 2):
                step(t, t % 2, t // 2)
            with pe.Fori(1, FULL // 2 - 1) as k:
                for par in range(2):
                    step(2 * k + par, par, k)
            for t in range(2 * (FULL // 2 - 1), TILES):
                step(t, t % 2, t // 2)


_INS = ["x", "adj", "L0_gnn_W", "L0_gnn_a_w", "L0_gnn_a_b", "L0_gnn_fc_w", "L0_gnn_fc_b", "L0_ffn_Wg",
        "L0_ffn_bg", "L0_ffn_W1", "L0_ffn_b1", "L0_ffn_W2", "L0_ffn_b2"]


def kernel(**inputs):
    import numpy as np
    import concourse.bacc as bacc
    from concourse.bass_utils import run_bass_kernel_spmd

    nc = bacc.Bacc("TRN2", target_bir_lowering=False, num_devices=1)
    arrays, args = {}, []
    for name in _INS:
        a = np.ascontiguousarray(inputs[name]).reshape(np.shape(inputs[name]) or (1,))
        arrays[name] = a
        args.append(nc.dram_tensor(name, a.shape, mybir.dt.from_np(a.dtype), kind="ExternalInput").ap())
    shape = arrays["x"].shape
    args.append(nc.dram_tensor("out", shape, F32, kind="ExternalOutput").ap())
    graph_attention_experts(nc, *args)
    return run_bass_kernel_spmd(nc, [arrays], core_ids=[0]).results[0]["out"]
```
